# Optimizing a Trainium2 kernel written in Bass

```python
import numpy as np
import jax
import jax.numpy as jnp

def _softmax(x, axis=-1):
    return jax.nn.softmax(x, axis=axis)

def _gelu(x):
    return jax.nn.gelu(x, approximate=True)

def _silu(x):
    return jax.nn.silu(x)

def _sigmoid(x):
    return jax.nn.sigmoid(x)

def _layernorm(x, axis=-1, eps=1e-05):
    m = jnp.mean(x, axis=axis, keepdims=True)
    v = jnp.var(x, axis=axis, keepdims=True)
    return (x - m) / jnp.sqrt(v + eps)

def _scatter_add(tgt, idx, src, axis=0):
    return tgt.at[idx].add(src)

def _segment_sum(src, seg, n):
    return jax.ops.segment_sum(src, seg, n)
kernel_name = 'mk_vit_tower_d1_tok_img768_r4_ec43dc'

def setup_inputs(seed: int=0):
    np.random.seed(seed)
    _w = jnp.asarray

    def _rec_inputs():
        import jax
        import jax.numpy as jnp
        _rk = jax.random.key(seed)
        x = -0.000147625 + 0.999875 * jax.random.normal(jax.random.fold_in(_rk, 1), (128, 12, 224, 224), jnp.float32)
        return x
    x = _rec_inputs()

    def _L0_tok_setup():
        import jax, jax.numpy as jnp
        import numpy as np
        IMG = 224
        PATCH = 16
        EMBED = 192
        C = 12
        B = 64
        key = jax.random.key(seed)
        k1, k2 = jax.random.split(key)
        x = jax.random.normal(k1, (B, C, IMG, IMG), dtype=jnp.float32)
        channel_weights = jax.random.normal(k2, (C, EMBED), dtype=jnp.float32)
        return {'x': x, 'channel_weights': channel_weights}
    _L0_tok_all = _L0_tok_setup()
    _L0_tok_in = {k: v for k, v in _L0_tok_all.items() if k in ('channel_weights',)}
    del _L0_tok_all

    def _L0_attn_setup():
        import jax, jax.numpy as jnp
        import numpy as np
        B, N, C = (64, 80, 192)
        NUM_HEADS = 12
        LENS_Z = 64
        SCALE = (C // NUM_HEADS) ** (-0.5)
        key = jax.random.key(seed)
        k1, k2, k3 = jax.random.split(key, 3)
        x = jax.random.normal(k1, (B, N, C), dtype=jnp.float32)
        proj_w = jax.random.normal(k2, (C, C), dtype=jnp.float32) * 0.02
        proj_b = jax.random.normal(k3, (C,), dtype=jnp.float32) * 0.02
        return {'x': x, 'proj_w': proj_w, 'proj_b': proj_b}
    _L0_attn_all = _L0_attn_setup()
    _L0_attn_in = {k: v for k, v in _L0_attn_all.items() if k in ('proj_w', 'proj_b')}
    del _L0_attn_all

    def _L0_ffn_setup():
        import jax, jax.numpy as jnp
        import numpy as np
        from jax import lax
        DIM = 192
        INTER = 128
        E = 8
        G = 4
        TOPK_G = 2
        TOPK = 2
        ROUTE_SCALE = 1.0

        def _gate(x2, gate_weight, gate_bias):
            T = x2.shape[0]
            scores = jax.nn.sigmoid(x2 @ gate_weight.T)
            s = scores + gate_bias
            sv = s.reshape(T, G, E // G)
            top2, _ = lax.top_k(sv, 2)
            group_scores = top2.sum(-1)
            _, gidx = lax.top_k(group_scores, TOPK_G)
            gmask = jnp.zeros((T, G), bool).at[jnp.arange(T)[:, None], gidx].set(True)
            masked = jnp.where(gmask[:, :, None], sv, -jnp.inf).reshape(T, E)
            _, idx = lax.top_k(masked, TOPK)
            w = jnp.take_along_axis(scores, idx, axis=1)
            w = w / (w.sum(-1, keepdims=True) + 1e-06) * ROUTE_SCALE
            return (w, idx)
        key = jax.random.key(seed)
        ks = jax.random.split(key, 9)
        s = 1.0 / np.sqrt(DIM)
        si = 1.0 / np.sqrt(INTER)
        return {'x': jax.random.normal(ks[0], (4, 1024, DIM), jnp.float32), 'gate_weight': jax.random.uniform(ks[1], (E, DIM), jnp.float32, -s, s), 'gate_bias': jnp.zeros((E,), jnp.float32), 'w1': jax.random.uniform(ks[2], (E, INTER, DIM), jnp.float32, -s, s), 'w2': jax.random.uniform(ks[3], (E, DIM, INTER), jnp.float32, -si, si), 'w3': jax.random.uniform(ks[4], (E, INTER, DIM), jnp.float32, -s, s), 'sw1': jax.random.uniform(ks[5], (INTER, DIM), jnp.float32, -s, s), 'sw2': jax.random.uniform(ks[6], (DIM, INTER), jnp.float32, -si, si), 'sw3': jax.random.uniform(ks[7], (INTER, DIM), jnp.float32, -s, s)}
    _L0_ffn_all = _L0_ffn_setup()
    _L0_ffn_in = {k: v for k, v in _L0_ffn_all.items() if k in ('gate_weight', 'gate_bias', 'w1', 'w2', 'w3', 'sw1', 'sw2', 'sw3')}
    del _L0_ffn_all
    return {'x': x, 'L0_tok_channel_weights': _L0_tok_in['channel_weights'], 'L0_attn_proj_w': _L0_attn_in['proj_w'], 'L0_attn_proj_b': _L0_attn_in['proj_b'], 'L0_ffn_gate_weight': _L0_ffn_in['gate_weight'], 'L0_ffn_gate_bias': _L0_ffn_in['gate_bias'], 'L0_ffn_w1': _L0_ffn_in['w1'], 'L0_ffn_w2': _L0_ffn_in['w2'], 'L0_ffn_w3': _L0_ffn_in['w3'], 'L0_ffn_sw1': _L0_ffn_in['sw1'], 'L0_ffn_sw2': _L0_ffn_in['sw2'], 'L0_ffn_sw3': _L0_ffn_in['sw3']}

def reference(x, L0_tok_channel_weights, L0_attn_proj_w, L0_attn_proj_b, L0_ffn_gate_weight, L0_ffn_gate_bias, L0_ffn_w1, L0_ffn_w2, L0_ffn_w3, L0_ffn_sw1, L0_ffn_sw2, L0_ffn_sw3):
    import jax
    import jax.numpy as jnp

    def _L0_tok_ref(x, channel_weights):
        import jax, jax.numpy as jnp
        import numpy as np
        IMG = 224
        PATCH = 16
        EMBED = 192
        C = 12
        B = 64
        Bb, Cc, H, W = x.shape
        K = PATCH
        n = H // K
        pooled = x.reshape(Bb, Cc, n, K, n, K).sum(axis=(3, 5))
        out = jnp.einsum('bcij,ce->bije', pooled, channel_weights)
        return out.reshape(Bb, n * n, EMBED)

    def _L0_attn_ref(x, proj_w, proj_b):
        import jax, jax.numpy as jnp
        import numpy as np
        B, N, C = (64, 80, 192)
        NUM_HEADS = 12
        LENS_Z = 64
        SCALE = (C // NUM_HEADS) ** (-0.5)
        q = x[:, :LENS_Z]
        k = x[:, LENS_Z:]
        v = k
        attn = jnp.einsum('bqc,bkc->bqk', q, k) * SCALE
        attn = jax.nn.softmax(attn, axis=-1)
        out = jnp.einsum('bqk,bkc->bqc', attn, v)
        out = jnp.transpose(out, (0, 2, 1)).reshape(out.shape[0], -1, C)
        out = out @ proj_w.T + proj_b
        return jnp.concatenate([out, k], axis=1)

    def _L0_ffn_ref(x, gate_weight, gate_bias, w1, w2, w3, sw1, sw2, sw3):
        import jax, jax.numpy as jnp
        import numpy as np
        from jax import lax
        DIM = 192
        INTER = 128
        E = 8
        G = 4
        TOPK_G = 2
        TOPK = 2
        ROUTE_SCALE = 1.0

        def _gate(x2, gate_weight, gate_bias):
            T = x2.shape[0]
            scores = jax.nn.sigmoid(x2 @ gate_weight.T)
            s = scores + gate_bias
            sv = s.reshape(T, G, E // G)
            top2, _ = lax.top_k(sv, 2)
            group_scores = top2.sum(-1)
            _, gidx = lax.top_k(group_scores, TOPK_G)
            gmask = jnp.zeros((T, G), bool).at[jnp.arange(T)[:, None], gidx].set(True)
            masked = jnp.where(gmask[:, :, None], sv, -jnp.inf).reshape(T, E)
            _, idx = lax.top_k(masked, TOPK)
            w = jnp.take_along_axis(scores, idx, axis=1)
            w = w / (w.sum(-1, keepdims=True) + 1e-06) * ROUTE_SCALE
            return (w, idx)
        B, S, D = x.shape
        x2 = x.reshape(-1, D)
        T = x2.shape[0]
        weights, indices = _gate(x2, gate_weight, gate_bias)
        cw = jnp.zeros((T, E), x.dtype).at[jnp.arange(T)[:, None], indices].add(weights)
        h1 = jnp.einsum('td,eid->tei', x2, w1)
        h3 = jnp.einsum('td,eid->tei', x2, w3)
        h = jax.nn.silu(h1) * h3
        y = jnp.einsum('tei,edi,te->td', h, w2, cw)
        z = jax.nn.silu(x2 @ sw1.T) * (x2 @ sw3.T) @ sw2.T
        return (y + z).reshape(B, S, D)
    h = _L0_tok_ref(x, L0_tok_channel_weights)
    h = h + _L0_attn_ref(_layernorm(h, axis=-1), L0_attn_proj_w, L0_attn_proj_b)
    h = h + _L0_ffn_ref(_layernorm(h, axis=-1), L0_ffn_gate_weight, L0_ffn_gate_bias, L0_ffn_w1, L0_ffn_w2, L0_ffn_w3, L0_ffn_sw1, L0_ffn_sw2, L0_ffn_sw3)
    return h

_drawn_inputs = setup_inputs


def setup_inputs(seed=0):
    import zlib

    import numpy as np

    out = dict(_drawn_inputs(seed))
    spreads = {'L0_ffn_gate_bias': (0.0, 0.8)}
    factors = {'L0_attn_proj_w': 8.0,
     'L0_attn_proj_b': 46.313,
     'L0_ffn_gate_weight': 8.0,
     'L0_ffn_w1': 8.0,
     'L0_ffn_w2': 8.0,
     'L0_ffn_w3': 8.0,
     'L0_ffn_sw1': 8.0,
     'L0_ffn_sw2': 8.0,
     'L0_ffn_sw3': 8.0}
    for name, (base, spread) in spreads.items():
        noise = np.random.default_rng([zlib.crc32(name.encode()), seed]).standard_normal(out[name].shape)
        drawn = base * np.exp(spread * noise) if base else spread * noise
        out[name] = jnp.asarray(drawn.astype(out[name].dtype))
    for name, factor in factors.items():
        out[name] = (out[name] * factor).astype(out[name].dtype)
    return out
```

```python
import concourse.bass as bass
from concourse import mybir
from concourse.alu_op_type import AluOpType as ALU
from contextlib import ExitStack

F32 = mybir.dt.float32
BF16 = mybir.dt.bfloat16
ACT = mybir.ActivationFunctionType
AX = mybir.AxisListType

NB, CH, IMG, PATCH = 128, 12, 224, 16
NP = IMG // PATCH
TOK, NQ, D = NP * NP, 64, 192
NK = TOK - NQ
NE, INTER = 8, 128
EX = NE + 1
EPS = 1e-5
GB = 16
NG = NB // GB
CG = 3
HALF = NP // 2
HT = HALF * NP
UNITS = 2 * GB
UC, XC = CH + 2, CH
SPL = 3
ROW = IMG * PATCH
TILES = CG * HALF
SLOTS = 3
assert TILES % SLOTS == 0
CHUNKS = [(True, 0, 512), (True, 512, 512)] + [(False, 512 * i, 512) for i in range(4)] + [(False, 2048, 64)]
KPAD = 2176
NCH = len(CHUNKS)
STEPS = NCH * EX
GT = 8 + 17
CWCOL = 1024 + GB * NK
DVE_J, ACT_J, POOL_J = (0, 7), (7, 10), (10, 14)

ITEMS = [("tok", 0), ("V", 0), ("stats", 0), ("stats2", 0), ("PHT", 0), ("PHT", 1), ("VHw", 0), ("VHT", 0), ("Uw", 0)]
ITEMS += [("S", 0), ("S", 1), ("S", 2), ("U", 0), ("ET", 0), ("ET", 1), ("U", 1), ("AH", 0)]
ITEMS += [("VHw", 1), ("VHT", 1), ("U", 2), ("S", 3), ("S", 4), ("S", 5), ("U", 3), ("ET", 2), ("ET", 3), ("U", 4), ("AH", 1)]
ITEMS += [("U", 5), ("An", 0), ("U", 6), ("M", 0), ("M", 1), ("U", 7), ("M", 2), ("M", 3), ("Xw", 0)]
for _i in range(8):
    ITEMS += [("H", _i), ("X", _i)]
ITEMS += [("x2", 0)] + [("XT", i) for i in range(4)] + [("G", 0), ("gate", 0)] + [("C", i) for i in range(7)]
PE_KINDS = ("tok", "V", "PHT", "VHT", "S", "U", "ET", "AH", "M", "X", "H", "XT", "G", "C")
DVE_KINDS = ("tok", "H", "AH", "ET")
ROUNDS = [it for it in ITEMS if it[0] in PE_KINDS]
NR = len(ROUNDS)
R = {it: i for i, it in enumerate(ROUNDS)}
BYDVE = [sum(1 for it in ROUNDS[:i + 1] if it[0] in DVE_KINDS) for i in range(NR)]
BYACT = [i + 1 - BYDVE[i] for i in range(NR)]
S_IMGS = [(0, 3), (3, 3), (6, 2), (8, 3), (11, 3), (14, 2)]
LINKS = 59

POOL_FROM = [0] * TILES
for _t in range(TILES):
    POOL_FROM[_t] = (_t * 18) // 16 if _t < 16 else 18 + ((_t - 16) * 12) // 5
A_FIRST = 30


def items_at(step):
    if step < A_FIRST:
        return []
    head = [it for it in ITEMS if it[0] != "C"]
    tail = [it for it in ITEMS if it[0] == "C"]
    span = 53 - A_FIRST
    s = step - A_FIRST
    if s < span:
        return head[len(head) * s // span:len(head) * (s + 1) // span]
    n = STEPS - 1 - 53
    s = step - 54
    return tail[s * 7 // (n + 0):(s + 1) * 7 // n] if 0 <= s < n else []


assert [it for s in range(STEPS) for it in items_at(s)] == ITEMS


def pool_at(step):
    return [t for t in range(TILES) if POOL_FROM[t] == step]


class G:

    def __init__(self, k, off):
        self.k, self.off = k, off

    def plus(self, n):
        return G(self.k, self.off + n)

    @property
    def par(self):
        return self.off % 2

    def num(self):
        return self.off if self.k is None else self.k * 2 + self.off

    def at(self, per_group, n):
        v = self.off * per_group + n
        return v if self.k is None else self.k * (2 * per_group) + v

    def bank(self, r):
        return (self.off * NR + r) % 2

    def stored(self, c):
        def upto(g, c):
            n = 0
            for gg in range(g + 1):
                for cc in range(NCH if gg < g else c + 1):
                    if (gg + cc) % 2 == (g + c) % 2:
                        n += 4 if cc < NCH - 1 else 1
            return n
        n = upto(self.off, c) * 16
        return n if self.k is None else self.k * (25 * 16) + n

    def before(self, c):
        n = 4 if c < NCH - 1 else 1
        v = self.stored(c)
        return v - 16 * n


def wait(eng, sem, value):
    if not isinstance(value, int) or value > 0:
        eng.wait_ge(sem, value)


def build(nc, x, cw, proj_w, proj_b, gate_w, gate_b, w1, w2, w3, sw1, sw2, sw3, out):
    ctx = ExitStack()
    with ctx:
        def sb(name, shape, dt=F32):
            return ctx.enter_context(nc.sbuf_tensor(name, shape, dt))

        def sem(name):
            return ctx.enter_context(nc.semaphore(name))

        ident = sb("ident", [128, 128])
        identb = sb("identb", [128, 128], BF16)
        mhalf = sb("mhalf", [128, UNITS])
        keymask = sb("keymask", [HT, UNITS])
        order8 = sb("order8", [128, 8])
        sel = sb("sel", [SPL * NE, NE, 128], BF16)
        CW14 = sb("CW14", [UC, D])
        CWx = sb("CWx", [SPL * SPL * UC, D], BF16)
        blockG = sb("blockG", [128, CG, UNITS * (CH + 1)])
        CWr = sb("CWr", [8 * CH, 3, 4, 128])
        projT = sb("projT", [NQ, 3, D])
        WT0 = sb("WT0", [128, 2 * EX * INTER])
        WT1 = sb("WT1", [64, 2 * EX * INTER])
        Wx = sb("Wx", [SPL * SPL * UC, 2 * EX * INTER + NE], BF16)
        W2T = sb("W2T", [INTER, EX, D])
        gT0 = sb("gT0", [128, NE])
        gT1 = sb("gT1", [64, NE])
        gbias = sb("gbias", [128, NE])
        xt = sb("xt", [128, SLOTS, ROW])
        pooled = sb("pooled", [128, CG, HT])
        kh_sum = sb("kh_sum", [128, 8, (POOL_J[1] - POOL_J[0]) * PATCH])
        tokT = sb("tokT", [126, 2, KPAD + GB * NK], BF16)
        x2T0 = sb("x2T0", [128, 1024])
        x2T1 = sb("x2T1", [64, 1024])
        UTq = sb("UTq", [126, 1024], BF16)
        cwT = sb("cwT", [SPL * NE, CWCOL], BF16)
        h2q = sb("h2q", [128, 8, D])
        HR = 3
        ffn = sb("ffn", [128, HR + 4, 512])
        stage = sb("stage", [128, 2, 4, D])
        Ptok = sb("Ptok", [HT, UNITS, CH])
        V = sb("V", [HT, UNITS, CH + 1])
        val = sb("val", [HT, UNITS, CH + 1])
        res = sb("res", [HT, UNITS, CH + 1])
        stat = sb("stat", [HT, 8, UNITS])
        SPT = sb("SPT", [HT, UNITS, SPL, SPL, UC], BF16)
        PH = sb("PH", [HT, UNITS, 32])
        PHT = sb("PHT", [128, 2, 4, HT])
        VHT = sb("VHT", [128, 8, NQ])
        attw = sb("attw", [128, 8 * 128 + 8 * TOK + 8 * D])
        sums = sb("sums", [NQ, 4, GB])
        Asb = sb("Asb", [NQ, 2, 8 * CH])
        Msb = sb("Msb", [8 * CH, 2, 3 * D])
        bst = sb("bst", [128, 8, 8])
        rq = sb("rq", [128, 3, 8])
        gt = sb("gt", [128, 4, GT * NE])
        gs = sb("gs", [128, 4, GT * 4])
        CS = sb("CS", [128, GT, SPL, NE], BF16)

        h = [ffn[:, i, :] for i in range(HR)]
        silu = [ffn[:, HR + i, :] for i in range(2)]
        gated = [ffn[:, HR + 2 + i, :] for i in range(2)]
        VHpad = attw[0:NQ, 0:1024].rearrange("p (b n) -> p b n", b=8)
        E = attw[0:NQ, 1024:1024 + 8 * TOK].rearrange("p (b n) -> p b n", b=8)
        ET = attw[0:HT, 1024 + 8 * TOK:1024 + 8 * TOK + 16 * NQ].rearrange("p (u q) -> p u q", u=16)
        X2T = [tokT[:, i, 0:KPAD] for i in range(2)]
        UTk = [tokT[:, i, KPAD:] for i in range(2)]
        x2q = attw[:, 1024 + 8 * TOK:].rearrange("p (t d) -> p t d", t=8)
        CWr_src = Msb[:, 0, 0:D]
        w13_nat = ffn[:, :, :].rearrange("p a b -> p (a b)")[:, 0:2 * EX * D].rearrange("p (e d) -> p e d", e=2 * EX)
        w2_natA = attw[:, 0:EX * INTER].rearrange("p (e i) -> p e i", e=EX)
        w2_natB = attw[0:64, EX * INTER:2 * EX * INTER].rearrange("p (e i) -> p e i", e=EX)
        WSP = tokT[0:CH, :, :].rearrange("p a b -> p (a b)")[:, 0:SPL * (2 * EX * INTER + NE)].rearrange(
            "p (s n) -> p s n", s=SPL)
        CSP = SPT[0:UC, :, :, :, :].rearrange("p a b c d -> p (a b c d)")[:, 0:SPL * D].rearrange("p (s n) -> p s n", s=SPL)
        pw_natA = h2q[:, 0, :]
        pw_natB = h2q[0:64, 1, :]
        g_nat = h2q[0:NE, 2, :]
        CWn = h2q[0:CH, 3, :]
        cres = h2q[0:UC, 4, :]
        CWcT = [rq[:, 0:3, :].rearrange("p a b -> p (a b)")[:, 0:CH], Asb[0:64, 0, 0:CH]]
        G13 = sums[0:CH, :, :].rearrange("p a b -> p (a b)")[:, 0:CH + 1]
        rep = sb("rep", [CH, CG, 128])
        repG = gs[:, :, :].rearrange("p a b -> p (a b)")[:, 0:CG * (CH + 1)].rearrange("p (k c) -> p k c", k=CG)
        bmask = PHT[:, 0, 0, 0:UNITS]
        rmask = gt[0:8 * CH, 0, 0:8]
        wres = x2q[0:CH, 0:6, :].rearrange("p a b -> p (a b)")

        bank = [ctx.enter_context(nc.psum_tensor(f"bank{i}", [128, 512], F32)) for i in range(8)]
        h1_ps, h3_ps, cw_ps, out_ps, aux = bank[0:2], bank[2], bank[3], bank[4:6], bank[6:8]

        x_in = [sem(f"x_in{i}") for i in range(SLOTS)]
        dve_summed, act_summed, pool_summed = sem("dve_summed"), sem("act_summed"), sem("pool_summed")
        pool_read, tree_step = sem("pool_read"), sem("tree_step")
        h1_ready, h3_ready, cw_ready = sem("h1_ready"), sem("h3_ready"), sem("cw_ready")
        silu_done, gated_done, h_done = sem("silu_done"), sem("gated_done"), sem("h_done")
        l2_step, evac_dve, evac_act = sem("l2_step"), sem("evac_dve"), sem("evac_act")
        out_stored = [sem(f"out_stored{i}") for i in range(2)]
        aux_full, aux_dve, aux_act = sem("aux_full"), sem("aux_dve"), sem("aux_act")
        dve_link, prep_link = sem("dve_link"), sem("prep_link")
        var_ready, rstd_ready = sem("var_ready"), sem("rstd_ready")
        ph_ready, vh_ready = sem("ph_ready"), sem("vh_ready")
        u_split, x_split, u_rep, x_rep = sem("u_split"), sem("x_split"), sem("u_rep"), sem("x_rep")
        max_ready, x2_ready, cs_ready = sem("max_ready"), sem("x2_ready"), sem("cs_ready")
        w_in, cw_in, pb_in, cwr_in, gb_in = sem("w_in"), sem("cw_in"), sem("pb_in"), sem("cwr_in"), sem("gb_in")
        const_done, prep_full, prep_dve, prep_act = sem("const_done"), sem("prep_full"), sem("prep_dve"), sem("prep_act")
        cwc_ready, cwx_split, w_split, wx_in = sem("cwc_ready"), sem("cwx_split"), sem("w_split"), sem("wx_in")
        ready = sem("ready")
        pool_link = sem("pool_link")
        pe_passed, dve_passed, pool_passed = sem("pe_passed"), sem("dve_passed"), sem("pool_passed")

        xv = x.rearrange("(g b) (k c) (s i h) w -> g k i b (c s) (h w)", b=GB, k=CG, s=2, h=PATCH)

        PREP = [("CWcT", 0), ("CWcT", 1), ("G", 0), ("gate", 0), ("repG", 0), ("gate", 1)]
        PREP += [("W0", i) for i in range(5)] + [("W1", i) for i in range(5)]
        PREP += [("Wc", i) for i in range(5)] + [("w2", i) for i in range(5)] + [("proj", 0), ("proj", 1)]
        WCOLS = 2 * EX * INTER
        P_AT = {it: i for i, it in enumerate(PREP)}

        def w4(i):
            return 4 * i, min(4, 2 * EX - 4 * i)

        def wc(i):
            return 512 * i, min(512, WCOLS + NE - 512 * i)

        def prep_copies(r):
            kind, i = PREP[r]
            ps = aux[r % 2]
            if kind == "CWcT":
                return [(CWcT[i][0:128 if i == 0 else 64, :], ps[0:128 if i == 0 else 64, 0:CH])]
            if kind == "G":
                return [(G13[:, 0:CH], ps[0:CH, 0:CH])]
            if kind == "repG":
                return [(repG, ps[:, 0:CG * (CH + 1)].rearrange("p (k c) -> p k c", k=CG))]
            if kind == "gate":
                n = 128 if i == 0 else 64
                return [((gT0 if i == 0 else gT1)[0:n, :], ps[0:n, 0:NE])]
            if kind in ("W0", "W1"):
                n = 128 if kind == "W0" else 64
                a, k = w4(i)
                return [((WT0 if kind == "W0" else WT1)[:, a * 128:(a + k) * 128], ps[0:n, 0:k * 128])]
            if kind == "w2":
                k = min(2, EX - 2 * i)
                return [(W2T[:, 2 * i:2 * i + k, :].rearrange("p e d -> p (e d)"), ps[:, 0:k * D])]
            if kind == "proj":
                k = 2 if i == 0 else 1
                return [(projT[:, 2 * i:2 * i + k, :].rearrange("p e d -> p (e d)"), ps[0:NQ, 0:k * D])]
            raise AssertionError(kind)

        block = ctx.enter_context(nc.Block())

        @block.sync
        def _(sp):
            sp.dma_start(CWn, cw).then_inc(cw_in, 16)
            for k, (w, shared) in enumerate(((w1, sw1), (w3, sw3))):
                sp.dma_start(w13_nat[:, k * EX:k * EX + NE, :], w.rearrange("e i d -> i e d")).then_inc(w_in, 16)
                sp.dma_start(w13_nat[:, k * EX + NE, :], shared).then_inc(w_in, 16)
            for nat, a, b in ((w2_natA, 0, 128), (w2_natB, 128, D)):
                sp.dma_start(nat[:, 0:NE, :], w2[:, a:b, :].rearrange("e d i -> d e i")).then_inc(w_in, 16)
                sp.dma_start(nat[:, NE, :], sw2[a:b, :]).then_inc(w_in, 16)
            sp.dma_start(pw_natA, proj_w[0:128, :]).then_inc(w_in, 16)
            sp.dma_start(pw_natB, proj_w[128:D, :]).then_inc(w_in, 16)
            sp.dma_start(g_nat, gate_w).then_inc(w_in, 16)
            sp.dma_start(gbias[:, :], gate_b.partition_broadcast(128)).then_inc(gb_in, 16)
            for t in range(SLOTS):
                sp.dma_start(xt[:, t, :], xv[0, t // HALF, t % HALF]).then_inc(x_in[t], 16)
            sp.wait_ge(const_done, 1)
            sp.dma_start(CW14[CH + 1:UC, :], proj_b.rearrange("(a d) -> a d", a=1)).then_inc(pb_in, 16)
            sp.wait_ge(cwc_ready, 1)
            for b in range(8):
                sp.dma_start(CWr_src[b * CH:(b + 1) * CH, :], CW14[0:CH, :]).then_inc(cwr_in, 16)
            sp.wait_ge(cwx_split, 1)
            for s in range(SPL):
                for q in range(SPL):
                    a = (s * SPL + q) * UC
                    sp.dma_start(CWx[a:a + UC, :], CSP[:, s, :]).then_inc(wx_in, 16)

            def load(g, t):
                for s in (dve_summed, act_summed, pool_read):
                    wait(sp, s, g.at(TILES, t - SLOTS + 1))
                sp.dma_start(xt[:, t % SLOTS, :], xv[g.num(), t // HALF, t % HALF]).then_inc(x_in[t % SLOTS], 16)

            def store(g, c):
                query, col, n = CHUNKS[c]
                st = stage[:, (g.par + c) % 2, :, :]
                done = out_stored[(g.par + c) % 2]
                if query:
                    sp.wait_ge(evac_dve, g.at(4, 2 * c + 2))
                else:
                    sp.wait_ge(evac_act, g.at(9, 2 * (c - 2) + 2 if c < NCH - 1 else 9))
                og = out.rearrange("(g b) t d -> g b t d", b=GB)[g.num()]
                for t in range((n + 127) // 128):
                    if query:
                        b0 = (col + 128 * t) // NQ
                        dst = og[b0:b0 + 2, 0:NQ, :]
                    elif c < NCH - 1:
                        dst = og[4 * t:4 * t + 4, NQ + col // GB:NQ + col // GB + 32, :]
                    else:
                        dst = og[:, TOK - 4:TOK, :]
                    sp.dma_start(dst, st[0:min(n, 128), t, :]).then_inc(done, 16)

            def ffn_dma(g, nxt, loads_after):
                for step in range(STEPS):
                    c, e = divmod(step, EX)
                    if nxt:
                        for t in pool_at(step):
                            if t + SLOTS < TILES:
                                load(g.plus(1), t + SLOTS)
                            elif loads_after:
                                load(g.plus(2), t + SLOTS - TILES)
                    if e == 3 and c > 0:
                        store(g, c - 1)
                store(g, NCH - 1)

            for t in range(3, TILES):
                load(G(None, 0), t)
            for t in range(3):
                load(G(None, 1), t)
            ffn_dma(G(None, 0), True, True)
            with sp.Fori(0, 2) as k:
                for off in (1, 2):
                    ffn_dma(G(k, off), True, True)
            ffn_dma(G(None, 5), True, True)
            ffn_dma(G(None, 6), True, False)
            ffn_dma(G(None, 7), False, False)
            for s in range(2):
                sp.wait_ge(out_stored[s], 25 * 16 * NG // 2)

        @block.gpsimd
        def _(pool):
            links = [0]

            def link(ins):
                links[0] += 1
                ins.then_inc(pool_link, 1)
                pool.wait_ge(pool_link, links[0])

            nc.gpsimd.memset(CW14[:, :], 1.0).then_inc(const_done, 1)
            link(nc.gpsimd.memset(ident[:, :], 0.0))
            link(nc.gpsimd.affine_select(out=ident[:, :], in_=ident[:, :], compare_op=ALU.not_equal, fill=1.0,
                                         base=0, pattern=[[-1, 128]], channel_multiplier=1))
            nc.gpsimd.tensor_copy(identb[:, :], ident[:, :]).then_inc(const_done, 1)
            nc.gpsimd.memset(mhalf[:, :], -0.5)
            for k in range(CG):
                link(nc.gpsimd.memset(rep[:, k, :], 0.0))
                link(nc.gpsimd.affine_select(out=rep[:, k, :].rearrange("p (b c s) -> p b c s", b=GB, c=4),
                                             in_=rep[:, k, :].rearrange("p (b c s) -> p b c s", b=GB, c=4),
                                             compare_op=ALU.not_equal, fill=1.0, base=-4 * k,
                                             pattern=[[0, GB], [-1, 4], [0, 2]], channel_multiplier=1))
            link(nc.gpsimd.memset(bmask, 0.0))
            for c in range(4):
                link(nc.gpsimd.affine_select(out=bmask.rearrange("p (s b) -> p s b", s=2),
                                             in_=bmask.rearrange("p (s b) -> p s b", s=2),
                                             compare_op=ALU.not_equal, fill=1.0, base=-2 * c,
                                             pattern=[[-1, 2], [-8, GB]], channel_multiplier=1))
            link(nc.gpsimd.memset(rmask, 1.0))
            link(nc.gpsimd.affine_select(out=rmask, in_=rmask, compare_op=ALU.is_ge, fill=0.0, base=0,
                                         pattern=[[-CH, 8]], channel_multiplier=1))
            link(nc.gpsimd.affine_select(out=rmask, in_=rmask, compare_op=ALU.is_ge, fill=0.0, base=CH - 1,
                                         pattern=[[CH, 8]], channel_multiplier=-1))
            link(nc.gpsimd.memset(sel[:, :, :], 0.0))
            for s in range(SPL):
                link(nc.gpsimd.affine_select(out=sel[:, :, :], in_=sel[:, :, :], compare_op=ALU.not_equal, fill=1.0,
                                             base=-NE * s, pattern=[[-1, NE], [0, 128]], channel_multiplier=1))
            for i in range(NE):
                nc.gpsimd.memset(order8[:, i:i + 1], float(NE - i))
            nc.gpsimd.memset(Wx[:, :], 0.0)
            link(nc.gpsimd.memset(keymask[:, :], 1.0))
            link(nc.gpsimd.memset(keymask[0:NQ, 0:GB], 0.0))
            nc.gpsimd.memset(PH[:, :, :], 0.0).then_inc(const_done, 1)

            def pool_tile(g, t):
                a, b = POOL_J
                n = b - a
                src = xt[:, t % SLOTS, :].rearrange("p (h w) -> p h w", h=PATCH)[:, :, a * PATCH:b * PATCH]
                row = kh_sum[:, 0, :].rearrange("p (j w) -> p j w", w=PATCH)

                def add(step, out, in0, in1):
                    nc.gpsimd.tensor_tensor(out=out, in0=in0, in1=in1, op=ALU.add).then_inc(tree_step, 1)
                    pool.wait_ge(tree_step, g.at(6 * TILES, 6 * t + step))

                pool.wait_ge(x_in[t % SLOTS], g.at(16 * (TILES // SLOTS), 16 * (t // SLOTS + 1)))
                wait(pool, pool_summed, g.at(TILES, t))
                nc.gpsimd.tensor_tensor(out=kh_sum[:, 0:8, :], in0=src[:, 0:8, :], in1=src[:, 8:16, :],
                                        op=ALU.add).then_inc(pool_read, 1)
                pool.wait_ge(pool_read, g.at(TILES, t + 1))
                add(1, kh_sum[:, 0:4, :], kh_sum[:, 0:4, :], kh_sum[:, 4:8, :])
                add(2, kh_sum[:, 0:2, :], kh_sum[:, 0:2, :], kh_sum[:, 2:4, :])
                add(3, kh_sum[:, 0, :], kh_sum[:, 0, :], kh_sum[:, 1, :])
                add(4, row[:, :, 0:8], row[:, :, 0:8], row[:, :, 8:16])
                add(5, row[:, :, 0:4], row[:, :, 0:4], row[:, :, 4:8])
                add(6, row[:, :, 0:2], row[:, :, 0:2], row[:, :, 2:4])
                if t == 0:
                    wait(pool, aux_full, g.at(NR, R[("V", 0)] + 1 - NR))
                at = (t % HALF) * NP
                nc.gpsimd.tensor_tensor(out=pooled[:, t // HALF, at + a:at + b], in0=row[:, :, 0], in1=row[:, :, 1],
                                        op=ALU.add).then_inc(pool_summed, 1)

            def item(g, kind, i):
                if kind == "stats":
                    pool.wait_ge(var_ready, g.at(3, 1))
                    nc.gpsimd.tensor_tensor(out=stat[:, 1, :], in0=stat[:, 0, :], in1=mhalf[0:HT, :],
                                            op=ALU.pow).then_inc(rstd_ready, 1)
                elif kind == "stats2":
                    pool.wait_ge(var_ready, g.at(3, 2))
                    nc.gpsimd.tensor_tensor(out=stat[:, 4, :], in0=stat[:, 3, :], in1=mhalf[0:HT, :],
                                            op=ALU.pow).then_inc(rstd_ready, 1)
                elif kind in ("Uw", "Xw"):
                    pool.wait_ge(u_split if kind == "Uw" else x_split, g.at(1, 1))
                    pool.sem_inc(pool_passed, 1)
                    done = u_rep if kind == "Uw" else x_rep
                    for r in (1, 2):
                        nc.gpsimd.tensor_copy(SPT[:, :, r, :, :].rearrange("p u s c -> p u (s c)"),
                                              SPT[:, :, 0, :, :].rearrange("p u s c -> p u (s c)")).then_inc(done, 1)
                elif kind == "x2":
                    pool.wait_ge(var_ready, g.at(3, 3))
                    nc.gpsimd.tensor_tensor(out=rq[:, 1, :], in0=rq[:, 0, :], in1=mhalf[:, 0:8],
                                            op=ALU.pow).then_inc(rstd_ready, 1)

            def ffn_pool(g, nxt):
                if not nxt:
                    return
                for step in range(STEPS):
                    for t in pool_at(step):
                        pool_tile(g.plus(1), t)
                    for kind, i in items_at(step):
                        item(g.plus(1), kind, i)

            for t in range(TILES):
                pool_tile(G(None, 0), t)
            pool.wait_ge(ready, 1)
            for kind, i in ITEMS:
                item(G(None, 0), kind, i)
            ffn_pool(G(None, 0), True)
            with pool.Fori(0, 2) as k:
                for off in (1, 2):
                    ffn_pool(G(k, off), True)
            ffn_pool(G(None, 5), True)
            ffn_pool(G(None, 6), True)

        @block.scalar
        def _(act):
            for r in range(1, len(PREP), 2):
                act.wait_ge(prep_full, r + 1)
                for o, i in prep_copies(r) if PREP[r][0] != "Wc" else []:
                    nc.scalar.copy(o, i).then_inc(prep_act, 1)
                if PREP[r][0] == "Wc":
                    a, n = wc(PREP[r][1])
                    if PREP[r][1] >= 2:
                        act.wait_ge(w_split, PREP[r][1] - 1)
                    nc.scalar.copy(wres[:, 512:512 + n], aux[1][0:CH, 0:n]).then_inc(prep_act, 1)

            act.wait_ge(w_split, 5)
            act.wait_ge(const_done, 3)
            for s in range(SPL):
                for q in range(SPL):
                    a = (s * SPL + q) * UC
                    act.dma_start(Wx[a:a + XC, :], WSP[:, s, :]).then_inc(wx_in, 16)

            def act_tile(g, t):
                act.wait_ge(x_in[t % SLOTS], g.at(16 * (TILES // SLOTS), 16 * (t // SLOTS + 1)))
                if t == 0:
                    wait(act, aux_full, g.at(NR, R[("V", 0)] + 1 - NR))
                src = xt[:, t % SLOTS, :].rearrange("p (h j w) -> p h j w", h=PATCH, j=NP)
                for j in range(*ACT_J):
                    at = (t % HALF) * NP + j
                    last = nc.scalar.activation(src[:, :, j, :], src[:, :, j, :],
                                                ACT.Copy, accum_out=pooled[:, t // HALF, at:at + 1])
                last.then_inc(act_summed, 1)

            def item(g, kind, i):
                if kind not in PE_KINDS or kind in DVE_KINDS:
                    return
                r = R[(kind, i)]
                ps = aux[g.bank(r)]
                act.wait_ge(aux_full, g.at(NR, r + 1))
                if kind == "V":
                    nc.scalar.copy(V[:, :, :].rearrange("p u c -> p (u c)"), ps[0:HT, 0:UNITS * (CH + 1)])\
                      .then_inc(aux_act, 1)
                elif kind == "PHT":
                    nc.scalar.copy(PHT[:, i, :, :].rearrange("p b t -> p (b t)"), ps[:, 0:4 * HT]).then_inc(aux_act, 1)
                elif kind == "VHT":
                    nc.scalar.copy(VHT[:, :, :].rearrange("p b q -> p (b q)"), ps[:, :]).then_inc(aux_act, 1)
                elif kind == "U":
                    src = ps[0:126, 0:2 * TOK].rearrange("p (b t) -> p b t", b=2)
                    nc.scalar.copy(UTq[:, :].rearrange("p (b t) -> p b t", b=GB)[:, 2 * i:2 * i + 2, :], src[:, :, 0:NQ])
                    keys_out(UTk[g.par], src[:, :, NQ:TOK], i).then_inc(aux_act, 1)
                elif kind == "X":
                    src = ps[0:126, 0:2 * NK].rearrange("p (b t) -> p b t", b=2)
                    keys_out(X2T[g.par], src, i).then_inc(aux_act, 1)
                elif kind == "S":
                    b0, nb = S_IMGS[i]
                    act.wait_ge(max_ready, g.at(6, i + 1))
                    for b in range(b0, b0 + nb):
                        last = nc.scalar.activation(E[:, b % 8, NQ:TOK], ps[0:NQ, (b - b0) * NK:(b - b0 + 1) * NK], ACT.Exp,
                                                    bias=sums[:, 0, b:b + 1], accum_out=sums[:, 1, b:b + 1])
                    last.then_inc(aux_act, 1)
                elif kind == "M":
                    half, part = divmod(i, 2)
                    n = 2 * D if part == 0 else D
                    nc.scalar.copy(Msb[:, half, 2 * D * part:2 * D * part + n], ps[0:8 * CH, 0:n]).then_inc(aux_act, 1)
                elif kind == "XT":
                    q, part = divmod(i, 2)
                    dst = x2T0 if part == 0 else x2T1
                    n = 128 if part == 0 else 64
                    nc.scalar.copy(dst[:, 512 * q:512 * q + 512], ps[0:n, :]).then_inc(aux_act, 1)
                elif kind == "G":
                    nc.scalar.activation(gt[:, 0, :], ps[:, 0:GT * NE], ACT.Exp, scale=-1.0).then_inc(aux_act, 1)
                elif kind == "C":
                    n = 512 if i < 6 else 64
                    nc.scalar.copy(cwT[:, 512 * i:512 * i + n], ps[0:SPL * NE, 0:n]).then_inc(aux_act, 1)

            def keys_out(dst, src, i):
                nc.scalar.copy(dst[:, 0:2048].rearrange("p (c b k) -> p b c k", c=4, b=GB)[:, 2 * i:2 * i + 2, :, :],
                               src[:, :, 0:128].rearrange("p b (c k) -> p b c k", c=4))
                return nc.scalar.copy(dst[:, 2048:2112].rearrange("p (b k) -> p b k", b=GB)[:, 2 * i:2 * i + 2, :],
                                      src[:, :, 128:NK])

            def evacuate(g, c):
                n = CHUNKS[c][2]
                act.wait_ge(l2_step, g.at(STEPS, (c + 1) * EX))
                wait(act, out_stored[(g.par + c) % 2], g.before(c))
                st = stage[:, (g.par + c) % 2, :, :].rearrange("p t d -> p (t d)")
                if c < NCH - 1:
                    for b in range(2):
                        nc.scalar.copy(st[:, 2 * D * b:2 * D * b + 2 * D], out_ps[b][:, 0:2 * D]).then_inc(evac_act, 1)
                else:
                    nc.scalar.copy(st[0:n, 0:D], out_ps[0][0:n, 0:D]).then_inc(evac_act, 1)

            def ffn_act(g, nxt):
                for step in range(STEPS):
                    c, e = divmod(step, EX)
                    n = CHUNKS[c][2]
                    if e == 2 and c > 2:
                        evacuate(g, c - 1)
                    act.wait_ge(h1_ready, g.at(STEPS, step + 1))
                    wait(act, gated_done, g.at(STEPS, step - 1))
                    p = (g.par + step) % 2
                    nc.scalar.activation(silu[p][:, 0:n], h1_ps[p][:, 0:n], ACT.Silu).then_inc(silu_done, 1)
                    if nxt:
                        for t in pool_at(step):
                            act_tile(g.plus(1), t)
                        for kind, i in items_at(step):
                            item(g.plus(1), kind, i)
                evacuate(g, NCH - 1)

            for t in range(TILES):
                act_tile(G(None, 0), t)
            act.wait_ge(ready, 1)
            for kind, i in ITEMS:
                item(G(None, 0), kind, i)
            ffn_act(G(None, 0), True)
            with act.Fori(0, 2) as k:
                for off in (1, 2):
                    ffn_act(G(k, off), True)
            ffn_act(G(None, 5), True)
            ffn_act(G(None, 6), True)
            ffn_act(G(None, 7), False)

        @block.vector
        def _(dve):
            links = [0]
            v = nc.vector

            plinks = [0]

            def plink(ins):
                plinks[0] += 1
                ins.then_inc(prep_link, 1)
                dve.wait_ge(prep_link, plinks[0])

            dve.wait_ge(cw_in, 16)
            dve.wait_ge(const_done, 1)
            plink(v.tensor_reduce(out=sums[0:CH, 1, 0:1], in_=CWn, axis=AX.X, op=ALU.add))
            plink(v.tensor_scalar(G13[:, CH:CH + 1], sums[0:CH, 1, 0:1], 1.0 / D, None, ALU.mult))
            v.tensor_scalar(CW14[0:CH, :], CWn, G13[:, CH:CH + 1], None, ALU.subtract).then_inc(cwc_ready, 1)
            dve.wait_ge(cwc_ready, 1)
            dve.wait_ge(pb_in, 16)
            plink(v.tensor_copy(CSP[:, 0, :], CW14[:, :]))
            plink(v.tensor_tensor(out=cres, in0=CW14[:, :], in1=CSP[:, 0, :], op=ALU.subtract))
            plink(v.tensor_copy(CSP[:, 1, :], cres))
            v.tensor_tensor(out=CSP[:, 2, :], in0=cres, in1=CSP[:, 1, :], op=ALU.subtract).then_inc(cwx_split, 1)

            def split_w(i, src):
                a, n = wc(i)
                plink(v.tensor_copy(WSP[:, 0, a:a + n], src))
                plink(v.tensor_tensor(out=src, in0=src, in1=WSP[:, 0, a:a + n], op=ALU.subtract))
                plink(v.tensor_copy(WSP[:, 1, a:a + n], src))
                v.tensor_tensor(out=WSP[:, 2, a:a + n], in0=src, in1=WSP[:, 1, a:a + n],
                                op=ALU.subtract).then_inc(w_split, 1)

            for r in range(0, len(PREP), 2):
                dve.wait_ge(prep_full, r + 1)
                if PREP[r][0] == "Wc":
                    i = PREP[r][1]
                    a, n = wc(i)
                    plink(v.tensor_copy(wres[:, 0:n], aux[0][0:CH, 0:n]))
                    v.sem_inc(prep_dve, 1)
                    split_w(i, wres[:, 0:n])
                    if i + 1 < 5:
                        dve.wait_ge(prep_act, r // 2 + 1)
                        split_w(i + 1, wres[:, 512:512 + wc(i + 1)[1]])
                else:
                    for o, i in prep_copies(r):
                        v.tensor_copy(o, i).then_inc(prep_dve, 1)
                if PREP[r][0] == "repG":
                    dve.wait_ge(prep_dve, r // 2 + 1)
                    dve.wait_ge(const_done, 3)
                    for k in range(CG):
                        plink(v.tensor_tensor(
                            out=blockG[:, k, :].rearrange("p (u c) -> p u c", u=UNITS),
                            in0=bmask.unsqueeze(2).to_broadcast([128, UNITS, CH + 1]),
                            in1=repG[:, k, :].unsqueeze(1).to_broadcast([128, UNITS, CH + 1]), op=ALU.mult))
            dve.wait_ge(cwr_in, 16 * 8)
            for b in range(8):
                plink(v.tensor_scalar(CWr[:, :, b // 2, 64 * (b % 2):64 * (b % 2) + 64],
                                      CWr_src.rearrange("p (i r) -> p r i", r=3), rmask[:, b:b + 1], None, ALU.mult))
            dve.wait_ge(prep_full, len(PREP))
            dve.wait_ge(wx_in, 18 * 16)
            plink(v.memset(VHpad, 0.0))
            plink(v.memset(E, 0.0))
            plink(v.memset(SPT[:, :, :, :, :].rearrange("p a b c d -> p (a b c d)"), 0.0))
            plink(v.memset(SPT[0:NQ, 0:GB, 0, 0, CH + 1:UC], 1.0))
            for i in range(2):
                plink(v.memset(X2T[i][:, 2112:KPAD], 0.0))
            dve.wait_ge(gb_in, 16)
            v.sem_inc(ready, 1)

            def link(g, ins):
                links[0] += 1
                ins.then_inc(dve_link, 1)
                dve.wait_ge(dve_link, g.at(LINKS, links[0]))

            def dve_tile(g, t, lo, hi):
                if lo == DVE_J[0]:
                    dve.wait_ge(x_in[t % SLOTS], g.at(16 * (TILES // SLOTS), 16 * (t // SLOTS + 1)))
                    if t == 0:
                        wait(dve, aux_full, g.at(NR, R[("V", 0)] + 1 - NR))
                src = xt[:, t % SLOTS, :].rearrange("p (h j w) -> p j h w", h=PATCH, j=NP)
                at = (t % HALF) * NP
                ins = v.tensor_reduce(out=pooled[:, t // HALF, at + lo:at + hi], in_=src[:, lo:hi, :, :],
                                      axis=AX.XY, op=ALU.add)
                if hi == DVE_J[1]:
                    ins.then_inc(dve_summed, 1)

            def first_of_max(g, vals, n, out_mask, best, tmp):
                shape = [128, GT, n]
                link(g, v.tensor_reduce(out=best, in_=vals, axis=AX.X, op=ALU.max))
                link(g, v.tensor_tensor(out=tmp, in0=vals, in1=best.unsqueeze(2).to_broadcast(shape), op=ALU.is_equal))
                link(g, v.tensor_tensor(out=tmp, in0=tmp, in1=order8[:, NE - n:NE].unsqueeze(1).to_broadcast(shape),
                                        op=ALU.mult))
                link(g, v.tensor_reduce(out=best, in_=tmp, axis=AX.X, op=ALU.max))
                link(g, v.tensor_tensor(out=out_mask, in0=tmp, in1=best.unsqueeze(2).to_broadcast(shape),
                                        op=ALU.is_equal))

            def split3(g, src, n, done):
                link(g, v.tensor_copy(SPT[:, :, 0, 0, 0:n], src))
                link(g, v.tensor_tensor(out=res[:, :, 0:n], in0=src, in1=SPT[:, :, 0, 0, 0:n], op=ALU.subtract))
                link(g, v.tensor_copy(SPT[:, :, 0, 1, 0:n], res[:, :, 0:n]))
                v.tensor_tensor(out=SPT[:, :, 0, 2, 0:n], in0=res[:, :, 0:n], in1=SPT[:, :, 0, 1, 0:n],
                                op=ALU.subtract).then_inc(done, 1)

            def item(g, kind, i):
                if kind in DVE_KINDS:
                    r = R[(kind, i)]
                    ps = aux[g.bank(r)]
                    dve.wait_ge(aux_full, g.at(NR, r + 1))
                if kind == "tok":
                    for k in range(CG):
                        ins = v.tensor_copy(
                            Ptok[:, :, 4 * k:4 * k + 4].rearrange("p (s b) c -> p s b c", s=2),
                            ps[0:HT, 128 * k:128 * k + 128].rearrange("p (b c s) -> p s b c", b=GB, c=4))
                    ins.then_inc(aux_dve, 1)
                elif kind == "stats":
                    links[0] = 0
                    dve.wait_ge(aux_dve, g.at(BYDVE[-1], BYDVE[R[("tok", 0)]]))
                    dve.wait_ge(aux_act, g.at(BYACT[-1], BYACT[R[("V", 0)]]))
                    link(g, v.tensor_tensor(out=val[:, :, 0:CH], in0=Ptok[:, :, :], in1=V[:, :, 0:CH], op=ALU.mult))
                    link(g, v.tensor_reduce(out=stat[:, 2, :], in_=val[:, :, 0:CH], axis=AX.X, op=ALU.add))
                    link(g, v.tensor_scalar(stat[:, 2, :], stat[:, 2, :], 1.0 / D, 0.0, ALU.mult, ALU.max))
                    v.tensor_scalar(stat[:, 0, :], stat[:, 2, :], EPS, None, ALU.add).then_inc(var_ready, 1)
                elif kind == "stats2":
                    dve.wait_ge(rstd_ready, g.at(3, 1))
                    link(g, v.tensor_tensor(out=stat[:, 5, :], in0=stat[:, 1, :], in1=keymask[:, :], op=ALU.mult))
                    link(g, v.tensor_scalar(stat[:, 5, :], stat[:, 5, :], 1.0, None, ALU.add))
                    link(g, v.tensor_tensor(out=stat[:, 6, :], in0=stat[:, 5, :], in1=stat[:, 5, :], op=ALU.mult))
                    link(g, v.tensor_tensor(out=stat[:, 6, :], in0=stat[:, 6, :], in1=stat[:, 2, :], op=ALU.mult))
                    v.tensor_scalar(stat[:, 3, :], stat[:, 6, :], EPS, None, ALU.add).then_inc(var_ready, 1)
                    wait(dve, aux_full, g.at(NR, R[("AH", 1)] + 1 - NR))
                    v.tensor_tensor(out=PH[:, :, 0:CH], in0=Ptok[:, :, :],
                                    in1=stat[:, 1, :].unsqueeze(2).to_broadcast([HT, UNITS, CH]),
                                    op=ALU.mult).then_inc(ph_ready, 1)
                elif kind == "VHw":
                    if i == 1:
                        dve.wait_ge(aux_full, g.at(NR, R[("VHT", 0)] + 1))
                    for q in range(2):
                        src = V[0:NQ, 8 * i + 4 * q:8 * i + 4 * q + 4, 0:CH]
                        dst = attw[0:NQ, 512 * q:512 * q + 640].rearrange("p (m n) -> p m n", m=4)[:, :, 0:CH]
                        ins = v.scalar_tensor_tensor(out=dst, in0=src, scalar=float(D // 12) ** -0.5,
                                                     in1=stat[0:NQ, 1, 8 * i + 4 * q:8 * i + 4 * q + 4].unsqueeze(2)
                                                     .to_broadcast([NQ, 4, CH]), op0=ALU.mult, op1=ALU.mult)
                    ins.then_inc(vh_ready, 1)
                elif kind == "Uw":
                    wait(dve, aux_full, g.at(NR, R[("X", 7)] + 1 - NR))
                    link(g, v.tensor_tensor(out=val[:, :, 0:CH], in0=Ptok[:, :, :],
                                            in1=stat[:, 5, :].unsqueeze(2).to_broadcast([HT, UNITS, CH]), op=ALU.mult))
                    link(g, v.tensor_copy(val[:, :, CH:CH + 1], V[:, :, CH:CH + 1]))
                    split3(g, val[:, :, :], CH + 1, u_split)
                elif kind == "Xw":
                    dve.wait_ge(rstd_ready, g.at(3, 2))
                    dve.wait_ge(u_split, g.at(1, 1))
                    link(g, v.tensor_tensor(out=stat[:, 7, :], in0=stat[:, 4, :], in1=stat[:, 5, :], op=ALU.mult))
                    link(g, v.tensor_tensor(out=val[:, :, 0:CH], in0=Ptok[:, :, :],
                                            in1=stat[:, 7, :].unsqueeze(2).to_broadcast([HT, UNITS, CH]), op=ALU.mult))
                    dve.wait_ge(aux_full, g.at(NR, R[("U", 7)] + 1))
                    split3(g, val[:, :, 0:CH], CH, x_split)
                elif kind == "S_max":
                    b0, nb = S_IMGS[i]
                    r = R[("S", i)]
                    dve.wait_ge(aux_full, g.at(NR, r + 1))
                    v.tensor_reduce(out=sums[:, 0, b0:b0 + nb],
                                    in_=aux[g.bank(r)][0:NQ, 0:nb * NK].rearrange("p (b k) -> p b k", b=nb),
                                    axis=AX.X, op=ALU.max, negate=True).then_inc(max_ready, 1)
                elif kind == "ET":
                    v.tensor_copy(ET[:, 8 * (i % 2):8 * (i % 2) + 8, :].rearrange("p u q -> p (u q)"), ps[0:HT, :])\
                     .then_inc(aux_dve, 1)
                elif kind == "AH":
                    link(g, v.reciprocal(sums[:, 2, 8 * i:8 * i + 8], sums[:, 1, 8 * i:8 * i + 8]))
                    v.tensor_tensor(out=Asb[:, i, :].rearrange("p (b c) -> p b c", b=8),
                                    in0=ps[0:NQ, 0:8 * CH].rearrange("p (b c) -> p b c", b=8),
                                    in1=sums[:, 2, 8 * i:8 * i + 8].unsqueeze(2).to_broadcast([NQ, 8, CH]),
                                    op=ALU.mult).then_inc(aux_dve, 1)
                elif kind == "H":
                    v.bn_stats(bst[:, i, 0:6], ps[:, 0:D])
                    v.tensor_copy(h2q[:, i, :], ps[:, 0:D]).then_inc(aux_dve, 1)
                elif kind == "x2":
                    dve.wait_ge(aux_dve, g.at(BYDVE[-1], BYDVE[R[("H", 7)]]))
                    dve.sem_inc(dve_passed, 1)
                    for t in range(8):
                        ins = v.bn_aggr(bst[:, t, 6:8], bst[:, t, 0:6])
                    link(g, ins)
                    v.tensor_scalar(rq[:, 0, :], bst[:, :, 7], EPS, None, ALU.add).then_inc(var_ready, 1)
                    dve.wait_ge(rstd_ready, g.at(3, 3))
                    for t in range(8):
                        v.tensor_scalar(x2q[:, t, :], h2q[:, t, :], bst[:, t, 6:7], rq[:, 1, t:t + 1],
                                        ALU.subtract, ALU.mult).then_inc(x2_ready, 1)
                elif kind == "gate":
                    gates(g)

            def gates(g):
                t3 = "p (t e) -> p t e"
                a, b, c, d = [gt[:, j, :].rearrange(t3, t=GT) for j in range(4)]
                ga, gb_, gc = [gs[:, j, :].rearrange(t3, t=GT) for j in range(3)]
                best = gs[:, 3, 0:GT]
                dve.wait_ge(aux_act, g.at(BYACT[-1], BYACT[R[("G", 0)]]))
                link(g, v.tensor_scalar(a, a, 1.0, None, ALU.add))
                link(g, v.reciprocal(a, a))
                link(g, v.tensor_tensor(out=b, in0=a, in1=gbias[:, :].unsqueeze(1).to_broadcast([128, GT, NE]),
                                        op=ALU.add))
                link(g, v.tensor_reduce(out=ga, in_=gt[:, 1, :].rearrange("p (t m e) -> p t m e", t=GT, m=4),
                                        axis=AX.X, op=ALU.add))
                first_of_max(g, ga, 4, gb_, best, gc)
                link(g, v.scalar_tensor_tensor(out=ga, in0=gb_, scalar=-1e30, in1=ga, op0=ALU.mult, op1=ALU.add))
                first_of_max(g, ga, 4, gc, best, ga)
                link(g, v.tensor_tensor(out=gb_, in0=gb_, in1=gc, op=ALU.add))
                m4 = gs[:, 1, :].rearrange("p (t m) -> p t m", t=GT).unsqueeze(3).to_broadcast([128, GT, 4, 2])
                b4, c4 = [gt[:, j, :].rearrange("p (t m e) -> p t m e", t=GT, m=4) for j in (1, 2)]
                link(g, v.tensor_tensor(out=b4, in0=b4, in1=m4, op=ALU.mult))
                link(g, v.tensor_scalar(gb_, gb_, -1.0, 1e30, ALU.add, ALU.mult))
                link(g, v.tensor_tensor(out=b4, in0=b4, in1=m4, op=ALU.add))
                first_of_max(g, b, NE, d, best, c)
                link(g, v.scalar_tensor_tensor(out=b, in0=d, scalar=-2e30, in1=b, op0=ALU.mult, op1=ALU.add))
                first_of_max(g, b, NE, b, best, c)
                link(g, v.tensor_tensor(out=d, in0=d, in1=b, op=ALU.add))
                link(g, v.tensor_tensor(out=a, in0=a, in1=d, op=ALU.mult))
                link(g, v.tensor_reduce(out=best, in_=a, axis=AX.X, op=ALU.add))
                link(g, v.tensor_scalar(best, best, 1e-6, None, ALU.add))
                link(g, v.reciprocal(best, best))
                link(g, v.tensor_tensor(out=a, in0=a, in1=best.unsqueeze(2).to_broadcast([128, GT, NE]), op=ALU.mult))
                wait(dve, aux_full, g.at(NR, 0))
                link(g, v.tensor_copy(CS[:, :, 0, :], a))
                link(g, v.tensor_tensor(out=b, in0=a, in1=CS[:, :, 0, :], op=ALU.subtract))
                link(g, v.tensor_copy(CS[:, :, 1, :], b))
                v.tensor_tensor(out=CS[:, :, 2, :], in0=b, in1=CS[:, :, 1, :], op=ALU.subtract).then_inc(cs_ready, 1)
                assert links[0] == LINKS, links[0]

            def items(g, todo):
                for kind, i in todo:
                    if kind == "S":
                        item(g, "S_max", i)
                    else:
                        item(g, kind, i)

            def evacuate(g, c):
                dve.wait_ge(l2_step, g.at(STEPS, (c + 1) * EX))
                wait(dve, out_stored[(g.par + c) % 2], g.before(c))
                for b in range(2):
                    v.tensor_tensor(out=stage[:, (g.par + c) % 2, 2 * b:2 * b + 2, :],
                                    in0=out_ps[b][:, 0:2 * D].rearrange("p (t d) -> p t d", t=2),
                                    in1=h2q[:, 4 * c + 2 * b:4 * c + 2 * b + 2, :], op=ALU.add).then_inc(evac_dve, 1)

            def ffn_dve(g, nxt):
                late = []
                for step in range(STEPS):
                    c, e = divmod(step, EX)
                    n = CHUNKS[c][2]
                    if e == 2 and c in (1, 2):
                        evacuate(g, c - 1)
                    p = (g.par + step) % 2
                    dve.wait_ge(silu_done, g.at(STEPS, step + 1))
                    dve.wait_ge(h3_ready, g.at(STEPS, step + 1))
                    if e == NE:
                        wait(dve, l2_step, g.at(STEPS, step - HR + 1))
                        v.tensor_tensor(out=h[step % HR][:, 0:n], in0=h3_ps[:, 0:n], in1=silu[p][:, 0:n],
                                        op=ALU.mult).then_inc(gated_done, 1)
                    else:
                        v.tensor_tensor(out=gated[p][:, 0:n], in0=h3_ps[:, 0:n], in1=silu[p][:, 0:n],
                                        op=ALU.mult).then_inc(gated_done, 1)
                    for t, lo, hi in late:
                        dve_tile(g.plus(1), t, lo, hi)
                    late = []
                    if nxt:
                        mid = (DVE_J[0] + DVE_J[1]) // 2
                        for t in pool_at(step):
                            dve_tile(g.plus(1), t, DVE_J[0], mid)
                            if step < 18:
                                dve_tile(g.plus(1), t, mid, DVE_J[1])
                            else:
                                late.append((t, mid, DVE_J[1]))
                    if e < NE:
                        dve.wait_ge(gated_done, g.at(STEPS, step + 1))
                        dve.wait_ge(cw_ready, g.at(NCH * NE, c * NE + e + 1))
                        wait(dve, l2_step, g.at(STEPS, step - HR + 1))
                        v.tensor_tensor(out=h[step % HR][:, 0:n], in0=cw_ps[:, 0:n], in1=gated[p][:, 0:n],
                                        op=ALU.mult).then_inc(h_done, 1)
                    if nxt:
                        items(g.plus(1), items_at(step))

            for t in range(TILES):
                dve_tile(G(None, 0), t, *DVE_J)
            items(G(None, 0), ITEMS)
            ffn_dve(G(None, 0), True)
            with dve.Fori(0, 2) as k:
                for off in (1, 2):
                    ffn_dve(G(k, off), True)
            ffn_dve(G(None, 5), True)
            ffn_dve(G(None, 6), True)
            ffn_dve(G(None, 7), False)

        @block.tensor
        def _(pe):
            mm = nc.tensor.matmul
            pe.wait_ge(const_done, 2)
            for r, (kind, i) in enumerate(PREP):
                ps = aux[r % 2]
                if r >= 2:
                    pe.wait_ge(prep_dve if r % 2 == 0 else prep_act, r // 2)
                if kind == "CWcT":
                    pe.wait_ge(cwc_ready, 1)
                    n = 128 if i == 0 else 64
                    last = nc.tensor.transpose(ps[0:n, 0:CH], CW14[0:CH, 128 * i:128 * i + n], ident[0:CH, 0:CH])
                elif kind == "G":
                    pe.wait_ge(prep_act, 1)
                    mm(ps[0:CH, 0:CH], CWcT[0], CWcT[0], start=True, stop=False)
                    last = mm(ps[0:CH, 0:CH], CWcT[1], CWcT[1], start=False, stop=True)
                elif kind == "repG":
                    pe.wait_ge(prep_dve, P_AT[("G", 0)] // 2 + 1)
                    pe.wait_ge(const_done, 3)
                    for k in range(CG):
                        last = mm(ps[:, k * (CH + 1):(k + 1) * (CH + 1)], rep[:, k, :], G13, start=True, stop=True)
                elif kind == "gate":
                    pe.wait_ge(w_in, 11 * 16)
                    n = 128 if i == 0 else 64
                    last = nc.tensor.transpose(ps[0:n, 0:NE], g_nat[:, 128 * i:128 * i + n], ident[0:NE, 0:NE])
                elif kind in ("W0", "W1"):
                    a, k = w4(i)
                    lo, n = (0, 128) if kind == "W0" else (128, 64)
                    for j in range(k):
                        last = nc.tensor.transpose(ps[0:n, 128 * j:128 * j + 128], w13_nat[:, a + j, lo:lo + n], ident[:, :])
                elif kind == "Wc":
                    pe.wait_ge(prep_dve, (P_AT[("W1", 4)] + 2) // 2)
                    pe.wait_ge(prep_act, (P_AT[("W1", 4)] + 1) // 2)
                    a, n = wc(i)
                    m = min(n, WCOLS - a)
                    mm(ps[0:CH, 0:m], CWcT[0], WT0[:, a:a + m], start=True, stop=False)
                    last = mm(ps[0:CH, 0:m], CWcT[1], WT1[:, a:a + m], start=False, stop=True)
                    if m < n:
                        mm(ps[0:CH, m:n], CWcT[0], gT0[:, :], start=True, stop=False)
                        last = mm(ps[0:CH, m:n], CWcT[1], gT1[:, :], start=False, stop=True)
                elif kind == "w2":
                    for j in range(min(2, EX - 2 * i)):
                        nc.tensor.transpose(ps[:, D * j:D * j + 128], w2_natA[:, 2 * i + j, :], ident[:, :])
                        last = nc.tensor.transpose(ps[:, D * j + 128:D * j + D], w2_natB[:, 2 * i + j, :], ident[0:64, 0:64])
                elif kind == "proj":
                    for j in range(2 if i == 0 else 1):
                        q = 2 * i + j
                        nc.tensor.transpose(ps[0:NQ, D * j:D * j + 128], pw_natA[:, NQ * q:NQ * q + NQ], ident[:, :])
                        last = nc.tensor.transpose(ps[0:NQ, D * j + 128:D * j + D], pw_natB[:, NQ * q:NQ * q + NQ],
                                                   ident[0:64, 0:64])
                last.then_inc(prep_full, 1)
            pe.wait_ge(prep_dve, (len(PREP) + 1) // 2)
            pe.wait_ge(prep_act, len(PREP) // 2)
            pe.wait_ge(ready, 1)

            def item(g, kind, i):
                if kind not in PE_KINDS:
                    return
                r = R[(kind, i)]
                ps = aux[g.bank(r)]
                act_rounds = dve_rounds = None
                if r < 2:
                    act_rounds = BYACT[NR - 2 + r] - BYACT[-1]
                elif ROUNDS[r - 2][0] in DVE_KINDS:
                    dve_rounds = BYDVE[r - 2]
                else:
                    act_rounds = BYACT[r - 2]
                source = {"S": ("VHT", i // 3), "ET": ("S", 3 * (i // 2) + (1 if i % 2 == 0 else 2)),
                          "AH": ("ET", 2 * i + 1), "M": ("AH", i // 2), "H": ("M", 3 if i >= 4 else 1), "G": ("XT", 3)}
                if kind in source:
                    src = R[source[kind]]
                    if kind == "H":
                        src = max(src, R[("U", 7)])
                    if ROUNDS[src][0] in DVE_KINDS:
                        dve_rounds = max(dve_rounds or 0, BYDVE[src])
                    else:
                        act_rounds = max(act_rounds or 0, BYACT[src])
                if act_rounds is not None:
                    wait(pe, aux_act, g.at(BYACT[-1], act_rounds))
                if dve_rounds is not None:
                    wait(pe, aux_dve, g.at(BYDVE[-1], dve_rounds))
                if kind == "tok":
                    for s in (dve_summed, act_summed, pool_summed):
                        pe.wait_ge(s, g.at(TILES, TILES))
                    for k in range(CG):
                        last = nc.tensor.transpose(ps[0:HT, 128 * k:128 * k + 128], pooled[:, k, :], ident[:, :])
                elif kind == "V":
                    for k in range(CG):
                        last = mm(ps[0:HT, 0:UNITS * (CH + 1)], pooled[:, k, :], blockG[:, k, :],
                                  start=(k == 0), stop=(k == CG - 1))
                elif kind == "PHT":
                    pe.wait_ge(ph_ready, g.at(1, 1))
                    for b in range(4):
                        u = GB * i + 4 * b
                        last = nc.tensor.transpose(ps[:, HT * b:HT * b + HT],
                                                   PH[:, u:u + 4, :].rearrange("p u c -> p (u c)"), ident[0:HT, 0:HT])
                elif kind == "VHT":
                    pe.wait_ge(vh_ready, g.at(2, i + 1))
                    pe.sem_inc(pe_passed, 1)
                    for b in range(8):
                        last = nc.tensor.transpose(ps[:, NQ * b:NQ * b + NQ], VHpad[:, b, :], ident[0:NQ, 0:NQ])
                elif kind == "S":
                    b0, nb = S_IMGS[i]
                    for b in range(b0, b0 + nb):
                        at = (b - b0) * NK
                        mm(ps[0:NQ, at:at + HT - NQ], VHT[:, b % 8, :], PHT[:, 0, b // 4, NQ:HT], start=True, stop=True)
                        last = mm(ps[0:NQ, at + HT - NQ:at + NK], VHT[:, b % 8, :], PHT[:, 1, b // 4, :],
                                  start=True, stop=True)
                elif kind == "ET":
                    pe.sem_inc(pe_passed, 1)
                    for j in range(8):
                        b, s = 4 * (i % 2) + j // 2, j % 2
                        last = nc.tensor.transpose(ps[0:HT, NQ * j:NQ * j + NQ], E[:, b, HT * s:HT * s + HT],
                                                   ident[0:NQ, 0:NQ])
                elif kind == "AH":
                    for b in range(8):
                        for s in range(2):
                            last = mm(ps[0:NQ, CH * b:CH * b + CH], ET[:, 2 * b + s, :], PH[:, GB * s + 8 * i + b, 0:CH],
                                      start=(s == 0), stop=(s == 1))
                elif kind == "M":
                    half, part = divmod(i, 2)
                    n = 2 if part == 0 else 1
                    last = mm(ps[0:8 * CH, 0:n * D], Asb[:, half, :],
                              projT[:, 2 * part:2 * part + n, :].rearrange("p r d -> p (r d)"), start=True, stop=True)
                elif kind == "U":
                    pe.wait_ge(u_rep, g.at(2, 2))
                    for j in range(2):
                        for s in range(2):
                            at = TOK * j + HT * s
                            last = mm(ps[0:126, at:at + HT],
                                      SPT[:, GB * s + 2 * i + j, :, :, :].rearrange("p a b c -> p (a b c)"),
                                      identb[0:HT, 0:HT], start=True, stop=True)
                elif kind == "X":
                    pe.wait_ge(x_rep, g.at(2, 2))
                    for j in range(2):
                        for s in range(2):
                            at = NK * j + (HT - NQ) * s
                            n = HT - NQ if s == 0 else HT
                            last = mm(ps[0:126, at:at + n],
                                      SPT[:, GB * s + 2 * i + j, :, :, :].rearrange("p a b c -> p (a b c)"),
                                      identb[0:HT, HT - n:HT], start=True, stop=True)
                elif kind == "H":
                    mm(ps[:, 0:D], UTq[:, 128 * i:128 * i + 128], CWx[:, :], start=True, stop=False)
                    for q in range(3):
                        last = mm(ps[:, 0:D], CWr[:, q, i % 4, :], Msb[:, i // 4, D * q:D * q + D],
                                  start=False, stop=(q == 2))
                elif kind == "XT":
                    q, part = divmod(i, 2)
                    pe.wait_ge(x2_ready, g.at(8, 4 * q + 4))
                    pe.sem_inc(pe_passed, 1)
                    lo, n = (0, 128) if part == 0 else (128, 64)
                    for j in range(4):
                        last = nc.tensor.transpose(ps[0:n, 128 * j:128 * j + 128], x2q[:, 4 * q + j, lo:lo + n], ident[:, :])
                elif kind == "G":
                    for t in range(8):
                        o = ps[:, NE * t:NE * t + NE]
                        mm(o, x2T0[:, 128 * t:128 * t + 128], gT0[:, :], start=True, stop=False)
                        mm(o, x2T1[:, 128 * t:128 * t + 128], gT1[:, :], start=False, stop=True)
                    for t in range(17):
                        last = mm(ps[:, NE * (8 + t):NE * (9 + t)], X2T[g.par][0:126, 128 * t:128 * t + 128],
                                  Wx[:, WCOLS:WCOLS + NE], start=True, stop=True)
                elif kind == "C":
                    pe.wait_ge(cs_ready, g.at(1, 1))
                    for j in range(4 if i < 6 else 1):
                        n = 128 if i < 6 else 64
                        last = mm(ps[0:SPL * NE, 128 * j:128 * j + n], CS[:, 4 * i + j, :, :].rearrange("p s e -> p (s e)"),
                                  identb[:, 0:n], start=True, stop=True)
                last.then_inc(aux_full, 1)

            def layer2(g, step):
                c, e = divmod(step, EX)
                query, col, n = CHUNKS[c]
                if e == 0:
                    if c in (1, 2):
                        pe.wait_ge(evac_dve, g.at(4, 2 * c))
                    elif c == 0:
                        wait(pe, evac_act, g.at(9, 0))
                    else:
                        pe.wait_ge(evac_act, g.at(9, 2 * (c - 2)))
                pe.wait_ge(h_done, g.at(NCH * NE, c * NE + min(e + 1, NE)))
                if e == NE:
                    pe.wait_ge(gated_done, g.at(STEPS, step + 1))
                m = min(n, 128)
                for t in range((n + 127) // 128):
                    o = out_ps[t // 2][0:m, D * (t % 2):D * (t % 2) + D]
                    if e == 0 and not query:
                        mm(o, UTk[g.par][:, col + 128 * t:col + 128 * t + m], CWx[:, :], start=(t % 2 == 0), stop=False,
                           skip_group_check=True)
                    last = mm(o, h[step % HR][:, 128 * t:128 * t + m], W2T[:, e, :],
                              start=(e == 0 and query and t % 2 == 0), stop=(e == NE), skip_group_check=True)
                last.then_inc(l2_step, 1)

            def ffn_pe(g, nxt):
                for step in range(STEPS):
                    c, e = divmod(step, EX)
                    query, col, n = CHUNKS[c]
                    p = (g.par + step) % 2
                    wait(pe, silu_done, g.at(STEPS, step - 1))
                    if step == 0:
                        pe.wait_ge(aux_act, g.at(BYACT[-1], BYACT[-1]))
                    for k, o in ((0, h1_ps[p]), (1, h3_ps)):
                        if k == 1:
                            if step >= 2:
                                layer2(g, step - 2)
                            wait(pe, gated_done, g.at(STEPS, step))
                        w = (k * EX + e) * INTER
                        if query:
                            mm(o[:, 0:n], WT0[:, w:w + INTER], x2T0[:, col:col + n], start=True, stop=False)
                            last = mm(o[:, 0:n], WT1[:, w:w + INTER], x2T1[:, col:col + n], start=False, stop=True)
                        else:
                            last = mm(o[:, 0:n], Wx[:, w:w + INTER], X2T[g.par][:, col:col + n], start=True, stop=True)
                        last.then_inc(h1_ready if k == 0 else h3_ready, 1)
                    if e < NE:
                        wait(pe, h_done, g.at(NCH * NE, c * NE + e))
                        at = 512 * c
                        mm(cw_ps[:, 0:n], sel[:, e, :], cwT[:, at:at + n], start=True, stop=True).then_inc(cw_ready, 1)
                    if nxt:
                        for kind, i in items_at(step):
                            item(g.plus(1), kind, i)
                layer2(g, STEPS - 2)
                layer2(g, STEPS - 1)

            for kind, i in ITEMS:
                item(G(None, 0), kind, i)
            ffn_pe(G(None, 0), True)
            with pe.Fori(0, 2) as k:
                for off in (1, 2):
                    ffn_pe(G(k, off), True)
            ffn_pe(G(None, 5), True)
            ffn_pe(G(None, 6), True)
            ffn_pe(G(None, 7), False)


INS = ["x", "L0_tok_channel_weights", "L0_attn_proj_w", "L0_attn_proj_b", "L0_ffn_gate_weight", "L0_ffn_gate_bias",
       "L0_ffn_w1", "L0_ffn_w2", "L0_ffn_w3", "L0_ffn_sw1", "L0_ffn_sw2", "L0_ffn_sw3"]


def kernel(**inputs):
    import numpy as np
    import concourse.bacc as bacc
    from concourse.bass_utils import run_bass_kernel_spmd

    nc = bacc.Bacc("TRN2", target_bir_lowering=False, num_devices=1)
    arrays, args = {}, []
    for name in INS:
        a = np.ascontiguousarray(inputs[name])
        arrays[f"in_{name}"] = a
        args.append(nc.dram_tensor(f"in_{name}", a.shape, mybir.dt.from_np(a.dtype), kind="ExternalInput").ap())
    out = nc.dram_tensor("out_0", (NB, TOK, D), F32, kind="ExternalOutput").ap()
    build(nc, *args, out)
    r = run_bass_kernel_spmd(nc, [arrays], core_ids=[0])
    return r.results[0]["out_0"]
```

```python
import concourse.bass as bass
from concourse import mybir
from concourse.alu_op_type import AluOpType as ALU
from contextlib import ExitStack

F32 = mybir.dt.float32
BF16 = mybir.dt.bfloat16
F32R = mybir.dt.float32r
ACT = mybir.ActivationFunctionType
AX = mybir.AxisListType

NB, CH, IMG, PATCH = 128, 12, 224, 16
NP = IMG // PATCH
TOK, NQ, D = NP * NP, 64, 192
NK = TOK - NQ
NE, INTER = 8, 128
EX = NE + 1
EPS = 1e-5
GB = 16
NG = NB // GB
CG = 3
HALF = NP // 2
HT = HALF * NP
UNITS = 2 * GB
UC, XC = CH + 2, CH
SPL = 3
ROW = IMG * PATCH
TILES = CG * HALF
SLOTS = 2
CHUNKS = [(True, 0, 512), (True, 512, 512)] + [(False, 512 * i, 512) for i in range(4)] + [(False, 2048, 64)]
KPAD = 2176
NCH = len(CHUNKS)
STEPS = NCH * EX
GT = 8 + 17
CWCOL = 1024 + GB * NK
SHARE = {"dve": (0, 4), "act": (4, 8), "pool": (8, NP)}
SHARE0 = {"dve": (0, 8), "act": (8, 12), "pool": (12, NP)}
POOL_MAX = 6
ROWS = 3

PLAN = {
    5: [("fin", 0)],
    6: [("tok", 0), ("V", 0)],
    7: [("stats", 0)],
    9: [("stats2", 0)],
    10: [("PHT", 0), ("VHw", 0), ("Uw", 0)],
    11: [("PHT", 1), ("VHT", 0), ("Uw", 1)],
    12: [("S", 0), ("Uw", 2)],
    13: [("S", 1)],
    14: [("S", 2), ("VHw", 1)],
    15: [("ET", 0), ("VHT", 1)],
    16: [("ET", 1), ("U", 0)],
    17: [("AH", 0), ("U", 1)],
    18: [("S", 3), ("U", 2)],
    19: [("S", 4)],
    20: [("S", 5), ("M", 0)],
    21: [("ET", 2), ("M", 1)],
    22: [("ET", 3), ("U", 3)],
    23: [("U", 4), ("U", 5)],
    24: [("AH", 1), ("U", 6)],
    25: [("U", 7), ("M", 2)],
    26: [("M", 3), ("Xw", 0)],
    27: [("H", 0), ("Xw", 1)],
    28: [("H", 1), ("Xw", 2)],
    29: [("H", 2)],
    30: [("H", 3)],
    31: [("H", 4)],
    32: [("H", 5), ("X", 0)],
    33: [("H", 6), ("X", 1)],
    34: [("H", 7), ("X", 2)],
    35: [("x2", 0), ("X", 3)],
    36: [("X", 4)],
    37: [("X", 5)],
    38: [("x2", 1)],
    39: [("x2", 2), ("X", 6)],
    40: [("XT", 0)],
    41: [("XT", 1), ("X", 7)],
    42: [("x2", 3)],
    43: [("x2", 4)],
    44: [("XT", 2)],
    45: [("XT", 3)],
    47: [("G", 0)],
    48: [("gate", 0)],
    49: [("gate", 1)],
    50: [("gate", 2)],
    51: [("gate", 3)],
    52: [("gate", 4)],
    53: [("gate", 5), ("gate", 6)],
    54: [("gate", 7), ("gate", 8)],
    55: [("gate", 9)],
    56: [("gate", 10)],
    57: [("gate", 11)],
    58: [("gate", 12)],
    59: [("C", 0), ("C", 1)],
    60: [("C", 2), ("C", 3)],
    61: [("C", 4), ("C", 5)],
    62: [("C", 6)],
}
A_FIRST = 5
ITEMS = [it for s in sorted(PLAN) for it in PLAN[s]]
PE_KINDS = ("tok", "V", "PHT", "VHT", "S", "U", "ET", "AH", "M", "X", "H", "XT", "G", "C")
DVE_KINDS = ("tok", "H", "AH", "ET", "XT")
ROUNDS = [it for it in ITEMS if it[0] in PE_KINDS]
NR = len(ROUNDS)
R = {it: i for i, it in enumerate(ROUNDS)}
BYDVE = [sum(1 for it in ROUNDS[:i + 1] if it[0] in DVE_KINDS) for i in range(NR)]
BYACT = [i + 1 - BYDVE[i] for i in range(NR)]
S_IMGS = [(0, 3), (3, 3), (6, 2), (8, 3), (11, 3), (14, 2)]
LINKS = 59

LATE = {7 + (i * 11) // 8: i for i in range(8)}
LATE.update({19 + 5 * i: 8 + i for i in range(9)})
EARLY = {i + i // 3: 17 + i for i in range(4)}
assert sorted(LATE.values()) + sorted(EARLY.values()) == list(range(TILES)) and max(EARLY) < A_FIRST


def items_at(step):
    return PLAN.get(step, [])


def tiles_at(g, step, groups_left=2):
    found = []
    if groups_left >= 1 and step in EARLY:
        found.append((g.plus(1), EARLY[step]))
    if groups_left >= 2 and step in LATE:
        found.append((g.plus(2), LATE[step]))
    return found


class G:

    def __init__(self, k, off):
        self.k, self.off = k, off

    def plus(self, n):
        return G(self.k, self.off + n)

    @property
    def par(self):
        return self.off % 2

    def num(self):
        return self.off if self.k is None else self.k * 2 + self.off

    def at(self, per_group, n):
        v = self.off * per_group + n
        return v if self.k is None else self.k * (2 * per_group) + v

    def slot(self, t):
        return (self.off * TILES + t) % SLOTS

    def landed(self, t):
        v = 16 * ((self.off * TILES + t) // SLOTS + 1)
        return v if self.k is None else self.k * (16 * 2 * TILES // SLOTS) + v

    def bank(self, r):
        return (self.off * NR + r) % 2

    def stored(self, c):
        def upto(g, c):
            n = 0
            for gg in range(g + 1):
                for cc in range(NCH if gg < g else c + 1):
                    if (gg + cc) % 2 == (g + c) % 2:
                        n += 4 if cc < NCH - 1 else 1
            return n
        n = upto(self.off, c) * 16
        return n if self.k is None else self.k * (25 * 16) + n

    def before(self, c):
        n = 4 if c < NCH - 1 else 1
        v = self.stored(c)
        return v - 16 * n


def wait(eng, sem, value):
    if not isinstance(value, int) or value > 0:
        eng.wait_ge(sem, value)


def build(nc, x, cw, proj_w, proj_b, gate_w, gate_b, w1, w2, w3, sw1, sw2, sw3, out):
    ctx = ExitStack()
    with ctx:
        def sb(name, shape, dt=F32):
            return ctx.enter_context(nc.sbuf_tensor(name, shape, dt))

        def sem(name):
            return ctx.enter_context(nc.semaphore(name))

        ident = sb("ident", [128, 128])
        identb = sb("identb", [128, 128], BF16)
        mhalf = sb("mhalf", [128, UNITS])
        keymask = sb("keymask", [HT, UNITS])
        order8 = sb("order8", [128, 8])
        sel = sb("sel", [SPL * NE, NE, 128], BF16)
        CW14 = sb("CW14", [UC, D])
        CWx = sb("CWx", [SPL * SPL * UC, D], BF16)
        blockG = sb("blockG", [128, CG, UNITS * (CH + 1)])
        CWr = sb("CWr", [8 * CH, 3, 4, 128])
        projT = sb("projT", [NQ, 3, D])
        WT0h = sb("WT0h", [128, 2 * EX * INTER], F32R)
        WT0l = sb("WT0l", [128, 2 * EX * INTER], F32R)
        WT1s = sb("WT1s", [128, 2 * EX * INTER], F32R)
        Wx = sb("Wx", [SPL * SPL * UC, 2 * EX * INTER + NE], BF16)
        W2T = sb("W2T", [INTER, EX, D])
        gT0h, gT0l, gT1s = sb("gT0h", [128, NE], F32R), sb("gT0l", [128, NE], F32R), sb("gT1s", [128, NE], F32R)
        gbias = sb("gbias", [128, NE])
        xt = sb("xt", [128, SLOTS, ROW])
        pooled = sb("pooled", [128, CG, HT])
        kh_sum = sb("kh_sum", [128, 8, POOL_MAX * PATCH])
        row_sum = sb("row_sum", [128, ROWS, POOL_MAX * PATCH])
        tokT = sb("tokT", [126, 2, KPAD + GB * NK], BF16)
        x0h, x0l = sb("x0h", [128, 1024], F32R), sb("x0l", [128, 1024], F32R)
        x1h, x1l = sb("x1h", [128, 1024], F32R), sb("x1l", [128, 1024], F32R)
        UTq = sb("UTq", [126, 1024], BF16)
        cwT = sb("cwT", [SPL * NE, CWCOL], BF16)
        h2q = sb("h2q", [128, 8, D])
        HR = 3
        ffn = sb("ffn", [128, HR + 4, 512])
        stage = sb("stage", [128, 2, 4, D])
        Ptok = sb("Ptok", [HT, UNITS, CH])
        V = sb("V", [HT, UNITS, CH + 1])
        val = sb("val", [HT, UNITS, CH + 1])
        res = sb("res", [HT, UNITS, CH + 1])
        stat = sb("stat", [HT, 8, UNITS])
        SPT = sb("SPT", [HT, UNITS, SPL, SPL, UC], BF16)
        PH = sb("PH", [HT, UNITS, 32])
        PHT = sb("PHT", [128, 2, 4, HT])
        VHT = sb("VHT", [128, 8, NQ])
        attw = sb("attw", [128, 8 * 128 + 8 * TOK + 16 * NQ])
        sums = sb("sums", [NQ, 4, GB])
        Asb = sb("Asb", [NQ, 2, 8 * CH])
        Msb = sb("Msb", [8 * CH, 2, 3 * D])
        bst = sb("bst", [128, 8, 8])
        rq = sb("rq", [128, 3, 8])
        gt = sb("gt", [128, 4, GT * NE])
        gs = sb("gs", [128, 4, GT * 4])
        CS = sb("CS", [128, GT, SPL, NE], BF16)

        h = [ffn[:, i, :] for i in range(HR)]
        silu = [ffn[:, HR + i, :] for i in range(2)]
        gated = [ffn[:, HR + 2 + i, :] for i in range(2)]
        VHpad = attw[0:NQ, 0:1024].rearrange("p (b n) -> p b n", b=8)
        E = attw[0:NQ, 1024:1024 + 8 * TOK].rearrange("p (b n) -> p b n", b=8)
        ET = attw[0:HT, 1024 + 8 * TOK:].rearrange("p (u q) -> p u q", u=16)
        X2T = [tokT[:, i, 0:KPAD] for i in range(2)]
        UTk = [tokT[:, i, KPAD:] for i in range(2)]
        x2q = attw[:, 1024 + 8 * TOK:1024 + 8 * TOK + 4 * D].rearrange("p (t d) -> p t d", t=4)
        CWr_src = Msb[:, 0, 0:D]
        w13_nat = ffn[:, :, :].rearrange("p a b -> p (a b)")[:, 0:2 * EX * D].rearrange("p (e d) -> p e d", e=2 * EX)
        w2_natA = attw[:, 0:EX * INTER].rearrange("p (e i) -> p e i", e=EX)
        w2_natB = attw[0:64, EX * INTER:2 * EX * INTER].rearrange("p (e i) -> p e i", e=EX)
        WSP = tokT[0:CH, :, :].rearrange("p a b -> p (a b)")[:, 0:SPL * (2 * EX * INTER + NE)].rearrange(
            "p (s n) -> p s n", s=SPL)
        CSP = SPT[0:UC, :, :, :, :].rearrange("p a b c d -> p (a b c d)")[:, 0:SPL * D].rearrange("p (s n) -> p s n", s=SPL)
        pw_natA = h2q[:, 0, :]
        pw_natB = h2q[0:64, 1, :]
        g_nat = h2q[0:NE, 2, :]
        CWn = h2q[0:CH, 3, :]
        cres = h2q[0:UC, 4, :]
        CWcT = [rq[:, 0:3, :].rearrange("p a b -> p (a b)")[:, 0:CH], gs[:, 3, 0:CH]]
        G13 = sums[0:CH, :, :].rearrange("p a b -> p (a b)")[:, 0:CH + 1]
        rep = val[0:CH, :, :].rearrange("p a b -> p (a b)")[:, 0:CG * 128].rearrange("p (k n) -> p k n", k=CG)
        repG = gs[:, :, :].rearrange("p a b -> p (a b)")[:, 0:CG * (CH + 1)].rearrange("p (k c) -> p k c", k=CG)
        bmask = PHT[:, 0, 0, 0:UNITS]
        rmask = gt[0:8 * CH, 0, 0:8]
        wres = attw[0:CH, 2 * EX * INTER:2 * EX * INTER + 1024]

        bank = [ctx.enter_context(nc.psum_tensor(f"bank{i}", [128, 512], F32)) for i in range(8)]
        h1_ps, h3_ps, cw_ps, out_ps, aux = bank[0:2], bank[2], bank[3], bank[4:6], bank[6:8]

        x_in = [sem(f"x_in{i}") for i in range(SLOTS)]
        dve_summed, act_summed, pool_summed = sem("dve_summed"), sem("act_summed"), sem("pool_summed")
        pool_read, tree_step, rows_used = sem("pool_read"), sem("tree_step"), sem("rows_used")
        h1_ready, h3_ready, cw_ready = sem("h1_ready"), sem("h3_ready"), sem("cw_ready")
        silu_done, gated_done, h_done = sem("silu_done"), sem("gated_done"), sem("h_done")
        l2_step, evac_dve, evac_act = sem("l2_step"), sem("evac_dve"), sem("evac_act")
        out_stored = [sem(f"out_stored{i}") for i in range(2)]
        aux_full, aux_dve, aux_act = sem("aux_full"), sem("aux_dve"), sem("aux_act")
        high_ready = sem("high_ready")
        dve_link, prep_link = sem("dve_link"), sem("prep_link")
        var_ready, rstd_ready = sem("var_ready"), sem("rstd_ready")
        ph_ready, vh_ready = sem("ph_ready"), sem("vh_ready")
        u_split, x_split, u_rep, x_rep = sem("u_split"), sem("x_split"), sem("u_rep"), sem("x_rep")
        max_ready, x2_ready, cs_ready = sem("max_ready"), sem("x2_ready"), sem("cs_ready")
        w_in, cw_in, pb_in, cwr_in, gb_in = sem("w_in"), sem("cw_in"), sem("pb_in"), sem("cwr_in"), sem("gb_in")
        const_done, prep_full, prep_dve, prep_act = sem("const_done"), sem("prep_full"), sem("prep_dve"), sem("prep_act")
        cwc_ready, cwx_split, w_split, wx_in = sem("cwc_ready"), sem("cwx_split"), sem("w_split"), sem("wx_in")
        ready = sem("ready")
        pool_link = sem("pool_link")
        pe_passed, dve_passed, pool_passed = sem("pe_passed"), sem("dve_passed"), sem("pool_passed")

        xv = x.rearrange("(g b) (k c) (s i h) w -> g k i b (c s) (h w)", b=GB, k=CG, s=2, h=PATCH)

        PREP = [("CWcT", 0), ("CWcT", 1), ("G", 0), ("gate", 0), ("repG", 0), ("gate", 1)]
        PREP += [("W0", i) for i in range(5)] + [("W1", i) for i in range(5)]
        PREP += [("Wc", i) for i in range(5)] + [("w2", i) for i in range(5)] + [("proj", 0), ("proj", 1)]
        WCOLS = 2 * EX * INTER
        P_AT = {it: i for i, it in enumerate(PREP)}
        P_DVE = [kind in ("W0", "W1", "gate") or i % 2 == 0 for i, (kind, _) in enumerate(PREP)]
        P_DVE_N = [sum(P_DVE[:i + 1]) for i in range(len(PREP))]
        P_ACT_N = [i + 1 - P_DVE_N[i] for i in range(len(PREP))]

        def w4(i):
            return 4 * i, min(4, 2 * EX - 4 * i)

        def wc(i):
            return 512 * i, min(512, WCOLS + NE - 512 * i)

        def prep_copies(r):
            kind, i = PREP[r]
            ps = aux[r % 2]
            if kind == "CWcT":
                return [(CWcT[i], ps[:, 0:CH])]
            if kind == "G":
                return [(G13[:, 0:CH], ps[0:CH, 0:CH])]
            if kind == "repG":
                return [(repG, ps[:, 0:CG * (CH + 1)].rearrange("p (k c) -> p k c", k=CG))]
            if kind == "w2":
                k = min(2, EX - 2 * i)
                return [(W2T[:, 2 * i:2 * i + k, :].rearrange("p e d -> p (e d)"), ps[:, 0:k * D])]
            if kind == "proj":
                k = 2 if i == 0 else 1
                return [(projT[:, 2 * i:2 * i + k, :].rearrange("p e d -> p (e d)"), ps[0:NQ, 0:k * D])]
            raise AssertionError(kind)

        def split_dst(r):
            kind, i = PREP[r]
            if kind == "gate":
                return NE, (gT0h if i == 0 else gT1s)[:, :], gT0l[:, :] if i == 0 else None
            a, k = w4(i)
            a, n = a * 128, k * 128
            return n, (WT0h if kind == "W0" else WT1s)[:, a:a + n], WT0l[:, a:a + n] if kind == "W0" else None

        block = ctx.enter_context(nc.Block())

        @block.sync
        def _(sp):
            sp.dma_start(CWn, cw).then_inc(cw_in, 16)
            for k, (w, shared) in enumerate(((w1, sw1), (w3, sw3))):
                sp.dma_start(w13_nat[:, k * EX:k * EX + NE, :], w.rearrange("e i d -> i e d")).then_inc(w_in, 16)
                sp.dma_start(w13_nat[:, k * EX + NE, :], shared).then_inc(w_in, 16)
            for nat, a, b in ((w2_natA, 0, 128), (w2_natB, 128, D)):
                sp.dma_start(nat[:, 0:NE, :], w2[:, a:b, :].rearrange("e d i -> d e i")).then_inc(w_in, 16)
                sp.dma_start(nat[:, NE, :], sw2[a:b, :]).then_inc(w_in, 16)
            sp.dma_start(pw_natA, proj_w[0:128, :]).then_inc(w_in, 16)
            sp.dma_start(pw_natB, proj_w[128:D, :]).then_inc(w_in, 16)
            sp.dma_start(g_nat, gate_w).then_inc(w_in, 16)
            sp.dma_start(gbias[:, :], gate_b.partition_broadcast(128)).then_inc(gb_in, 16)
            for t in range(SLOTS):
                sp.dma_start(xt[:, t, :], xv[0, t // HALF, t % HALF]).then_inc(x_in[t], 16)
            sp.wait_ge(const_done, 1)
            sp.dma_start(CW14[CH + 1:UC, :], proj_b.rearrange("(a d) -> a d", a=1)).then_inc(pb_in, 16)
            sp.wait_ge(cwc_ready, 1)
            for b in range(8):
                sp.dma_start(CWr_src[b * CH:(b + 1) * CH, :], CW14[0:CH, :]).then_inc(cwr_in, 16)
            sp.wait_ge(cwx_split, 1)
            for s in range(SPL):
                for q in range(SPL):
                    a = (s * SPL + q) * UC
                    sp.dma_start(CWx[a:a + UC, :], CSP[:, s, :]).then_inc(wx_in, 16)

            def load(g, t):
                for s in (dve_summed, act_summed, pool_read):
                    wait(sp, s, g.at(TILES, t - SLOTS + 1))
                slot = g.slot(t)
                sp.dma_start(xt[:, slot, :], xv[g.num(), t // HALF, t % HALF]).then_inc(x_in[slot], 16)

            def store(g, c):
                query, col, n = CHUNKS[c]
                st = stage[:, (g.par + c) % 2, :, :]
                done = out_stored[(g.par + c) % 2]
                if query:
                    sp.wait_ge(evac_dve, g.at(4, 2 * c + 2))
                else:
                    sp.wait_ge(evac_act, g.at(9, 2 * (c - 2) + 2 if c < NCH - 1 else 9))
                og = out.rearrange("(g b) t d -> g b t d", b=GB)[g.num()]
                for t in range((n + 127) // 128):
                    if query:
                        b0 = (col + 128 * t) // NQ
                        dst = og[b0:b0 + 2, 0:NQ, :]
                    elif c < NCH - 1:
                        dst = og[4 * t:4 * t + 4, NQ + col // GB:NQ + col // GB + 32, :]
                    else:
                        dst = og[:, TOK - 4:TOK, :]
                    sp.dma_start(dst, st[0:min(n, 128), t, :]).then_inc(done, 16)

            def load_after(g, t):
                if t + SLOTS < TILES:
                    load(g, t + SLOTS)
                elif g.k is not None or g.off < NG - 1:
                    load(g.plus(1), t + SLOTS - TILES)

            def ffn_dma(g, left):
                for step in range(STEPS):
                    c, e = divmod(step, EX)
                    for gt_, t in tiles_at(g, step, left):
                        load_after(gt_, t)
                    if e == 3 and c > 0:
                        store(g, c - 1)
                store(g, NCH - 1)

            for t in range(TILES):
                load_after(G(None, 0), t)
            for step in range(A_FIRST, STEPS):
                for gt_, t in tiles_at(G(None, -1), step):
                    load_after(gt_, t)
            ffn_dma(G(None, 0), 2)
            with sp.Fori(0, 2) as k:
                for off in (1, 2):
                    ffn_dma(G(k, off), 2)
            ffn_dma(G(None, 5), 2)
            ffn_dma(G(None, 6), 1)
            ffn_dma(G(None, 7), 0)
            for s in range(2):
                sp.wait_ge(out_stored[s], 25 * 16 * NG // 2)

        @block.gpsimd
        def _(pool):
            links = [0]

            def link(ins):
                links[0] += 1
                ins.then_inc(pool_link, 1)
                pool.wait_ge(pool_link, links[0])

            nc.gpsimd.memset(CW14[:, :], 1.0).then_inc(const_done, 1)
            link(nc.gpsimd.memset(ident[:, :], 0.0))
            link(nc.gpsimd.affine_select(out=ident[:, :], in_=ident[:, :], compare_op=ALU.not_equal, fill=1.0,
                                         base=0, pattern=[[-1, 128]], channel_multiplier=1))
            nc.gpsimd.tensor_copy(identb[:, :], ident[:, :]).then_inc(const_done, 1)
            nc.gpsimd.memset(mhalf[:, :], -0.5)
            for k in range(CG):
                link(nc.gpsimd.memset(rep[:, k, :], 0.0))
                link(nc.gpsimd.affine_select(out=rep[:, k, :].rearrange("p (b c s) -> p b c s", b=GB, c=4),
                                             in_=rep[:, k, :].rearrange("p (b c s) -> p b c s", b=GB, c=4),
                                             compare_op=ALU.not_equal, fill=1.0, base=-4 * k,
                                             pattern=[[0, GB], [-1, 4], [0, 2]], channel_multiplier=1))
            link(nc.gpsimd.memset(bmask, 0.0))
            for c in range(4):
                link(nc.gpsimd.affine_select(out=bmask.rearrange("p (s b) -> p s b", s=2),
                                             in_=bmask.rearrange("p (s b) -> p s b", s=2),
                                             compare_op=ALU.not_equal, fill=1.0, base=-2 * c,
                                             pattern=[[-1, 2], [-8, GB]], channel_multiplier=1))
            link(nc.gpsimd.memset(rmask, 1.0))
            link(nc.gpsimd.affine_select(out=rmask, in_=rmask, compare_op=ALU.is_ge, fill=0.0, base=0,
                                         pattern=[[-CH, 8]], channel_multiplier=1))
            link(nc.gpsimd.affine_select(out=rmask, in_=rmask, compare_op=ALU.is_ge, fill=0.0, base=CH - 1,
                                         pattern=[[CH, 8]], channel_multiplier=-1))
            link(nc.gpsimd.memset(sel[:, :, :], 0.0))
            for s in range(SPL):
                link(nc.gpsimd.affine_select(out=sel[:, :, :], in_=sel[:, :, :], compare_op=ALU.not_equal, fill=1.0,
                                             base=-NE * s, pattern=[[-1, NE], [0, 128]], channel_multiplier=1))
            for i in range(NE):
                nc.gpsimd.memset(order8[:, i:i + 1], float(NE - i))
            nc.gpsimd.memset(Wx[:, :], 0.0)
            link(nc.gpsimd.memset(keymask[:, :], 1.0))
            link(nc.gpsimd.memset(keymask[0:NQ, 0:GB], 0.0))
            nc.gpsimd.memset(PH[:, :, :], 0.0).then_inc(const_done, 1)

            def pool_tile(g, t, a, b):
                n = (b - a) * PATCH
                src = xt[:, g.slot(t), :].rearrange("p (h w) -> p h w", h=PATCH)[:, :, a * PATCH:b * PATCH]
                kh = kh_sum[:, :, 0:n]

                def add(step, out, in0, in1):
                    nc.gpsimd.tensor_tensor(out=out, in0=in0, in1=in1, op=ALU.add).then_inc(tree_step, 1)
                    pool.wait_ge(tree_step, g.at(2 * TILES, 2 * t + step))

                pool.wait_ge(x_in[g.slot(t)], g.landed(t))
                wait(pool, pool_summed, g.at(TILES, t))
                nc.gpsimd.tensor_tensor(out=kh, in0=src[:, 0:8, :], in1=src[:, 8:16, :],
                                        op=ALU.add).then_inc(pool_read, 1)
                pool.wait_ge(pool_read, g.at(TILES, t + 1))
                add(1, kh[:, 0:4, :], kh[:, 0:4, :], kh[:, 4:8, :])
                add(2, kh[:, 0:2, :], kh[:, 0:2, :], kh[:, 2:4, :])
                wait(pool, rows_used, g.at(TILES, t - ROWS + 1))
                nc.gpsimd.tensor_tensor(out=row_sum[:, t % ROWS, 0:n], in0=kh[:, 0, :], in1=kh[:, 1, :],
                                        op=ALU.add).then_inc(pool_summed, 1)

            def item(g, kind, i):
                if kind == "stats":
                    pool.wait_ge(var_ready, g.at(3, 1))
                    nc.gpsimd.tensor_tensor(out=stat[:, 1, :], in0=stat[:, 0, :], in1=mhalf[0:HT, :],
                                            op=ALU.pow).then_inc(rstd_ready, 1)
                elif kind == "stats2":
                    pool.wait_ge(var_ready, g.at(3, 2))
                    nc.gpsimd.tensor_tensor(out=stat[:, 4, :], in0=stat[:, 3, :], in1=mhalf[0:HT, :],
                                            op=ALU.pow).then_inc(rstd_ready, 1)
                elif kind in ("Uw", "Xw") and i == 2:
                    pool.wait_ge(u_split if kind == "Uw" else x_split, g.at(1, 1))
                    pool.sem_inc(pool_passed, 1)
                    done = u_rep if kind == "Uw" else x_rep
                    for r in (1, 2):
                        nc.gpsimd.tensor_copy(SPT[:, :, r, :, :].rearrange("p u s c -> p u (s c)"),
                                              SPT[:, :, 0, :, :].rearrange("p u s c -> p u (s c)")).then_inc(done, 1)
                elif kind == "x2" and i == 0:
                    pool.wait_ge(var_ready, g.at(3, 3))
                    nc.gpsimd.tensor_tensor(out=rq[:, 1, :], in0=rq[:, 0, :], in1=mhalf[:, 0:8],
                                            op=ALU.pow).then_inc(rstd_ready, 1)

            def step_pool(g, step, left):
                for gt_, t in tiles_at(g, step, left):
                    pool_tile(gt_, t, *SHARE["pool"])
                if left:
                    for kind, i in items_at(step):
                        item(g.plus(1), kind, i)

            def ffn_pool(g, left):
                for step in range(STEPS):
                    step_pool(g, step, left)

            for t in range(TILES):
                pool_tile(G(None, 0), t, *SHARE0["pool"])
            pool.wait_ge(ready, 1)
            for step in range(A_FIRST, STEPS):
                step_pool(G(None, -1), step, 2)
            ffn_pool(G(None, 0), 2)
            with pool.Fori(0, 2) as k:
                for off in (1, 2):
                    ffn_pool(G(k, off), 2)
            ffn_pool(G(None, 5), 2)
            ffn_pool(G(None, 6), 1)

        @block.scalar
        def _(act):
            def prep(r):
                act.wait_ge(prep_full, r + 1)
                kind, i = PREP[r]
                if kind == "Wc":
                    n = wc(i)[1]
                    if i >= 2:
                        act.wait_ge(w_split, i - 1)
                    nc.scalar.copy(wres[:, 512:512 + n], aux[r % 2][0:CH, 0:n]).then_inc(prep_act, 1)
                else:
                    for o, src in prep_copies(r):
                        nc.scalar.copy(o, src).then_inc(prep_act, 1)

            def act_tile(g, t, a, b):
                act.wait_ge(x_in[g.slot(t)], g.landed(t))
                if t == 0:
                    wait(act, aux_full, g.at(NR, R[("V", 0)] + 1 - NR))
                src = xt[:, g.slot(t), :].rearrange("p (h j w) -> p h j w", h=PATCH, j=NP)
                for j in range(a, b):
                    at = (t % HALF) * NP + j
                    last = nc.scalar.activation(src[:, :, j, :], src[:, :, j, :], ACT.Copy,
                                                accum_out=pooled[:, t // HALF, at:at + 1])
                last.then_inc(act_summed, 1)

            todo = [r for r in range(len(PREP)) if not P_DVE[r]]
            for r in todo:
                prep(r)
            act.wait_ge(w_split, 5)
            act.wait_ge(const_done, 3)
            for s in range(SPL):
                for q in range(SPL):
                    a = (s * SPL + q) * UC
                    act.dma_start(Wx[a:a + XC, :], WSP[:, s, :]).then_inc(wx_in, 16)

            def item(g, kind, i):
                if kind not in PE_KINDS or kind in DVE_KINDS and kind != "XT":
                    return
                r = R[(kind, i)]
                ps = aux[g.bank(r)]
                act.wait_ge(aux_full, g.at(NR, r + 1))
                if kind == "V":
                    nc.scalar.copy(V[:, :, :].rearrange("p u c -> p (u c)"), ps[0:HT, 0:UNITS * (CH + 1)])\
                      .then_inc(aux_act, 1)
                elif kind == "PHT":
                    nc.scalar.copy(PHT[:, i, :, :].rearrange("p b t -> p (b t)"), ps[:, 0:4 * HT]).then_inc(aux_act, 1)
                elif kind == "VHT":
                    nc.scalar.copy(VHT[:, :, :].rearrange("p b q -> p (b q)"), ps[:, :]).then_inc(aux_act, 1)
                elif kind == "U":
                    src = ps[0:126, 0:2 * TOK].rearrange("p (b t) -> p b t", b=2)
                    nc.scalar.copy(UTq[:, :].rearrange("p (b t) -> p b t", b=GB)[:, 2 * i:2 * i + 2, :], src[:, :, 0:NQ])
                    keys_out(UTk[g.par], src[:, :, NQ:TOK], i).then_inc(aux_act, 1)
                elif kind == "X":
                    src = ps[0:126, 0:2 * NK].rearrange("p (b t) -> p b t", b=2)
                    keys_out(X2T[g.par], src, i).then_inc(aux_act, 1)
                elif kind == "S":
                    b0, nb = S_IMGS[i]
                    act.wait_ge(max_ready, g.at(6, i + 1))
                    for b in range(b0, b0 + nb):
                        last = nc.scalar.activation(E[:, b % 8, NQ:TOK], ps[0:NQ, (b - b0) * NK:(b - b0 + 1) * NK], ACT.Exp,
                                                    bias=sums[:, 0, b:b + 1], accum_out=sums[:, 1, b:b + 1])
                    last.then_inc(aux_act, 1)
                elif kind == "M":
                    half, part = divmod(i, 2)
                    n = 2 * D if part == 0 else D
                    nc.scalar.copy(Msb[:, half, 2 * D * part:2 * D * part + n], ps[0:8 * CH, 0:n]).then_inc(aux_act, 1)
                elif kind == "XT":
                    q, part = divmod(i, 2)
                    nc.scalar.copy((x0h if part == 0 else x1h)[:, 512 * q:512 * q + 512], ps[:, :]).then_inc(high_ready, 1)
                elif kind == "G":
                    nc.scalar.activation(gt[:, 0, :], ps[:, 0:GT * NE], ACT.Exp, scale=-1.0).then_inc(aux_act, 1)
                elif kind == "C":
                    n = 512 if i < 6 else 64
                    nc.scalar.copy(cwT[:, 512 * i:512 * i + n], ps[0:SPL * NE, 0:n]).then_inc(aux_act, 1)

            def keys_out(dst, src, i):
                nc.scalar.copy(dst[:, 0:2048].rearrange("p (c b k) -> p b c k", c=4, b=GB)[:, 2 * i:2 * i + 2, :, :],
                               src[:, :, 0:128].rearrange("p b (c k) -> p b c k", c=4))
                return nc.scalar.copy(dst[:, 2048:2112].rearrange("p (b k) -> p b k", b=GB)[:, 2 * i:2 * i + 2, :],
                                      src[:, :, 128:NK])

            def evacuate(g, c):
                n = CHUNKS[c][2]
                act.wait_ge(l2_step, g.at(STEPS, (c + 1) * EX))
                wait(act, out_stored[(g.par + c) % 2], g.before(c))
                st = stage[:, (g.par + c) % 2, :, :].rearrange("p t d -> p (t d)")
                if c < NCH - 1:
                    for b in range(2):
                        nc.scalar.copy(st[:, 2 * D * b:2 * D * b + 2 * D], out_ps[b][:, 0:2 * D]).then_inc(evac_act, 1)
                else:
                    nc.scalar.copy(st[0:n, 0:D], out_ps[0][0:n, 0:D]).then_inc(evac_act, 1)

            def step_act(g, step, left):
                for gt_, t in tiles_at(g, step, left):
                    act_tile(gt_, t, *SHARE["act"])
                if left:
                    for kind, i in items_at(step):
                        item(g.plus(1), kind, i)

            def ffn_act(g, left):
                for step in range(STEPS):
                    c, e = divmod(step, EX)
                    n = CHUNKS[c][2]
                    if e == 2 and c > 2:
                        evacuate(g, c - 1)
                    act.wait_ge(h1_ready, g.at(STEPS, step + 1))
                    wait(act, gated_done, g.at(STEPS, step - 1))
                    p = (g.par + step) % 2
                    nc.scalar.activation(silu[p][:, 0:n], h1_ps[p][:, 0:n], ACT.Silu).then_inc(silu_done, 1)
                    step_act(g, step, left)
                evacuate(g, NCH - 1)

            for t in range(TILES):
                act_tile(G(None, 0), t, *SHARE0["act"])
            act.wait_ge(ready, 1)
            for step in range(A_FIRST, STEPS):
                step_act(G(None, -1), step, 2)
            ffn_act(G(None, 0), 2)
            with act.Fori(0, 2) as k:
                for off in (1, 2):
                    ffn_act(G(k, off), 2)
            ffn_act(G(None, 5), 2)
            ffn_act(G(None, 6), 1)
            ffn_act(G(None, 7), 0)

        @block.vector
        def _(dve):
            links = [0]
            v = nc.vector

            plinks = [0]

            def plink(ins):
                plinks[0] += 1
                ins.then_inc(prep_link, 1)
                dve.wait_ge(prep_link, plinks[0])

            dve.wait_ge(cw_in, 16)
            dve.wait_ge(const_done, 1)
            plink(v.tensor_reduce(out=sums[0:CH, 1, 0:1], in_=CWn, axis=AX.X, op=ALU.add))
            plink(v.tensor_scalar(G13[:, CH:CH + 1], sums[0:CH, 1, 0:1], 1.0 / D, None, ALU.mult))
            v.tensor_scalar(CW14[0:CH, :], CWn, G13[:, CH:CH + 1], None, ALU.subtract).then_inc(cwc_ready, 1)
            dve.wait_ge(cwc_ready, 1)
            dve.wait_ge(pb_in, 16)
            plink(v.tensor_copy(CSP[:, 0, :], CW14[:, :]))
            plink(v.tensor_tensor(out=cres, in0=CW14[:, :], in1=CSP[:, 0, :], op=ALU.subtract))
            plink(v.tensor_copy(CSP[:, 1, :], cres))
            v.tensor_tensor(out=CSP[:, 2, :], in0=cres, in1=CSP[:, 1, :], op=ALU.subtract).then_inc(cwx_split, 1)

            def split_w(i, src):
                a, n = wc(i)
                plink(v.tensor_copy(WSP[:, 0, a:a + n], src))
                plink(v.tensor_tensor(out=src, in0=src, in1=WSP[:, 0, a:a + n], op=ALU.subtract))
                plink(v.tensor_copy(WSP[:, 1, a:a + n], src))
                v.tensor_tensor(out=WSP[:, 2, a:a + n], in0=src, in1=WSP[:, 1, a:a + n],
                                op=ALU.subtract).then_inc(w_split, 1)

            def prep(r):
                dve.wait_ge(prep_full, r + 1)
                if PREP[r][0] == "Wc":
                    i = PREP[r][1]
                    a, n = wc(i)
                    plink(v.tensor_copy(wres[:, 0:n], aux[r % 2][0:CH, 0:n]))
                    v.sem_inc(prep_dve, 1)
                    split_w(i, wres[:, 0:n])
                    if i + 1 < 5:
                        dve.wait_ge(prep_act, P_ACT_N[r + 1])
                        split_w(i + 1, wres[:, 512:512 + wc(i + 1)[1]])
                elif PREP[r][0] in ("W0", "W1", "gate"):
                    n, high, low = split_dst(r)
                    ps = aux[r % 2]
                    plink(v.tensor_copy(high, ps[:, 0:n]))
                    if low is None:
                        high, low, ps = high[64:128], high[64:128], ps[64:128]
                    v.tensor_tensor(out=low, in0=ps[:, 0:n], in1=high.bitcast(F32), op=ALU.subtract).then_inc(prep_dve, 1)
                else:
                    for o, i in prep_copies(r):
                        v.tensor_copy(o, i).then_inc(prep_dve, 1)
                if PREP[r][0] == "repG":
                    dve.wait_ge(prep_dve, P_DVE_N[r])
                    dve.wait_ge(const_done, 3)
                    for k in range(CG):
                        plink(v.tensor_tensor(
                            out=blockG[:, k, :].rearrange("p (u c) -> p u c", u=UNITS),
                            in0=bmask.unsqueeze(2).to_broadcast([128, UNITS, CH + 1]),
                            in1=repG[:, k, :].unsqueeze(1).to_broadcast([128, UNITS, CH + 1]), op=ALU.mult))

            for r in range(len(PREP)):
                if P_DVE[r]:
                    prep(r)
            dve.wait_ge(cwr_in, 16 * 8)
            for b in range(8):
                plink(v.tensor_scalar(CWr[:, :, b // 2, 64 * (b % 2):64 * (b % 2) + 64],
                                      CWr_src.rearrange("p (i r) -> p r i", r=3), rmask[:, b:b + 1], None, ALU.mult))
            dve.wait_ge(prep_full, len(PREP))
            dve.wait_ge(wx_in, 18 * 16)
            plink(v.memset(VHpad, 0.0))
            plink(v.memset(E, 0.0))
            plink(v.memset(SPT[:, :, :, :, :].rearrange("p a b c d -> p (a b c d)"), 0.0))
            plink(v.memset(SPT[0:NQ, 0:GB, 0, 0, CH + 1:UC], 1.0))
            for i in range(2):
                plink(v.memset(X2T[i][:, 2112:KPAD], 0.0))
            dve.wait_ge(gb_in, 16)
            v.sem_inc(ready, 1)

            def link(g, ins):
                links[0] += 1
                ins.then_inc(dve_link, 1)
                dve.wait_ge(dve_link, g.at(LINKS, links[0]))

            def dve_tile(g, t, lo, hi):
                dve.wait_ge(x_in[g.slot(t)], g.landed(t))
                if t == 0:
                    wait(dve, aux_full, g.at(NR, R[("V", 0)] + 1 - NR))
                src = xt[:, g.slot(t), :].rearrange("p (h j w) -> p j h w", h=PATCH, j=NP)
                at = (t % HALF) * NP
                v.tensor_reduce(out=pooled[:, t // HALF, at + lo:at + hi], in_=src[:, lo:hi, :, :],
                                axis=AX.XY, op=ALU.add).then_inc(dve_summed, 1)

            def finish_rows(g, t, lo, hi):
                dve.wait_ge(pool_summed, g.at(TILES, t + 1))
                at = (t % HALF) * NP
                v.tensor_reduce(out=pooled[:, t // HALF, at + lo:at + hi],
                                in_=row_sum[:, t % ROWS, 0:(hi - lo) * PATCH].rearrange("p (j w) -> p j w", w=PATCH),
                                axis=AX.X, op=ALU.add).then_inc(rows_used, 1)

            def dve_sums(g, t, share):
                dve_tile(g, t, *share["dve"])
                if t > 0:
                    finish_rows(g, t - 1, *share["pool"])

            def mark_max(g, vals, n, best, tmp):
                shape = [128, GT, n]
                link(g, v.tensor_reduce(out=best, in_=vals, axis=AX.X, op=ALU.max))
                link(g, v.tensor_tensor(out=tmp, in0=vals, in1=best.unsqueeze(2).to_broadcast(shape), op=ALU.is_equal))
                link(g, v.tensor_tensor(out=tmp, in0=tmp, in1=order8[:, NE - n:NE].unsqueeze(1).to_broadcast(shape),
                                        op=ALU.mult))

            def pick_first(g, n, out_mask, best, tmp):
                link(g, v.tensor_reduce(out=best, in_=tmp, axis=AX.X, op=ALU.max))
                link(g, v.tensor_tensor(out=out_mask, in0=tmp, in1=best.unsqueeze(2).to_broadcast([128, GT, n]),
                                        op=ALU.is_equal))

            def split3(g, part, src, n, done):
                if part == 1:
                    link(g, v.tensor_copy(SPT[:, :, 0, 0, 0:n], src))
                    link(g, v.tensor_tensor(out=res[:, :, 0:n], in0=src, in1=SPT[:, :, 0, 0, 0:n], op=ALU.subtract))
                else:
                    link(g, v.tensor_copy(SPT[:, :, 0, 1, 0:n], res[:, :, 0:n]))
                    v.tensor_tensor(out=SPT[:, :, 0, 2, 0:n], in0=res[:, :, 0:n], in1=SPT[:, :, 0, 1, 0:n],
                                    op=ALU.subtract).then_inc(done, 1)

            def item(g, kind, i, first=False):
                if kind in DVE_KINDS:
                    r = R[(kind, i)]
                    ps = aux[g.bank(r)]
                    dve.wait_ge(aux_full, g.at(NR, r + 1))
                if kind == "fin":
                    finish_rows(g, TILES - 1, *(SHARE0 if first else SHARE)["pool"])
                elif kind == "tok":
                    for k in range(CG):
                        ins = v.tensor_copy(
                            Ptok[:, :, 4 * k:4 * k + 4].rearrange("p (s b) c -> p s b c", s=2),
                            ps[0:HT, 128 * k:128 * k + 128].rearrange("p (b c s) -> p s b c", b=GB, c=4))
                    ins.then_inc(aux_dve, 1)
                elif kind == "stats":
                    links[0] = 0
                    dve.wait_ge(aux_dve, g.at(BYDVE[-1], BYDVE[R[("tok", 0)]]))
                    dve.wait_ge(aux_act, g.at(BYACT[-1], BYACT[R[("V", 0)]]))
                    link(g, v.tensor_tensor(out=val[:, :, 0:CH], in0=Ptok[:, :, :], in1=V[:, :, 0:CH], op=ALU.mult))
                    link(g, v.tensor_reduce(out=stat[:, 2, :], in_=val[:, :, 0:CH], axis=AX.X, op=ALU.add))
                    link(g, v.tensor_scalar(stat[:, 2, :], stat[:, 2, :], 1.0 / D, 0.0, ALU.mult, ALU.max))
                    v.tensor_scalar(stat[:, 0, :], stat[:, 2, :], EPS, None, ALU.add).then_inc(var_ready, 1)
                elif kind == "stats2":
                    dve.wait_ge(rstd_ready, g.at(3, 1))
                    link(g, v.tensor_tensor(out=stat[:, 5, :], in0=stat[:, 1, :], in1=keymask[:, :], op=ALU.mult))
                    link(g, v.tensor_scalar(stat[:, 5, :], stat[:, 5, :], 1.0, None, ALU.add))
                    link(g, v.tensor_tensor(out=stat[:, 6, :], in0=stat[:, 5, :], in1=stat[:, 5, :], op=ALU.mult))
                    link(g, v.tensor_tensor(out=stat[:, 6, :], in0=stat[:, 6, :], in1=stat[:, 2, :], op=ALU.mult))
                    v.tensor_scalar(stat[:, 3, :], stat[:, 6, :], EPS, None, ALU.add).then_inc(var_ready, 1)
                    wait(dve, aux_full, g.at(NR, R[("AH", 1)] + 1 - NR))
                    v.tensor_tensor(out=PH[:, :, 0:CH], in0=Ptok[:, :, :],
                                    in1=stat[:, 1, :].unsqueeze(2).to_broadcast([HT, UNITS, CH]),
                                    op=ALU.mult).then_inc(ph_ready, 1)
                elif kind == "VHw":
                    if i == 1:
                        dve.wait_ge(aux_full, g.at(NR, R[("VHT", 0)] + 1))
                    for q in range(2):
                        src = V[0:NQ, 8 * i + 4 * q:8 * i + 4 * q + 4, 0:CH]
                        dst = attw[0:NQ, 512 * q:512 * q + 640].rearrange("p (m n) -> p m n", m=4)[:, :, 0:CH]
                        ins = v.scalar_tensor_tensor(out=dst, in0=src, scalar=float(D // 12) ** -0.5,
                                                     in1=stat[0:NQ, 1, 8 * i + 4 * q:8 * i + 4 * q + 4].unsqueeze(2)
                                                     .to_broadcast([NQ, 4, CH]), op0=ALU.mult, op1=ALU.mult)
                    ins.then_inc(vh_ready, 1)
                elif kind == "Uw" and i == 0:
                    wait(dve, aux_full, g.at(NR, R[("X", 7)] + 1 - NR))
                    link(g, v.tensor_tensor(out=val[:, :, 0:CH], in0=Ptok[:, :, :],
                                            in1=stat[:, 5, :].unsqueeze(2).to_broadcast([HT, UNITS, CH]), op=ALU.mult))
                    link(g, v.tensor_copy(val[:, :, CH:CH + 1], V[:, :, CH:CH + 1]))
                elif kind == "Uw":
                    split3(g, i, val[:, :, :], CH + 1, u_split)
                elif kind == "Xw" and i == 0:
                    dve.wait_ge(rstd_ready, g.at(3, 2))
                    dve.wait_ge(u_split, g.at(1, 1))
                    link(g, v.tensor_tensor(out=stat[:, 7, :], in0=stat[:, 4, :], in1=stat[:, 5, :], op=ALU.mult))
                    link(g, v.tensor_tensor(out=val[:, :, 0:CH], in0=Ptok[:, :, :],
                                            in1=stat[:, 7, :].unsqueeze(2).to_broadcast([HT, UNITS, CH]), op=ALU.mult))
                elif kind == "Xw":
                    if i == 1:
                        dve.wait_ge(aux_full, g.at(NR, R[("U", 7)] + 1))
                    split3(g, i, val[:, :, 0:CH], CH, x_split)
                elif kind == "S_max":
                    b0, nb = S_IMGS[i]
                    r = R[("S", i)]
                    dve.wait_ge(aux_full, g.at(NR, r + 1))
                    v.tensor_reduce(out=sums[:, 0, b0:b0 + nb],
                                    in_=aux[g.bank(r)][0:NQ, 0:nb * NK].rearrange("p (b k) -> p b k", b=nb),
                                    axis=AX.X, op=ALU.max, negate=True).then_inc(max_ready, 1)
                elif kind == "ET":
                    v.tensor_copy(ET[:, 8 * (i % 2):8 * (i % 2) + 8, :].rearrange("p u q -> p (u q)"), ps[0:HT, :])\
                     .then_inc(aux_dve, 1)
                elif kind == "AH":
                    link(g, v.reciprocal(sums[:, 2, 8 * i:8 * i + 8], sums[:, 1, 8 * i:8 * i + 8]))
                    v.tensor_tensor(out=Asb[:, i, :].rearrange("p (b c) -> p b c", b=8),
                                    in0=ps[0:NQ, 0:8 * CH].rearrange("p (b c) -> p b c", b=8),
                                    in1=sums[:, 2, 8 * i:8 * i + 8].unsqueeze(2).to_broadcast([NQ, 8, CH]),
                                    op=ALU.mult).then_inc(aux_dve, 1)
                elif kind == "H":
                    v.bn_stats(bst[:, i, 0:6], ps[:, 0:D])
                    v.tensor_copy(h2q[:, i, :], ps[:, 0:D]).then_inc(aux_dve, 1)
                elif kind == "x2" and i == 0:
                    dve.wait_ge(aux_dve, g.at(BYDVE[-1], BYDVE[R[("H", 7)]]))
                    dve.sem_inc(dve_passed, 1)
                    for t in range(8):
                        ins = v.bn_aggr(bst[:, t, 6:8], bst[:, t, 0:6])
                    link(g, ins)
                    v.tensor_scalar(rq[:, 0, :], bst[:, :, 7], EPS, None, ALU.add).then_inc(var_ready, 1)
                elif kind == "x2":
                    if i == 1:
                        dve.wait_ge(rstd_ready, g.at(3, 3))
                    if i == 3:
                        dve.wait_ge(aux_full, g.at(NR, R[("XT", 1)] + 1))
                    for t in range(2 * i - 2, 2 * i):
                        v.tensor_scalar(x2q[:, t % 4, :], h2q[:, t, :], bst[:, t, 6:7], rq[:, 1, t:t + 1],
                                        ALU.subtract, ALU.mult).then_inc(x2_ready, 1)
                elif kind == "XT":
                    q, part = divmod(i, 2)
                    high, low = (x0h, x0l) if part == 0 else (x1h, x1l)
                    dve.wait_ge(high_ready, g.at(4, i + 1))
                    v.tensor_tensor(out=low[:, 512 * q:512 * q + 512], in0=ps[:, :],
                                    in1=high[:, 512 * q:512 * q + 512].bitcast(F32), op=ALU.subtract).then_inc(aux_dve, 1)
                elif kind == "gate":
                    gates(g, i)

            def gates(g, part):
                t3 = "p (t e) -> p t e"
                a, b, c, d = [gt[:, j, :].rearrange(t3, t=GT) for j in range(4)]
                ga, gb_, gc = [gs[:, j, :].rearrange(t3, t=GT) for j in range(3)]
                best = gs[:, 3, 0:GT]
                m4 = gs[:, 1, :].rearrange("p (t m) -> p t m", t=GT).unsqueeze(3).to_broadcast([128, GT, 4, 2])
                b4 = gt[:, 1, :].rearrange("p (t m e) -> p t m e", t=GT, m=4)
                if part == 0:
                    dve.wait_ge(aux_act, g.at(BYACT[-1], BYACT[R[("G", 0)]]))
                    link(g, v.tensor_scalar(a, a, 1.0, None, ALU.add))
                    link(g, v.reciprocal(a, a))
                    link(g, v.tensor_tensor(out=b, in0=a, in1=gbias[:, :].unsqueeze(1).to_broadcast([128, GT, NE]),
                                            op=ALU.add))
                elif part == 1:
                    link(g, v.tensor_reduce(out=ga, in_=b4, axis=AX.X, op=ALU.add))
                    mark_max(g, ga, 4, best, gc)
                elif part == 2:
                    pick_first(g, 4, gb_, best, gc)
                    link(g, v.scalar_tensor_tensor(out=ga, in0=gb_, scalar=-1e30, in1=ga, op0=ALU.mult, op1=ALU.add))
                elif part == 3:
                    mark_max(g, ga, 4, best, ga)
                elif part == 4:
                    pick_first(g, 4, gc, best, ga)
                    link(g, v.tensor_tensor(out=gb_, in0=gb_, in1=gc, op=ALU.add))
                elif part == 5:
                    link(g, v.tensor_tensor(out=b4, in0=b4, in1=m4, op=ALU.mult))
                    link(g, v.tensor_scalar(gb_, gb_, -1.0, 1e30, ALU.add, ALU.mult))
                    link(g, v.tensor_tensor(out=b4, in0=b4, in1=m4, op=ALU.add))
                elif part == 6:
                    mark_max(g, b, NE, best, c)
                elif part == 7:
                    pick_first(g, NE, d, best, c)
                    link(g, v.scalar_tensor_tensor(out=b, in0=d, scalar=-2e30, in1=b, op0=ALU.mult, op1=ALU.add))
                elif part == 8:
                    mark_max(g, b, NE, best, c)
                elif part == 9:
                    pick_first(g, NE, b, best, c)
                    link(g, v.tensor_tensor(out=d, in0=d, in1=b, op=ALU.add))
                elif part == 10:
                    link(g, v.tensor_tensor(out=a, in0=a, in1=d, op=ALU.mult))
                    link(g, v.tensor_reduce(out=best, in_=a, axis=AX.X, op=ALU.add))
                    link(g, v.tensor_scalar(best, best, 1e-6, None, ALU.add))
                elif part == 11:
                    link(g, v.reciprocal(best, best))
                    link(g, v.tensor_tensor(out=a, in0=a, in1=best.unsqueeze(2).to_broadcast([128, GT, NE]), op=ALU.mult))
                    wait(dve, aux_full, g.at(NR, 0))
                    link(g, v.tensor_copy(CS[:, :, 0, :], a))
                elif part == 12:
                    link(g, v.tensor_tensor(out=b, in0=a, in1=CS[:, :, 0, :], op=ALU.subtract))
                    link(g, v.tensor_copy(CS[:, :, 1, :], b))
                    v.tensor_tensor(out=CS[:, :, 2, :], in0=b, in1=CS[:, :, 1, :], op=ALU.subtract).then_inc(cs_ready, 1)
                    assert links[0] == LINKS, links[0]

            def step_dve(g, step, left, first=False):
                for gt_, t in tiles_at(g, step, left):
                    dve_sums(gt_, t, SHARE)
                if left:
                    for kind, i in items_at(step):
                        item(g.plus(1), "S_max" if kind == "S" else kind, i, first)

            def evacuate(g, c):
                dve.wait_ge(l2_step, g.at(STEPS, (c + 1) * EX))
                wait(dve, out_stored[(g.par + c) % 2], g.before(c))
                for b in range(2):
                    v.tensor_tensor(out=stage[:, (g.par + c) % 2, 2 * b:2 * b + 2, :],
                                    in0=out_ps[b][:, 0:2 * D].rearrange("p (t d) -> p t d", t=2),
                                    in1=h2q[:, 4 * c + 2 * b:4 * c + 2 * b + 2, :], op=ALU.add).then_inc(evac_dve, 1)

            def ffn_dve(g, left):
                for step in range(STEPS):
                    c, e = divmod(step, EX)
                    n = CHUNKS[c][2]
                    if e == 2 and c in (1, 2):
                        evacuate(g, c - 1)
                    p = (g.par + step) % 2
                    dve.wait_ge(silu_done, g.at(STEPS, step + 1))
                    dve.wait_ge(h3_ready, g.at(STEPS, step + 1))
                    if e == NE:
                        wait(dve, l2_step, g.at(STEPS, step - HR + 1))
                        v.tensor_tensor(out=h[step % HR][:, 0:n], in0=h3_ps[:, 0:n], in1=silu[p][:, 0:n],
                                        op=ALU.mult).then_inc(gated_done, 1)
                    else:
                        v.tensor_tensor(out=gated[p][:, 0:n], in0=h3_ps[:, 0:n], in1=silu[p][:, 0:n],
                                        op=ALU.mult).then_inc(gated_done, 1)
                    if e < NE:
                        dve.wait_ge(gated_done, g.at(STEPS, step + 1))
                        dve.wait_ge(cw_ready, g.at(NCH * NE, c * NE + e + 1))
                        wait(dve, l2_step, g.at(STEPS, step - HR + 1))
                        v.tensor_tensor(out=h[step % HR][:, 0:n], in0=cw_ps[:, 0:n], in1=gated[p][:, 0:n],
                                        op=ALU.mult).then_inc(h_done, 1)
                    step_dve(g, step, left)

            for t in range(TILES):
                dve_sums(G(None, 0), t, SHARE0)
            for step in range(A_FIRST, STEPS):
                step_dve(G(None, -1), step, 2, first=True)
            ffn_dve(G(None, 0), 2)
            with dve.Fori(0, 2) as k:
                for off in (1, 2):
                    ffn_dve(G(k, off), 2)
            ffn_dve(G(None, 5), 2)
            ffn_dve(G(None, 6), 1)
            ffn_dve(G(None, 7), 0)

        @block.tensor
        def _(pe):
            mm = nc.tensor.matmul
            pe.wait_ge(const_done, 2)
            for r, (kind, i) in enumerate(PREP):
                ps = aux[r % 2]
                if r >= 2:
                    pe.wait_ge(prep_dve if P_DVE[r - 2] else prep_act, P_DVE_N[r - 2] if P_DVE[r - 2] else P_ACT_N[r - 2])
                if kind == "CWcT":
                    pe.wait_ge(cwc_ready, 1)
                    n = 128 if i == 0 else 64
                    last = nc.tensor.transpose(ps[0:n, 0:CH], CW14[0:CH, 128 * i:128 * i + n], ident[0:CH, 0:CH])
                    if i == 1:
                        last = mm(ps[64:128, 0:CH], CW14[0:CH, 128:D], ident[0:CH, 0:CH], start=True, stop=True)
                elif kind == "G":
                    pe.wait_ge(prep_dve, 1)
                    pe.wait_ge(prep_act, 1)
                    mm(ps[0:CH, 0:CH], CWcT[0], CWcT[0], start=True, stop=False)
                    last = mm(ps[0:CH, 0:CH], CWcT[1][0:64], CWcT[1][0:64], start=False, stop=True)
                elif kind == "repG":
                    pe.wait_ge(prep_dve, P_DVE_N[P_AT[("G", 0)]])
                    pe.wait_ge(const_done, 3)
                    for k in range(CG):
                        last = mm(ps[:, k * (CH + 1):(k + 1) * (CH + 1)], rep[:, k, :], G13, start=True, stop=True)
                elif kind == "gate":
                    pe.wait_ge(w_in, 11 * 16)
                    n = 128 if i == 0 else 64
                    last = nc.tensor.transpose(ps[0:n, 0:NE], g_nat[:, 128 * i:128 * i + n], ident[0:NE, 0:NE])
                    if i == 1:
                        last = mm(ps[64:128, 0:NE], g_nat[:, 128:D], ident[0:NE, 0:NE], start=True, stop=True)
                elif kind == "W0":
                    a, k = w4(i)
                    for j in range(k):
                        last = nc.tensor.transpose(ps[:, 128 * j:128 * j + 128], w13_nat[:, a + j, 0:128], ident[:, :])
                elif kind == "W1":
                    a, k = w4(i)
                    for j in range(k):
                        nc.tensor.transpose(ps[0:64, 128 * j:128 * j + 128], w13_nat[:, a + j, 128:D], ident[:, :])
                        last = mm(ps[64:128, 128 * j:128 * j + 128], w13_nat[:, a + j, 128:D], ident[:, :],
                                  start=True, stop=True)
                elif kind == "Wc":
                    pe.wait_ge(prep_dve, P_DVE_N[P_AT[("W1", 4)]])
                    a, n = wc(i)
                    m = min(n, WCOLS - a)
                    for lo, hi, parts in ((0, m, [w[:, a:a + m] for w in (WT0h, WT0l, WT1s)]),
                                          (m, n, [w[:, :] for w in (gT0h, gT0l, gT1s)])):
                        if lo < hi:
                            for q in range(3):
                                last = mm(ps[0:CH, lo:hi], CWcT[q // 2], parts[q].bitcast(F32), start=(q == 0), stop=(q == 2))
                elif kind == "w2":
                    for j in range(min(2, EX - 2 * i)):
                        nc.tensor.transpose(ps[:, D * j:D * j + 128], w2_natA[:, 2 * i + j, :], ident[:, :])
                        last = nc.tensor.transpose(ps[:, D * j + 128:D * j + D], w2_natB[:, 2 * i + j, :], ident[0:64, 0:64])
                elif kind == "proj":
                    for j in range(2 if i == 0 else 1):
                        q = 2 * i + j
                        nc.tensor.transpose(ps[0:NQ, D * j:D * j + 128], pw_natA[:, NQ * q:NQ * q + NQ], ident[:, :])
                        last = nc.tensor.transpose(ps[0:NQ, D * j + 128:D * j + D], pw_natB[:, NQ * q:NQ * q + NQ],
                                                   ident[0:64, 0:64])
                last.then_inc(prep_full, 1)
            pe.wait_ge(prep_dve, P_DVE_N[-1])
            pe.wait_ge(prep_act, P_ACT_N[-1])
            pe.wait_ge(ready, 1)

            def products(o, left, right):
                for q in range(len(left)):
                    ins = mm(o, left[q], right[q], start=(q == 0), stop=(q == len(left) - 1))
                return ins

            def item(g, kind, i):
                if kind not in PE_KINDS:
                    return
                r = R[(kind, i)]
                ps = aux[g.bank(r)]
                act_rounds = dve_rounds = None
                if r < 2:
                    act_rounds = BYACT[NR - 2 + r] - BYACT[-1]
                elif ROUNDS[r - 2][0] in DVE_KINDS:
                    dve_rounds = BYDVE[r - 2]
                else:
                    act_rounds = BYACT[r - 2]
                source = {"S": ("VHT", i // 3), "ET": ("S", 3 * (i // 2) + (1 if i % 2 == 0 else 2)),
                          "AH": ("ET", 2 * i + 1), "M": ("AH", i // 2), "H": ("M", 3 if i >= 4 else 1), "G": ("XT", 3)}
                if kind in source:
                    src = R[source[kind]]
                    if kind == "H":
                        src = max(src, R[("U", 7)])
                    if ROUNDS[src][0] in DVE_KINDS:
                        dve_rounds = max(dve_rounds or 0, BYDVE[src])
                    else:
                        act_rounds = max(act_rounds or 0, BYACT[src])
                if act_rounds is not None:
                    wait(pe, aux_act, g.at(BYACT[-1], act_rounds))
                if dve_rounds is not None:
                    wait(pe, aux_dve, g.at(BYDVE[-1], dve_rounds))
                if kind == "tok":
                    for s in (dve_summed, act_summed, rows_used):
                        pe.wait_ge(s, g.at(TILES, TILES))
                    for k in range(CG):
                        last = nc.tensor.transpose(ps[0:HT, 128 * k:128 * k + 128], pooled[:, k, :], ident[:, :])
                elif kind == "V":
                    for k in range(CG):
                        last = mm(ps[0:HT, 0:UNITS * (CH + 1)], pooled[:, k, :], blockG[:, k, :],
                                  start=(k == 0), stop=(k == CG - 1))
                elif kind == "PHT":
                    pe.wait_ge(ph_ready, g.at(1, 1))
                    for b in range(4):
                        u = GB * i + 4 * b
                        last = nc.tensor.transpose(ps[:, HT * b:HT * b + HT],
                                                   PH[:, u:u + 4, :].rearrange("p u c -> p (u c)"), ident[0:HT, 0:HT])
                elif kind == "VHT":
                    pe.wait_ge(vh_ready, g.at(2, i + 1))
                    pe.sem_inc(pe_passed, 1)
                    for b in range(8):
                        last = nc.tensor.transpose(ps[:, NQ * b:NQ * b + NQ], VHpad[:, b, :], ident[0:NQ, 0:NQ])
                elif kind == "S":
                    b0, nb = S_IMGS[i]
                    for b in range(b0, b0 + nb):
                        at = (b - b0) * NK
                        mm(ps[0:NQ, at:at + HT - NQ], VHT[:, b % 8, :], PHT[:, 0, b // 4, NQ:HT], start=True, stop=True)
                        last = mm(ps[0:NQ, at + HT - NQ:at + NK], VHT[:, b % 8, :], PHT[:, 1, b // 4, :],
                                  start=True, stop=True)
                elif kind == "ET":
                    pe.sem_inc(pe_passed, 1)
                    for j in range(8):
                        b, s = 4 * (i % 2) + j // 2, j % 2
                        last = nc.tensor.transpose(ps[0:HT, NQ * j:NQ * j + NQ], E[:, b, HT * s:HT * s + HT],
                                                   ident[0:NQ, 0:NQ])
                elif kind == "AH":
                    for b in range(8):
                        for s in range(2):
                            last = mm(ps[0:NQ, CH * b:CH * b + CH], ET[:, 2 * b + s, :], PH[:, GB * s + 8 * i + b, 0:CH],
                                      start=(s == 0), stop=(s == 1))
                elif kind == "M":
                    half, part = divmod(i, 2)
                    n = 2 if part == 0 else 1
                    last = mm(ps[0:8 * CH, 0:n * D], Asb[:, half, :],
                              projT[:, 2 * part:2 * part + n, :].rearrange("p r d -> p (r d)"), start=True, stop=True)
                elif kind == "U":
                    pe.wait_ge(u_rep, g.at(2, 2))
                    for j in range(2):
                        for s in range(2):
                            at = TOK * j + HT * s
                            last = mm(ps[0:126, at:at + HT],
                                      SPT[:, GB * s + 2 * i + j, :, :, :].rearrange("p a b c -> p (a b c)"),
                                      identb[0:HT, 0:HT], start=True, stop=True)
                elif kind == "X":
                    pe.wait_ge(x_rep, g.at(2, 2))
                    for j in range(2):
                        for s in range(2):
                            at = NK * j + (HT - NQ) * s
                            n = HT - NQ if s == 0 else HT
                            last = mm(ps[0:126, at:at + n],
                                      SPT[:, GB * s + 2 * i + j, :, :, :].rearrange("p a b c -> p (a b c)"),
                                      identb[0:HT, HT - n:HT], start=True, stop=True)
                elif kind == "H":
                    mm(ps[:, 0:D], UTq[:, 128 * i:128 * i + 128], CWx[:, :], start=True, stop=False)
                    for q in range(3):
                        last = mm(ps[:, 0:D], CWr[:, q, i % 4, :], Msb[:, i // 4, D * q:D * q + D],
                                  start=False, stop=(q == 2))
                elif kind == "XT":
                    q, part = divmod(i, 2)
                    pe.wait_ge(x2_ready, g.at(8, 4 * q + 4))
                    pe.sem_inc(pe_passed, 1)
                    for j in range(4):
                        at = slice(128 * j, 128 * j + 128)
                        if part == 0:
                            last = nc.tensor.transpose(ps[:, at], x2q[:, j, 0:128], ident[:, :])
                        else:
                            nc.tensor.transpose(ps[0:64, at], x2q[:, j, 128:D], ident[:, :])
                            last = mm(ps[64:128, at], x2q[:, j, 128:D], ident[:, :], start=True, stop=True)
                elif kind == "G":
                    for t in range(8):
                        o = ps[:, NE * t:NE * t + NE]
                        at = slice(128 * t, 128 * t + 128)
                        products(o, [x0h[:, at], x0h[:, at], x0l[:, at], x1h[:, at], x1l[:, at]],
                                 [gT0h[:, :], gT0l[:, :], gT0h[:, :], gT1s[:, :], gT1s[:, :]])
                    for t in range(17):
                        last = mm(ps[:, NE * (8 + t):NE * (9 + t)], X2T[g.par][0:126, 128 * t:128 * t + 128],
                                  Wx[:, WCOLS:WCOLS + NE], start=True, stop=True)
                elif kind == "C":
                    pe.wait_ge(cs_ready, g.at(1, 1))
                    for j in range(4 if i < 6 else 1):
                        n = 128 if i < 6 else 64
                        last = mm(ps[0:SPL * NE, 128 * j:128 * j + n], CS[:, 4 * i + j, :, :].rearrange("p s e -> p (s e)"),
                                  identb[:, 0:n], start=True, stop=True)
                last.then_inc(aux_full, 1)

            def layer2(g, step):
                c, e = divmod(step, EX)
                query, col, n = CHUNKS[c]
                if e == 0:
                    if c in (1, 2):
                        pe.wait_ge(evac_dve, g.at(4, 2 * c))
                    elif c == 0:
                        wait(pe, evac_act, g.at(9, 0))
                    else:
                        pe.wait_ge(evac_act, g.at(9, 2 * (c - 2)))
                pe.wait_ge(h_done, g.at(NCH * NE, c * NE + min(e + 1, NE)))
                if e == NE:
                    pe.wait_ge(gated_done, g.at(STEPS, step + 1))
                m = min(n, 128)
                for t in range((n + 127) // 128):
                    o = out_ps[t // 2][0:m, D * (t % 2):D * (t % 2) + D]
                    if e == 0 and not query:
                        mm(o, UTk[g.par][:, col + 128 * t:col + 128 * t + m], CWx[:, :], start=(t % 2 == 0), stop=False,
                           skip_group_check=True)
                    last = mm(o, h[step % HR][:, 128 * t:128 * t + m], W2T[:, e, :],
                              start=(e == 0 and query and t % 2 == 0), stop=(e == NE), skip_group_check=True)
                last.then_inc(l2_step, 1)

            def ffn_pe(g, left):
                for step in range(STEPS):
                    c, e = divmod(step, EX)
                    query, col, n = CHUNKS[c]
                    p = (g.par + step) % 2
                    wait(pe, silu_done, g.at(STEPS, step - 1))
                    if step == 0:
                        pe.wait_ge(aux_act, g.at(BYACT[-1], BYACT[-1]))
                    for k, o in ((0, h1_ps[p]), (1, h3_ps)):
                        if k == 1:
                            if step >= 2:
                                layer2(g, step - 2)
                            wait(pe, gated_done, g.at(STEPS, step))
                        w = (k * EX + e) * INTER
                        if query:
                            w, at = slice(w, w + INTER), slice(col, col + n)
                            last = products(o[:, 0:n], [WT0h[:, w], WT0l[:, w], WT0h[:, w], WT1s[:, w], WT1s[:, w]],
                                            [x0h[:, at], x0h[:, at], x0l[:, at], x1h[:, at], x1l[:, at]])
                        else:
                            last = mm(o[:, 0:n], Wx[:, w:w + INTER], X2T[g.par][:, col:col + n], start=True, stop=True)
                        last.then_inc(h1_ready if k == 0 else h3_ready, 1)
                    if e < NE:
                        wait(pe, h_done, g.at(NCH * NE, c * NE + e))
                        at = 512 * c
                        mm(cw_ps[:, 0:n], sel[:, e, :], cwT[:, at:at + n], start=True, stop=True).then_inc(cw_ready, 1)
                    if left:
                        for kind, i in items_at(step):
                            item(g.plus(1), kind, i)
                layer2(g, STEPS - 2)
                layer2(g, STEPS - 1)

            for kind, i in ITEMS:
                item(G(None, 0), kind, i)
            ffn_pe(G(None, 0), 1)
            with pe.Fori(0, 2) as k:
                for off in (1, 2):
                    ffn_pe(G(k, off), 1)
            ffn_pe(G(None, 5), 1)
            ffn_pe(G(None, 6), 1)
            ffn_pe(G(None, 7), 0)


INS = ["x", "L0_tok_channel_weights", "L0_attn_proj_w", "L0_attn_proj_b", "L0_ffn_gate_weight", "L0_ffn_gate_bias",
       "L0_ffn_w1", "L0_ffn_w2", "L0_ffn_w3", "L0_ffn_sw1", "L0_ffn_sw2", "L0_ffn_sw3"]


def kernel(**inputs):
    import numpy as np
    import concourse.bacc as bacc
    from concourse.bass_utils import run_bass_kernel_spmd

    nc = bacc.Bacc("TRN2", target_bir_lowering=False, num_devices=1)
    arrays, args = {}, []
    for name in INS:
        a = np.ascontiguousarray(inputs[name])
        arrays[f"in_{name}"] = a
        args.append(nc.dram_tensor(f"in_{name}", a.shape, mybir.dt.from_np(a.dtype), kind="ExternalInput").ap())
    out = nc.dram_tensor("out_0", (NB, TOK, D), F32, kind="ExternalOutput").ap()
    build(nc, *args, out)
    r = run_bass_kernel_spmd(nc, [arrays], core_ids=[0])
    return r.results[0]["out_0"]
```

```python
import concourse.bass as bass
from concourse import mybir
from concourse.alu_op_type import AluOpType as ALU
from contextlib import ExitStack

F32 = mybir.dt.float32
BF16 = mybir.dt.bfloat16
F32R = mybir.dt.float32r
ACT = mybir.ActivationFunctionType
AX = mybir.AxisListType

NB, CH, IMG, PATCH = 128, 12, 224, 16
NP = IMG // PATCH
TOK, NQ, D = NP * NP, 64, 192
NK = TOK - NQ
NE, INTER = 8, 128
EX = NE + 1
EPS = 1e-5
GB = 16
NG = NB // GB
CG = 3
HALF = NP // 2
HT = HALF * NP
UNITS = 2 * GB
UC, XC = CH + 2, CH
SPL = 3
ROW = IMG * PATCH
TILES = CG * HALF
SLOTS = 2
CHUNKS = [(True, 0, 512), (True, 512, 512), (False, 0, 512), (False, 2048, 64)]
CHUNKS += [(False, 512 * i, 512) for i in (1, 2, 3)]
TT = [(n + 127) // 128 for _, _, n in CHUNKS]
QCH = 2
EVAC = [sum((t + 1) // 2 for t in TT[QCH:c + 1]) for c in range(len(TT))]
KPAD = 2176
NCH = len(CHUNKS)
STEPS = NCH * EX
GT = 8 + 17
CWCOL = 1024 + GB * NK
SHARE = {"dve": (0, 7), "act": (7, 9), "pool": (9, NP)}
SHARE_K = {"dve": (0, 1), "act": (1, 8), "pool": (8, NP)}
SHARE0 = {"dve": (0, 8), "act": (8, 12), "pool": (12, NP)}
POOL_MAX = 6
ROWS = 3

PLAN = {
    2: [("fin", 0)],
    3: [("tok", 0), ("V", 0)],
    4: [("stats", 0)],
    6: [("stats2", 0)],
    7: [("PHT", 0), ("VHw", 0), ("Uw", 0)],
    8: [("PHT", 1), ("VHT", 0), ("Uw", 1)],
    9: [("S", 0), ("S", 1), ("Uw", 2)],
    11: [("S", 2), ("VHw", 1)],
    12: [("ET", 0), ("VHT", 1)],
    13: [("ET", 1), ("U", 0)],
    14: [("AH", 0), ("S", 3), ("S", 4)],
    16: [("S", 5), ("U", 1)],
    18: [("U", 2)],
    19: [("ET", 2), ("M", 0)],
    20: [("ET", 3), ("M", 1)],
    21: [("AH", 1), ("U", 3), ("U", 4)],
    22: [("U", 5), ("U", 6)],
    23: [("U", 7), ("M", 2)],
    24: [("M", 3), ("Xw", 0)],
    25: [("H", 0), ("Xw", 1)],
    26: [("H", 1), ("Xw", 2)],
    27: [("H", 2)],
    28: [("H", 3), ("H", 4)],
    29: [("H", 5)],
    30: [("H", 6), ("H", 7)],
    31: [("x2", 0), ("X", 0)],
    32: [("X", 1), ("X", 2)],
    33: [("x2", 1), ("X", 3)],
    34: [("x2", 2), ("X", 4)],
    35: [("X", 5)],
    36: [("XT", 0), ("XT", 1)],
    37: [("x2", 3), ("X", 6)],
    38: [("x2", 4), ("X", 7)],
    39: [("XT", 2)],
    40: [("XT", 3)],
    41: [("GQ", 0)],
    42: [("GQ", 1), ("keyG", 0)],
    43: [("keyG", 1), ("G", 0)],
    59: [("C", 0), ("C", 1)],
    60: [("C", 2), ("C", 6)],
    61: [("C", 3), ("C", 4), ("C", 5)],
}
A_FIRST = 2
GATES = 40
for _s in range(14):
    PLAN[45 + _s] = [("gate", n) for n in range(3 * _s, min(GATES, 3 * _s + 3))] + PLAN.get(45 + _s, [])
ITEMS = [it for s in sorted(PLAN) for it in PLAN[s]]
PE_KINDS = ("tok", "V", "PHT", "VHT", "S", "U", "ET", "AH", "M", "X", "H", "XT", "GQ", "G", "C")
DVE_KINDS = ("tok", "H", "AH", "XT")
ROUNDS = [it for it in ITEMS if it[0] in PE_KINDS]
NR = len(ROUNDS)
R = {it: i for i, it in enumerate(ROUNDS)}
BYDVE = [sum(1 for it in ROUNDS[:i + 1] if it[0] in DVE_KINDS) for i in range(NR)]
BYACT = [i + 1 - BYDVE[i] for i in range(NR)]
S_IMGS = [(0, 3), (3, 3), (6, 2), (8, 3), (11, 3), (14, 2)]
LINKS = 61

LATE = {s: i for i, s in enumerate([4, 6, 8, 10, 12, 13, 16, 19, 22, 25, 29, 36, 38, 41, 46, 49, 52, 55, 58])}
EARLY = {0: 19, 1: 20}
LATE0 = {s: i for i, s in enumerate([4, 6, 8, 10, 12, 14, 16, 18, 20, 22, 25, 28, 31, 34, 38, 44, 47, 50, 53])}



def items_at(step):
    return PLAN.get(step, [])


def share(g, t):
    if g.k is None and (g.off == 0 or g.off == 1 and t < len(LATE)):
        return SHARE0
    among_keys = any(LATE[s] == t for s in LATE if s >= QCH * EX)
    return SHARE_K if among_keys else SHARE


def tiles_at(g, step, groups_left=2):
    found = []
    if groups_left >= 1 and step in EARLY:
        found.append((g.plus(1), EARLY[step]))
    late = LATE0 if g.off < 0 else LATE
    if groups_left >= 2 and step in late:
        found.append((g.plus(2), late[step]))
    return found


class G:

    def __init__(self, k, off):
        self.k, self.off = k, off

    def plus(self, n):
        return G(self.k, self.off + n)

    @property
    def par(self):
        return self.off % 2

    def num(self):
        return self.off if self.k is None else self.k * 2 + self.off

    def at(self, per_group, n):
        v = self.off * per_group + n
        return v if self.k is None else self.k * (2 * per_group) + v

    def slot(self, t):
        return (self.off * TILES + t) % SLOTS

    def landed(self, t):
        v = 16 * ((self.off * TILES + t) // SLOTS + 1)
        return v if self.k is None else self.k * (16 * 2 * TILES // SLOTS) + v

    def bank(self, r):
        return (self.off * NR + r) % 2

    def stored(self, c):
        def upto(g, c):
            n = 0
            for gg in range(g + 1):
                for cc in range(NCH if gg < g else c + 1):
                    if (gg + cc) % 2 == (g + c) % 2:
                        n += TT[cc]
            return n
        n = upto(self.off, c) * 16
        return n if self.k is None else self.k * (sum(TT) * 16) + n

    def before(self, c):
        return self.stored(c) - 16 * TT[c]


def wait(eng, sem, value):
    if not isinstance(value, int) or value > 0:
        eng.wait_ge(sem, value)


def build(nc, x, cw, proj_w, proj_b, gate_w, gate_b, w1, w2, w3, sw1, sw2, sw3, out):
    ctx = ExitStack()
    with ctx:
        def sb(name, shape, dt=F32):
            return ctx.enter_context(nc.sbuf_tensor(name, shape, dt))

        def sem(name):
            return ctx.enter_context(nc.semaphore(name))

        ident = sb("ident", [128, 128])
        identb = sb("identb", [128, 128], BF16)
        mhalf = sb("mhalf", [128, UNITS])
        keymask = sb("keymask", [HT, UNITS])
        order8 = sb("order8", [128, 8])
        sel = sb("sel", [128, NE, 128], BF16)
        CW14 = sb("CW14", [UC, D])
        CWx = sb("CWx", [SPL * SPL * UC, D], BF16)
        blockG = sb("blockG", [128, CG, UNITS * (CH + 1)])
        CWr = sb("CWr", [128, 3, 4, 128])
        projT = sb("projT", [NQ, 3, D])
        WT0h = sb("WT0h", [128, 2 * EX * INTER], F32R)
        WT0l = sb("WT0l", [128, 2 * EX * INTER], F32R)
        WT1s = sb("WT1s", [128, 2 * EX * INTER], F32R)
        Wx = sb("Wx", [SPL * SPL * UC, 2 * EX * INTER + NE], BF16)
        W2T = sb("W2T", [INTER, EX, D])
        gT0h, gT0l, gT1s = sb("gT0h", [128, NE], F32R), sb("gT0l", [128, NE], F32R), sb("gT1s", [128, NE], F32R)
        gbias = sb("gbias", [128, NE])
        xt = sb("xt", [128, SLOTS, ROW])
        pooled = sb("pooled", [128, CG, HT])
        kh_sum = sb("kh_sum", [128, 8, POOL_MAX * PATCH])
        row_sum = sb("row_sum", [128, ROWS, POOL_MAX * PATCH])
        tokT = sb("tokT", [126, 2, KPAD + GB * NK], BF16)
        x0h, x0l = sb("x0h", [128, 1024], F32R), sb("x0l", [128, 1024], F32R)
        x1h, x1l = sb("x1h", [128, 1024], F32R), sb("x1l", [128, 1024], F32R)
        UTq = sb("UTq", [126, 1024], BF16)
        cwT = sb("cwT", [128, CWCOL], BF16)
        h2q = sb("h2q", [128, 8, D])
        HR = 3
        ffn = sb("ffn", [128, HR + 4, 512])
        stage = sb("stage", [128, 2, 4, D])
        Ptok = sb("Ptok", [HT, UNITS, CH])
        V = sb("V", [HT, UNITS, CH + 1])
        val = sb("val", [HT, UNITS, CH + 1])
        res = sb("res", [HT, UNITS, CH + 1])
        stat = sb("stat", [HT, 8, UNITS])
        SPT = sb("SPT", [HT, UNITS, SPL, SPL, UC], BF16)
        PH = sb("PH", [HT, UNITS, 32])
        PHT = sb("PHT", [128, 2, 4, HT])
        VHT = sb("VHT", [128, 8, NQ])
        attw = sb("attw", [128, 8 * 128 + 8 * TOK + 16 * NQ])
        sums = sb("sums", [NQ, 4, GB])
        Asb = sb("Asb", [NQ, 2, 8 * CH])
        Msb = sb("Msb", [128, 2, 3 * D])
        bst = sb("bst", [128, 8, 8])
        rq = sb("rq", [128, 3, 8])
        gt = sb("gt", [128, 4, GT * NE])
        gs = sb("gs", [128, 4, GT * 4])
        CS = sb("CS", [128, GT, SPL, NE], BF16)

        h = [ffn[:, i, :] for i in range(HR)]
        silu = [ffn[:, HR + i, :] for i in range(2)]
        gated = [ffn[:, HR + 2 + i, :] for i in range(2)]
        VHpad = attw[0:NQ, 0:1024].rearrange("p (b n) -> p b n", b=8)
        E = attw[0:NQ, 1024:1024 + 8 * TOK].rearrange("p (b n) -> p b n", b=8)
        ET = attw[0:HT, 1024 + 8 * TOK:].rearrange("p (u q) -> p u q", u=16)
        X2T = [tokT[:, i, 0:KPAD] for i in range(2)]
        UTk = [tokT[:, i, KPAD:] for i in range(2)]
        x2q = attw[:, 1024 + 8 * TOK:1024 + 8 * TOK + 4 * D].rearrange("p (t d) -> p t d", t=4)
        logT = attw[0:NE, 1024 + 8 * TOK:1024 + 8 * TOK + 1024]
        CWr_src = Msb[0:8 * CH, 0, 0:D]
        w13_nat = ffn[:, :, :].rearrange("p a b -> p (a b)")[:, 0:2 * EX * D].rearrange("p (e d) -> p e d", e=2 * EX)
        w2_natA = attw[:, 0:EX * INTER].rearrange("p (e i) -> p e i", e=EX)
        w2_natB = attw[0:64, EX * INTER:2 * EX * INTER].rearrange("p (e i) -> p e i", e=EX)
        WSP = tokT[0:CH, :, :].rearrange("p a b -> p (a b)")[:, 0:SPL * (2 * EX * INTER + NE)].rearrange(
            "p (s n) -> p s n", s=SPL)
        CSP = SPT[0:UC, :, :, :, :].rearrange("p a b c d -> p (a b c d)")[:, 0:SPL * D].rearrange("p (s n) -> p s n", s=SPL)
        pw_natA = h2q[:, 0, :]
        pw_natB = h2q[0:64, 1, :]
        g_nat = h2q[0:NE, 2, :]
        CWn = h2q[0:CH, 3, :]
        cres = h2q[0:UC, 4, :]
        CWcT = [rq[:, 0:3, :].rearrange("p a b -> p (a b)")[:, 0:CH], gs[:, 3, 0:CH]]
        G13 = sums[0:CH, :, :].rearrange("p a b -> p (a b)")[:, 0:CH + 1]
        rep = val[0:CH, :, :].rearrange("p a b -> p (a b)")[:, 0:CG * 128].rearrange("p (k n) -> p k n", k=CG)
        repG = gs[:, :, :].rearrange("p a b -> p (a b)")[:, 0:CG * (CH + 1)].rearrange("p (k c) -> p k c", k=CG)
        bmask = PHT[:, 0, 0, 0:UNITS]
        rmask = gt[0:8 * CH, 0, 0:8]
        wres = attw[0:CH, 2 * EX * INTER:2 * EX * INTER + 1024]

        bank = [ctx.enter_context(nc.psum_tensor(f"bank{i}", [128, 512], F32)) for i in range(8)]
        cw_ps, out_ps, aux = bank[3], bank[4:6], bank[6:8]

        def h_ps(step, k):
            return bank[(2 * step + k) % 3]

        assert 2 * STEPS % 3 == 0


        x_in = [sem(f"x_in{i}") for i in range(SLOTS)]
        dve_summed, act_summed, pool_summed = sem("dve_summed"), sem("act_summed"), sem("pool_summed")
        pool_read, tree_step, rows_used = sem("pool_read"), sem("tree_step"), sem("rows_used")
        h1_ready, h3_ready, cw_ready = sem("h1_ready"), sem("h3_ready"), sem("cw_ready")
        silu_done, gated_done, h_done = sem("silu_done"), sem("gated_done"), sem("h_done")
        l2_step, evac_dve, evac_act = sem("l2_step"), sem("evac_dve"), sem("evac_act")
        out_stored = [sem(f"out_stored{i}") for i in range(2)]
        aux_full, aux_dve, aux_act = sem("aux_full"), sem("aux_dve"), sem("aux_act")
        high_ready = sem("high_ready")
        dve_link, prep_link = sem("dve_link"), sem("prep_link")
        var_ready, rstd_ready = sem("var_ready"), sem("rstd_ready")
        ph_ready, vh_ready = sem("ph_ready"), sem("vh_ready")
        u_rep, x_rep = sem("u_rep"), sem("x_rep")
        max_ready, x2_ready, cs_ready = sem("max_ready"), sem("x2_ready"), sem("cs_ready")
        w_in, cw_in, pb_in, cwr_in, gb_in = sem("w_in"), sem("cw_in"), sem("pb_in"), sem("cwr_in"), sem("gb_in")
        const_done, prep_full, prep_dve, prep_act = sem("const_done"), sem("prep_full"), sem("prep_dve"), sem("prep_act")
        cwc_ready, cwx_split, w_split, wx_in, cwx_in = sem("cwc_ready"), sem("cwx_split"), sem("w_split"), sem("wx_in"), sem("cwx_in")
        ready = sem("ready")
        pool_link = sem("pool_link")
        pe_passed, dve_passed = sem("pe_passed"), sem("dve_passed")

        xv = x.rearrange("(g b) (k c) (s i h) w -> g k i b (c s) (h w)", b=GB, k=CG, s=2, h=PATCH)

        PREP = [("CWcT", 0), ("CWcT", 1), ("G", 0), ("gate", 0), ("repG", 0), ("gate", 1)]
        PREP += [("W0", i) for i in range(5)] + [("W1", i) for i in range(5)]
        PREP += [("Wc", i) for i in range(5)] + [("w2", i) for i in range(5)] + [("proj", 0), ("proj", 1)]
        WCOLS = 2 * EX * INTER

        def tiles_after(r):
            return [t for t in range(TILES) if min(len(PREP) - 1, 3 + t * 4 // 3) == r]

        P_AT = {it: i for i, it in enumerate(PREP)}
        P_DVE = [kind in ("W0", "W1", "gate") or i % 2 == 0 for i, (kind, _) in enumerate(PREP)]
        P_DVE_N = [sum(P_DVE[:i + 1]) for i in range(len(PREP))]
        P_ACT_N = [i + 1 - P_DVE_N[i] for i in range(len(PREP))]

        def w4(i):
            return 4 * i, min(4, 2 * EX - 4 * i)

        def wc(i):
            return 512 * i, min(512, WCOLS + NE - 512 * i)

        def prep_copies(r):
            kind, i = PREP[r]
            ps = aux[r % 2]
            if kind == "CWcT":
                return [(CWcT[i], ps[:, 0:CH])]
            if kind == "G":
                return [(G13[:, 0:CH], ps[0:CH, 0:CH])]
            if kind == "repG":
                return [(repG, ps[:, 0:CG * (CH + 1)].rearrange("p (k c) -> p k c", k=CG))]
            if kind == "w2":
                k = min(2, EX - 2 * i)
                return [(W2T[:, 2 * i:2 * i + k, :].rearrange("p e d -> p (e d)"), ps[:, 0:k * D])]
            if kind == "proj":
                k = 2 if i == 0 else 1
                return [(projT[:, 2 * i:2 * i + k, :].rearrange("p e d -> p (e d)"), ps[0:NQ, 0:k * D])]
            raise AssertionError(kind)

        def split_dst(r):
            kind, i = PREP[r]
            if kind == "gate":
                return NE, (gT0h if i == 0 else gT1s)[:, :], gT0l[:, :] if i == 0 else None
            a, k = w4(i)
            a, n = a * 128, k * 128
            return n, (WT0h if kind == "W0" else WT1s)[:, a:a + n], WT0l[:, a:a + n] if kind == "W0" else None

        block = ctx.enter_context(nc.Block())

        @block.sync
        def _(sp):
            sp.dma_start(CWn, cw).then_inc(cw_in, 16)
            sp.wait_ge(const_done, 1)
            sp.dma_start(CW14[CH + 1:UC, :], proj_b.rearrange("(a d) -> a d", a=1)).then_inc(pb_in, 16)
            for k, (w, shared) in enumerate(((w1, sw1), (w3, sw3))):
                sp.dma_start(w13_nat[:, k * EX:k * EX + NE, :], w.rearrange("e i d -> i e d")).then_inc(w_in, 16)
                sp.dma_start(w13_nat[:, k * EX + NE, :], shared).then_inc(w_in, 16)
            for nat, a, b in ((w2_natA, 0, 128), (w2_natB, 128, D)):
                sp.dma_start(nat[:, 0:NE, :], w2[:, a:b, :].rearrange("e d i -> d e i")).then_inc(w_in, 16)
                sp.dma_start(nat[:, NE, :], sw2[a:b, :]).then_inc(w_in, 16)
            sp.dma_start(pw_natA, proj_w[0:128, :]).then_inc(w_in, 16)
            sp.dma_start(pw_natB, proj_w[128:D, :]).then_inc(w_in, 16)
            sp.dma_start(g_nat, gate_w).then_inc(w_in, 16)
            sp.dma_start(gbias[:, :], gate_b.partition_broadcast(128)).then_inc(gb_in, 16)
            for t in range(SLOTS):
                sp.dma_start(xt[:, t, :], xv[0, t // HALF, t % HALF]).then_inc(x_in[t], 16)
            sp.wait_ge(cwc_ready, 1)
            for b in range(8):
                sp.dma_start(CWr_src[b * CH:(b + 1) * CH, :], CW14[0:CH, :]).then_inc(cwr_in, 16)
            sp.wait_ge(cwx_split, 1)
            for s in range(SPL):
                for q in range(SPL):
                    a = (s * SPL + q) * UC
                    sp.dma_start(CWx[a:a + UC, :], CSP[:, s, :]).then_inc(cwx_in, 16)

            def load(g, t):
                for s in (dve_summed, act_summed, pool_read):
                    wait(sp, s, g.at(TILES, t - SLOTS + 1))
                slot = g.slot(t)
                sp.dma_start(xt[:, slot, :], xv[g.num(), t // HALF, t % HALF]).then_inc(x_in[slot], 16)

            def store(g, c):
                query, col, n = CHUNKS[c]
                st = stage[:, (g.par + c) % 2, :, :]
                done = out_stored[(g.par + c) % 2]
                if query:
                    sp.wait_ge(evac_dve, g.at(4, 2 * c + 2))
                else:
                    sp.wait_ge(evac_act, g.at(EVAC[-1], EVAC[c]))
                og = out.rearrange("(g b) t d -> g b t d", b=GB)[g.num()]
                for t in range((n + 127) // 128):
                    if query:
                        b0 = (col + 128 * t) // NQ
                        dst = og[b0:b0 + 2, 0:NQ, :]
                    elif n == 512:
                        dst = og[4 * t:4 * t + 4, NQ + col // GB:NQ + col // GB + 32, :]
                    else:
                        dst = og[:, TOK - 4:TOK, :]
                    sp.dma_start(dst, st[0:min(n, 128), t, :]).then_inc(done, 16)

            def load_after(g, t):
                if t + SLOTS < TILES:
                    load(g, t + SLOTS)
                elif g.k is not None or g.off < NG - 1:
                    load(g.plus(1), t + SLOTS - TILES)

            def ffn_dma(g, left):
                for step in range(STEPS):
                    c, e = divmod(step, EX)
                    for gt_, t in tiles_at(g, step, left):
                        load_after(gt_, t)
                    if e == 3 and c > 0:
                        store(g, c - 1)
                store(g, NCH - 1)

            for t in range(TILES):
                load_after(G(None, 0), t)
            for step in range(A_FIRST, STEPS):
                for gt_, t in tiles_at(G(None, -1), step):
                    load_after(gt_, t)
            ffn_dma(G(None, 0), 2)
            with sp.Fori(0, 2) as k:
                for off in (1, 2):
                    ffn_dma(G(k, off), 2)
            ffn_dma(G(None, 5), 2)
            ffn_dma(G(None, 6), 1)
            ffn_dma(G(None, 7), 0)
            for s in range(2):
                sp.wait_ge(out_stored[s], sum(TT) * 16 * NG // 2)

        @block.gpsimd
        def _(pool):
            links = [0]

            def link(ins):
                links[0] += 1
                ins.then_inc(pool_link, 1)
                pool.wait_ge(pool_link, links[0])

            nc.gpsimd.memset(CW14[:, :], 1.0).then_inc(const_done, 1)
            link(nc.gpsimd.memset(ident[:, :], 0.0))
            link(nc.gpsimd.affine_select(out=ident[:, :], in_=ident[:, :], compare_op=ALU.not_equal, fill=1.0,
                                         base=0, pattern=[[-1, 128]], channel_multiplier=1))
            nc.gpsimd.tensor_copy(identb[:, :], ident[:, :]).then_inc(const_done, 1)
            nc.gpsimd.memset(mhalf[:, :], -0.5)
            for k in range(CG):
                link(nc.gpsimd.memset(rep[:, k, :], 0.0))
                link(nc.gpsimd.affine_select(out=rep[:, k, :].rearrange("p (b c s) -> p b c s", b=GB, c=4),
                                             in_=rep[:, k, :].rearrange("p (b c s) -> p b c s", b=GB, c=4),
                                             compare_op=ALU.not_equal, fill=1.0, base=-4 * k,
                                             pattern=[[0, GB], [-1, 4], [0, 2]], channel_multiplier=1))
            link(nc.gpsimd.memset(bmask, 0.0))
            for c in range(4):
                link(nc.gpsimd.affine_select(out=bmask.rearrange("p (s b) -> p s b", s=2),
                                             in_=bmask.rearrange("p (s b) -> p s b", s=2),
                                             compare_op=ALU.not_equal, fill=1.0, base=-2 * c,
                                             pattern=[[-1, 2], [-8, GB]], channel_multiplier=1))
            link(nc.gpsimd.memset(rmask, 1.0))
            link(nc.gpsimd.affine_select(out=rmask, in_=rmask, compare_op=ALU.is_ge, fill=0.0, base=0,
                                         pattern=[[-CH, 8]], channel_multiplier=1))
            link(nc.gpsimd.affine_select(out=rmask, in_=rmask, compare_op=ALU.is_ge, fill=0.0, base=CH - 1,
                                         pattern=[[CH, 8]], channel_multiplier=-1))
            link(nc.gpsimd.memset(sel[:, :, :], 0.0))
            for s in range(SPL):
                link(nc.gpsimd.affine_select(out=sel[:, :, :], in_=sel[:, :, :], compare_op=ALU.not_equal, fill=1.0,
                                             base=-NE * s, pattern=[[-1, NE], [0, 128]], channel_multiplier=1))
            for i in range(NE):
                nc.gpsimd.memset(order8[:, i:i + 1], float(NE - i))
            nc.gpsimd.memset(Wx[:, :], 0.0)
            link(nc.gpsimd.memset(keymask[:, :], 1.0))
            link(nc.gpsimd.memset(keymask[0:NQ, 0:GB], 0.0))
            nc.gpsimd.memset(PH[:, :, :], 0.0).then_inc(const_done, 1)

            def pool_tile(g, t, a, b):
                n = (b - a) * PATCH
                src = xt[:, g.slot(t), :].rearrange("p (h w) -> p h w", h=PATCH)[:, :, a * PATCH:b * PATCH]
                kh = kh_sum[:, :, 0:n]

                def add(step, out, in0, in1):
                    nc.gpsimd.tensor_tensor(out=out, in0=in0, in1=in1, op=ALU.add).then_inc(tree_step, 1)
                    pool.wait_ge(tree_step, g.at(2 * TILES, 2 * t + step))

                pool.wait_ge(x_in[g.slot(t)], g.landed(t))
                wait(pool, pool_summed, g.at(TILES, t))
                nc.gpsimd.tensor_tensor(out=kh, in0=src[:, 0:8, :], in1=src[:, 8:16, :],
                                        op=ALU.add).then_inc(pool_read, 1)
                pool.wait_ge(pool_read, g.at(TILES, t + 1))
                add(1, kh[:, 0:4, :], kh[:, 0:4, :], kh[:, 4:8, :])
                add(2, kh[:, 0:2, :], kh[:, 0:2, :], kh[:, 2:4, :])
                wait(pool, rows_used, g.at(TILES, t - ROWS + 1))
                nc.gpsimd.tensor_tensor(out=row_sum[:, t % ROWS, 0:n], in0=kh[:, 0, :], in1=kh[:, 1, :],
                                        op=ALU.add).then_inc(pool_summed, 1)

            def item(g, kind, i):
                if kind == "stats":
                    pool.wait_ge(var_ready, g.at(3, 1))
                    nc.gpsimd.tensor_tensor(out=stat[:, 1, :], in0=stat[:, 0, :], in1=mhalf[0:HT, :],
                                            op=ALU.pow).then_inc(rstd_ready, 1)
                elif kind == "stats2":
                    pool.wait_ge(var_ready, g.at(3, 2))
                    nc.gpsimd.tensor_tensor(out=stat[:, 4, :], in0=stat[:, 3, :], in1=mhalf[0:HT, :],
                                            op=ALU.pow).then_inc(rstd_ready, 1)
                elif kind == "x2" and i == 0:
                    pool.wait_ge(var_ready, g.at(3, 3))
                    nc.gpsimd.tensor_tensor(out=rq[:, 1, :], in0=rq[:, 0, :], in1=mhalf[:, 0:8],
                                            op=ALU.pow).then_inc(rstd_ready, 1)

            def step_pool(g, step, left):
                for gt_, t in tiles_at(g, step, left):
                    pool_tile(gt_, t, *share(gt_, t)["pool"])
                if left:
                    for kind, i in items_at(step):
                        item(g.plus(1), kind, i)

            def ffn_pool(g, left):
                for step in range(STEPS):
                    step_pool(g, step, left)

            for t in range(TILES):
                pool_tile(G(None, 0), t, *share(G(None, 0), t)["pool"])
            pool.wait_ge(ready, 1)
            for step in range(A_FIRST, STEPS):
                step_pool(G(None, -1), step, 2)
            ffn_pool(G(None, 0), 2)
            with pool.Fori(0, 2) as k:
                for off in (1, 2):
                    ffn_pool(G(k, off), 2)
            ffn_pool(G(None, 5), 2)
            ffn_pool(G(None, 6), 1)

        @block.scalar
        def _(act):
            def prep(r):
                act.wait_ge(prep_full, r + 1)
                kind, i = PREP[r]
                if kind == "Wc":
                    n = wc(i)[1]
                    if i >= 2:
                        act.wait_ge(w_split, i - 1)
                    nc.scalar.copy(wres[:, 512:512 + n], aux[r % 2][0:CH, 0:n]).then_inc(prep_act, 1)
                else:
                    for o, src in prep_copies(r):
                        nc.scalar.copy(o, src).then_inc(prep_act, 1)

            def act_tile(g, t, a, b, last_part=True):
                act.wait_ge(x_in[g.slot(t)], g.landed(t))
                if t == 0:
                    wait(act, aux_full, g.at(NR, R[("V", 0)] + 1 - NR))
                src = xt[:, g.slot(t), :].rearrange("p (h j w) -> p h j w", h=PATCH, j=NP)
                for j in range(a, b):
                    at = (t % HALF) * NP + j
                    last = nc.scalar.activation(src[:, :, j, :], src[:, :, j, :], ACT.Copy,
                                                accum_out=pooled[:, t // HALF, at:at + 1])
                if last_part:
                    last.then_inc(act_summed, 1)

            for r in range(len(PREP)):
                if not P_DVE[r]:
                    prep(r)
                if r == P_AT[("Wc", 4)] + 2:
                    act.wait_ge(w_split, 5)
                    act.wait_ge(const_done, 3)
                    for s in range(SPL):
                        for q in range(SPL):
                            a = (s * SPL + q) * UC
                            act.dma_start(Wx[a:a + XC, :], WSP[:, s, :]).then_inc(wx_in, 16)
                for t in tiles_after(r):
                    act_tile(G(None, 0), t, *SHARE0["act"])
            def item(g, kind, i):
                if kind not in PE_KINDS or kind in DVE_KINDS and kind != "XT":
                    return
                r = R[(kind, i)]
                ps = aux[g.bank(r)]
                act.wait_ge(aux_full, g.at(NR, r + 1))
                if kind == "V":
                    nc.scalar.copy(V[:, :, :].rearrange("p u c -> p (u c)"), ps[0:HT, 0:UNITS * (CH + 1)])\
                      .then_inc(aux_act, 1)
                elif kind == "PHT":
                    nc.scalar.copy(PHT[:, i, :, :].rearrange("p b t -> p (b t)"), ps[:, 0:4 * HT]).then_inc(aux_act, 1)
                elif kind == "VHT":
                    nc.scalar.copy(VHT[:, :, :].rearrange("p b q -> p (b q)"), ps[:, :]).then_inc(aux_act, 1)
                elif kind == "U":
                    src = ps[0:126, 0:2 * TOK].rearrange("p (b t) -> p b t", b=2)
                    nc.scalar.copy(UTq[:, :].rearrange("p (b t) -> p b t", b=GB)[:, 2 * i:2 * i + 2, :], src[:, :, 0:NQ])
                    keys_out(UTk[g.par], src[:, :, NQ:TOK], i).then_inc(aux_act, 1)
                elif kind == "X":
                    src = ps[0:126, 0:2 * NK].rearrange("p (b t) -> p b t", b=2)
                    keys_out(X2T[g.par], src, i).then_inc(aux_act, 1)
                elif kind == "S":
                    b0, nb = S_IMGS[i]
                    act.wait_ge(max_ready, g.at(6, i + 1))
                    for b in range(b0, b0 + nb):
                        last = nc.scalar.activation(E[:, b % 8, NQ:TOK], ps[0:NQ, (b - b0) * NK:(b - b0 + 1) * NK], ACT.Exp,
                                                    bias=sums[:, 0, b:b + 1], accum_out=sums[:, 1, b:b + 1])
                    last.then_inc(aux_act, 1)
                elif kind == "ET":
                    nc.scalar.copy(ET[:, 8 * (i % 2):8 * (i % 2) + 8, :].rearrange("p u q -> p (u q)"), ps[0:HT, :])\
                      .then_inc(aux_act, 1)
                elif kind == "M":
                    half, part = divmod(i, 2)
                    n = 2 * D if part == 0 else D
                    nc.scalar.copy(Msb[0:8 * CH, half, 2 * D * part:2 * D * part + n], ps[0:8 * CH, 0:n]).then_inc(aux_act, 1)
                elif kind == "XT":
                    q, part = divmod(i, 2)
                    nc.scalar.copy((x0h if part == 0 else x1h)[:, 512 * q:512 * q + 512], ps[:, :]).then_inc(high_ready, 1)
                elif kind == "GQ":
                    nc.scalar.copy(logT[:, 512 * i:512 * i + 512], ps[0:NE, :]).then_inc(aux_act, 1)
                elif kind == "G":
                    nc.scalar.activation(gt[:, 0, :], ps[:, 0:GT * NE], ACT.Exp, scale=-1.0).then_inc(aux_act, 1)
                elif kind == "C":
                    n = 512 if i < 6 else 64
                    nc.scalar.copy(cwT[0:SPL * NE, 512 * i:512 * i + n], ps[0:SPL * NE, 0:n]).then_inc(aux_act, 1)

            def keys_out(dst, src, i):
                nc.scalar.copy(dst[:, 0:2048].rearrange("p (c b k) -> p b c k", c=4, b=GB)[:, 2 * i:2 * i + 2, :, :],
                               src[:, :, 0:128].rearrange("p b (c k) -> p b c k", c=4))
                return nc.scalar.copy(dst[:, 2048:2112].rearrange("p (b k) -> p b k", b=GB)[:, 2 * i:2 * i + 2, :],
                                      src[:, :, 128:NK])

            def evacuate(g, c):
                n = CHUNKS[c][2]
                act.wait_ge(l2_step, g.at(STEPS, (c + 1) * EX))
                wait(act, out_stored[(g.par + c) % 2], g.before(c))
                st = stage[:, (g.par + c) % 2, :, :].rearrange("p t d -> p (t d)")
                if n == 512:
                    for b in range(2):
                        nc.scalar.copy(st[:, 2 * D * b:2 * D * b + 2 * D], out_ps[b][:, 0:2 * D]).then_inc(evac_act, 1)
                else:
                    nc.scalar.copy(st[0:n, 0:D], out_ps[0][0:n, 0:D]).then_inc(evac_act, 1)

            def step_act(g, step, left):
                for gt_, t in tiles_at(g, step - 1, left) if step > 0 else []:
                    a, b = share(gt_, t)["act"]
                    if b - a > 4:
                        act_tile(gt_, t, a + 4, b)
                for gt_, t in tiles_at(g, step, left):
                    a, b = share(gt_, t)["act"]
                    act_tile(gt_, t, a, min(b, a + 4), b - a <= 4)
                if left:
                    for kind, i in items_at(step):
                        item(g.plus(1), kind, i)

            def ffn_act(g, left):
                for step in range(STEPS):
                    c, e = divmod(step, EX)
                    n = CHUNKS[c][2]
                    act.wait_ge(h1_ready, g.at(STEPS, step + 1))
                    wait(act, gated_done, g.at(STEPS, step - 1))
                    p = (g.par + step) % 2
                    nc.scalar.activation(silu[p][:, 0:n], h_ps(step, 0)[:, 0:n], ACT.Silu).then_inc(silu_done, 1)
                    if e == 1 and c > 2:
                        evacuate(g, c - 1)
                    step_act(g, step, left)
                evacuate(g, NCH - 1)

            act.wait_ge(ready, 1)
            for step in range(A_FIRST, STEPS):
                step_act(G(None, -1), step, 2)
            ffn_act(G(None, 0), 2)
            with act.Fori(0, 2) as k:
                for off in (1, 2):
                    ffn_act(G(k, off), 2)
            ffn_act(G(None, 5), 2)
            ffn_act(G(None, 6), 1)
            ffn_act(G(None, 7), 0)

        @block.vector
        def _(dve):
            links = [0]
            v = nc.vector

            plinks = [0]

            def plink(ins):
                plinks[0] += 1
                ins.then_inc(prep_link, 1)
                dve.wait_ge(prep_link, plinks[0])

            def dve_tile(g, t, lo, hi):
                dve.wait_ge(x_in[g.slot(t)], g.landed(t))
                if t == 0:
                    wait(dve, aux_full, g.at(NR, R[("V", 0)] + 1 - NR))
                src = xt[:, g.slot(t), :].rearrange("p (h j w) -> p j h w", h=PATCH, j=NP)
                at = (t % HALF) * NP
                v.tensor_reduce(out=pooled[:, t // HALF, at + lo:at + hi], in_=src[:, lo:hi, :, :],
                                axis=AX.XY, op=ALU.add).then_inc(dve_summed, 1)

            def finish_rows(g, t, lo, hi):
                dve.wait_ge(pool_summed, g.at(TILES, t + 1))
                at = (t % HALF) * NP
                v.tensor_reduce(out=pooled[:, t // HALF, at + lo:at + hi],
                                in_=row_sum[:, t % ROWS, 0:(hi - lo) * PATCH].rearrange("p (j w) -> p j w", w=PATCH),
                                axis=AX.X, op=ALU.add).then_inc(rows_used, 1)

            def dve_sums(g, t):
                dve_tile(g, t, *share(g, t)["dve"])
                if t > 0:
                    finish_rows(g, t - 1, *share(g, t - 1)["pool"])

            plink(v.memset(cwT[:, :], 0.0))
            plink(v.memset(CWr[8 * CH:128, :, :, :], 0.0))
            plink(v.memset(Msb[8 * CH:128, :, :], 0.0))
            dve.wait_ge(cw_in, 16)
            dve.wait_ge(const_done, 1)
            plink(v.tensor_reduce(out=sums[0:CH, 1, 0:1], in_=CWn, axis=AX.X, op=ALU.add))
            plink(v.tensor_scalar(G13[:, CH:CH + 1], sums[0:CH, 1, 0:1], 1.0 / D, None, ALU.mult))
            v.tensor_scalar(CW14[0:CH, :], CWn, G13[:, CH:CH + 1], None, ALU.subtract).then_inc(cwc_ready, 1)
            dve.wait_ge(cwc_ready, 1)
            dve.wait_ge(pb_in, 16)
            plink(v.tensor_copy(CSP[:, 0, :], CW14[:, :]))
            plink(v.tensor_tensor(out=cres, in0=CW14[:, :], in1=CSP[:, 0, :], op=ALU.subtract))
            plink(v.tensor_copy(CSP[:, 1, :], cres))
            v.tensor_tensor(out=CSP[:, 2, :], in0=cres, in1=CSP[:, 1, :], op=ALU.subtract).then_inc(cwx_split, 1)

            def split_w(i, src):
                a, n = wc(i)
                plink(v.tensor_copy(WSP[:, 0, a:a + n], src))
                plink(v.tensor_tensor(out=src, in0=src, in1=WSP[:, 0, a:a + n], op=ALU.subtract))
                plink(v.tensor_copy(WSP[:, 1, a:a + n], src))
                v.tensor_tensor(out=WSP[:, 2, a:a + n], in0=src, in1=WSP[:, 1, a:a + n],
                                op=ALU.subtract).then_inc(w_split, 1)

            def prep(r):
                dve.wait_ge(prep_full, r + 1)
                if PREP[r][0] == "Wc":
                    i = PREP[r][1]
                    a, n = wc(i)
                    plink(v.tensor_copy(wres[:, 0:n], aux[r % 2][0:CH, 0:n]))
                    v.sem_inc(prep_dve, 1)
                    split_w(i, wres[:, 0:n])
                    if i + 1 < 5:
                        dve.wait_ge(prep_act, P_ACT_N[r + 1])
                        split_w(i + 1, wres[:, 512:512 + wc(i + 1)[1]])
                elif PREP[r][0] in ("W0", "W1", "gate"):
                    n, high, low = split_dst(r)
                    ps = aux[r % 2]
                    plink(v.tensor_copy(high, ps[:, 0:n]))
                    if low is None:
                        high, low, ps = high[64:128], high[64:128], ps[64:128]
                    v.tensor_tensor(out=low, in0=ps[:, 0:n], in1=high.bitcast(F32), op=ALU.subtract).then_inc(prep_dve, 1)
                else:
                    for o, i in prep_copies(r):
                        v.tensor_copy(o, i).then_inc(prep_dve, 1)
                if PREP[r][0] == "repG":
                    dve.wait_ge(prep_dve, P_DVE_N[r])
                    dve.wait_ge(const_done, 3)
                    for k in range(CG):
                        plink(v.tensor_tensor(
                            out=blockG[:, k, :].rearrange("p (u c) -> p u c", u=UNITS),
                            in0=bmask.unsqueeze(2).to_broadcast([128, UNITS, CH + 1]),
                            in1=repG[:, k, :].unsqueeze(1).to_broadcast([128, UNITS, CH + 1]), op=ALU.mult))

            def spread_cwc():
                dve.wait_ge(cwr_in, 16 * 8)
                for b in range(8):
                    plink(v.tensor_scalar(CWr[0:8 * CH, :, b // 2, 64 * (b % 2):64 * (b % 2) + 64],
                                          CWr_src.rearrange("p (i r) -> p r i", r=3), rmask[:, b:b + 1], None, ALU.mult))
                dve.wait_ge(cwx_in, 9 * 16)
                plink(v.memset(SPT[:, :, :, :, :].rearrange("p a b c d -> p (a b c d)"), 0.0))
                plink(v.memset(SPT[0:NQ, 0:GB, 0, 0, CH + 1:UC], 1.0))

            for r in range(len(PREP)):
                if P_DVE[r]:
                    prep(r)
                for t in tiles_after(r):
                    dve_sums(G(None, 0), t)
                if r == 4:
                    spread_cwc()
            dve.wait_ge(prep_full, len(PREP))
            dve.wait_ge(wx_in, 9 * 16)
            plink(v.memset(VHpad, 0.0))
            plink(v.memset(E, 0.0))
            for i in range(2):
                plink(v.memset(X2T[i][:, 2112:KPAD], 0.0))
            dve.wait_ge(gb_in, 16)
            v.sem_inc(ready, 1)

            def link(g, ins):
                links[0] += 1
                ins.then_inc(dve_link, 1)
                dve.wait_ge(dve_link, g.at(LINKS, links[0]))

            def split3(g, part, src, n, done):
                if part == 1:
                    link(g, v.tensor_copy(SPT[:, :, 0, 0, 0:n], src))
                    link(g, v.tensor_tensor(out=res[:, :, 0:n], in0=src, in1=SPT[:, :, 0, 0, 0:n], op=ALU.subtract))
                else:
                    link(g, v.tensor_copy(SPT[:, :, 0, 1, 0:n], res[:, :, 0:n]))
                    link(g, v.tensor_tensor(out=SPT[:, :, 0, 2, 0:n], in0=res[:, :, 0:n], in1=SPT[:, :, 0, 1, 0:n],
                                            op=ALU.subtract))
                    for r in (1, 2):
                        v.tensor_copy(SPT[:, :, r, :, :].rearrange("p u s c -> p u (s c)"),
                                      SPT[:, :, 0, :, :].rearrange("p u s c -> p u (s c)")).then_inc(done, 1)

            def item(g, kind, i):
                if kind in DVE_KINDS:
                    r = R[(kind, i)]
                    ps = aux[g.bank(r)]
                    dve.wait_ge(aux_full, g.at(NR, r + 1))
                if kind == "fin":
                    finish_rows(g, TILES - 1, *share(g, TILES - 1)["pool"])
                elif kind == "tok":
                    for k in range(CG):
                        ins = v.tensor_copy(
                            Ptok[:, :, 4 * k:4 * k + 4].rearrange("p (s b) c -> p s b c", s=2),
                            ps[0:HT, 128 * k:128 * k + 128].rearrange("p (b c s) -> p s b c", b=GB, c=4))
                    ins.then_inc(aux_dve, 1)
                elif kind == "stats":
                    links[0] = 0
                    dve.wait_ge(aux_dve, g.at(BYDVE[-1], BYDVE[R[("tok", 0)]]))
                    dve.wait_ge(aux_act, g.at(BYACT[-1], BYACT[R[("V", 0)]]))
                    link(g, v.tensor_tensor(out=val[:, :, 0:CH], in0=Ptok[:, :, :], in1=V[:, :, 0:CH], op=ALU.mult))
                    link(g, v.tensor_reduce(out=stat[:, 2, :], in_=val[:, :, 0:CH], axis=AX.X, op=ALU.add))
                    link(g, v.tensor_scalar(stat[:, 2, :], stat[:, 2, :], 1.0 / D, 0.0, ALU.mult, ALU.max))
                    v.tensor_scalar(stat[:, 0, :], stat[:, 2, :], EPS, None, ALU.add).then_inc(var_ready, 1)
                elif kind == "stats2":
                    dve.wait_ge(rstd_ready, g.at(3, 1))
                    link(g, v.tensor_tensor(out=stat[:, 5, :], in0=stat[:, 1, :], in1=keymask[:, :], op=ALU.mult))
                    link(g, v.tensor_scalar(stat[:, 5, :], stat[:, 5, :], 1.0, None, ALU.add))
                    link(g, v.tensor_tensor(out=stat[:, 6, :], in0=stat[:, 5, :], in1=stat[:, 5, :], op=ALU.mult))
                    link(g, v.tensor_tensor(out=stat[:, 6, :], in0=stat[:, 6, :], in1=stat[:, 2, :], op=ALU.mult))
                    v.tensor_scalar(stat[:, 3, :], stat[:, 6, :], EPS, None, ALU.add).then_inc(var_ready, 1)
                    wait(dve, aux_full, g.at(NR, R[("AH", 1)] + 1 - NR))
                    v.tensor_tensor(out=PH[:, :, 0:CH], in0=Ptok[:, :, :],
                                    in1=stat[:, 1, :].unsqueeze(2).to_broadcast([HT, UNITS, CH]),
                                    op=ALU.mult).then_inc(ph_ready, 1)
                elif kind == "VHw":
                    if i == 1:
                        dve.wait_ge(aux_full, g.at(NR, R[("VHT", 0)] + 1))
                    for q in range(2):
                        src = V[0:NQ, 8 * i + 4 * q:8 * i + 4 * q + 4, 0:CH]
                        dst = attw[0:NQ, 512 * q:512 * q + 640].rearrange("p (m n) -> p m n", m=4)[:, :, 0:CH]
                        ins = v.scalar_tensor_tensor(out=dst, in0=src, scalar=float(D // 12) ** -0.5,
                                                     in1=stat[0:NQ, 1, 8 * i + 4 * q:8 * i + 4 * q + 4].unsqueeze(2)
                                                     .to_broadcast([NQ, 4, CH]), op0=ALU.mult, op1=ALU.mult)
                    ins.then_inc(vh_ready, 1)
                elif kind == "Uw" and i == 0:
                    wait(dve, aux_full, g.at(NR, R[("X", 7)] + 1 - NR))
                    link(g, v.tensor_tensor(out=val[:, :, 0:CH], in0=Ptok[:, :, :],
                                            in1=stat[:, 5, :].unsqueeze(2).to_broadcast([HT, UNITS, CH]), op=ALU.mult))
                    link(g, v.tensor_copy(val[:, :, CH:CH + 1], V[:, :, CH:CH + 1]))
                elif kind == "Uw":
                    split3(g, i, val[:, :, :], CH + 1, u_rep)
                elif kind == "Xw" and i == 0:
                    dve.wait_ge(rstd_ready, g.at(3, 2))
                    link(g, v.tensor_tensor(out=stat[:, 7, :], in0=stat[:, 4, :], in1=stat[:, 5, :], op=ALU.mult))
                    link(g, v.tensor_tensor(out=val[:, :, 0:CH], in0=Ptok[:, :, :],
                                            in1=stat[:, 7, :].unsqueeze(2).to_broadcast([HT, UNITS, CH]), op=ALU.mult))
                elif kind == "Xw":
                    if i == 1:
                        dve.wait_ge(aux_full, g.at(NR, R[("U", 7)] + 1))
                    split3(g, i, val[:, :, 0:CH], CH, x_rep)
                elif kind == "S_max":
                    b0, nb = S_IMGS[i]
                    r = R[("S", i)]
                    dve.wait_ge(aux_full, g.at(NR, r + 1))
                    v.tensor_reduce(out=sums[:, 0, b0:b0 + nb],
                                    in_=aux[g.bank(r)][0:NQ, 0:nb * NK].rearrange("p (b k) -> p b k", b=nb),
                                    axis=AX.X, op=ALU.max, negate=True).then_inc(max_ready, 1)
                elif kind == "AH":
                    link(g, v.reciprocal(sums[:, 2, 8 * i:8 * i + 8], sums[:, 1, 8 * i:8 * i + 8]))
                    v.tensor_tensor(out=Asb[:, i, :].rearrange("p (b c) -> p b c", b=8),
                                    in0=ps[0:NQ, 0:8 * CH].rearrange("p (b c) -> p b c", b=8),
                                    in1=sums[:, 2, 8 * i:8 * i + 8].unsqueeze(2).to_broadcast([NQ, 8, CH]),
                                    op=ALU.mult).then_inc(aux_dve, 1)
                elif kind == "H":
                    v.bn_stats(bst[:, i, 0:6], ps[:, 0:D])
                    v.tensor_copy(h2q[:, i, :], ps[:, 0:D]).then_inc(aux_dve, 1)
                elif kind == "x2" and i == 0:
                    dve.wait_ge(aux_dve, g.at(BYDVE[-1], BYDVE[R[("H", 7)]]))
                    dve.sem_inc(dve_passed, 1)
                    for t in range(8):
                        ins = v.bn_aggr(bst[:, t, 6:8], bst[:, t, 0:6])
                    link(g, ins)
                    v.tensor_scalar(rq[:, 0, :], bst[:, :, 7], EPS, None, ALU.add).then_inc(var_ready, 1)
                elif kind == "x2":
                    if i == 1:
                        dve.wait_ge(rstd_ready, g.at(3, 3))
                    if i == 3:
                        dve.wait_ge(aux_full, g.at(NR, R[("XT", 1)] + 1))
                    for t in range(2 * i - 2, 2 * i):
                        v.tensor_scalar(x2q[:, t % 4, :], h2q[:, t, :], bst[:, t, 6:7], rq[:, 1, t:t + 1],
                                        ALU.subtract, ALU.mult).then_inc(x2_ready, 1)
                elif kind == "XT":
                    q, part = divmod(i, 2)
                    high, low = (x0h, x0l) if part == 0 else (x1h, x1l)
                    dve.wait_ge(high_ready, g.at(4, i + 1))
                    v.tensor_tensor(out=low[:, 512 * q:512 * q + 512], in0=ps[:, :],
                                    in1=high[:, 512 * q:512 * q + 512].bitcast(F32), op=ALU.subtract).then_inc(aux_dve, 1)
                elif kind == "gate":
                    gates(g, i)

            def gates(g, n):
                t3 = "p (t e) -> p t e"
                a, b, c, d = [gt[:, j, :].rearrange(t3, t=GT) for j in range(4)]
                ga, gb_, gc = [gs[:, j, :].rearrange(t3, t=GT) for j in range(3)]
                best = gs[:, 3, 0:GT]
                m4 = gs[:, 1, :].rearrange("p (t m) -> p t m", t=GT).unsqueeze(3).to_broadcast([128, GT, 4, 2])
                b4 = gt[:, 1, :].rearrange("p (t m e) -> p t m e", t=GT, m=4)
                def over(x, n):
                    return x.unsqueeze(2).to_broadcast([128, GT, n])

                def order(n):
                    return order8[:, NE - n:NE].unsqueeze(1).to_broadcast([128, GT, n])

                if n == 0:
                    dve.wait_ge(aux_act, g.at(BYACT[-1], BYACT[R[("G", 0)]]))
                else:
                    dve.wait_ge(dve_link, g.at(LINKS, links[0]))
                if n == 0:
                    ins = v.tensor_scalar(a, a, 1.0, None, ALU.add)
                elif n == 1:
                    ins = v.reciprocal(a, a)
                elif n == 2:
                    ins = v.tensor_tensor(out=b, in0=a, in1=gbias[:, :].unsqueeze(1).to_broadcast([128, GT, NE]), op=ALU.add)
                elif n == 3:
                    ins = v.tensor_reduce(out=ga, in_=b4, axis=AX.X, op=ALU.add)
                elif n == 4:
                    ins = v.tensor_reduce(out=best, in_=ga, axis=AX.X, op=ALU.max)
                elif n == 5:
                    ins = v.tensor_tensor(out=gc, in0=ga, in1=over(best, 4), op=ALU.is_equal)
                elif n == 6:
                    ins = v.tensor_tensor(out=gc, in0=gc, in1=order(4), op=ALU.mult)
                elif n == 7:
                    ins = v.tensor_reduce(out=best, in_=gc, axis=AX.X, op=ALU.max)
                elif n == 8:
                    ins = v.tensor_tensor(out=gb_, in0=gc, in1=over(best, 4), op=ALU.is_equal)
                elif n == 9:
                    ins = v.scalar_tensor_tensor(out=ga, in0=gb_, scalar=-1e30, in1=ga, op0=ALU.mult, op1=ALU.add)
                elif n == 10:
                    ins = v.tensor_reduce(out=best, in_=ga, axis=AX.X, op=ALU.max)
                elif n == 11:
                    ins = v.tensor_tensor(out=ga, in0=ga, in1=over(best, 4), op=ALU.is_equal)
                elif n == 12:
                    ins = v.tensor_tensor(out=ga, in0=ga, in1=order(4), op=ALU.mult)
                elif n == 13:
                    ins = v.tensor_reduce(out=best, in_=ga, axis=AX.X, op=ALU.max)
                elif n == 14:
                    ins = v.tensor_tensor(out=gc, in0=ga, in1=over(best, 4), op=ALU.is_equal)
                elif n == 15:
                    ins = v.tensor_tensor(out=gb_, in0=gb_, in1=gc, op=ALU.add)
                elif n == 16:
                    ins = v.tensor_tensor(out=b4, in0=b4, in1=m4, op=ALU.mult)
                elif n == 17:
                    ins = v.tensor_scalar(gb_, gb_, -1.0, 1e30, ALU.add, ALU.mult)
                elif n == 18:
                    ins = v.tensor_tensor(out=b4, in0=b4, in1=m4, op=ALU.add)
                elif n == 19:
                    ins = v.tensor_reduce(out=best, in_=b, axis=AX.X, op=ALU.max)
                elif n == 20:
                    ins = v.tensor_tensor(out=c, in0=b, in1=over(best, NE), op=ALU.is_equal)
                elif n == 21:
                    ins = v.tensor_tensor(out=c, in0=c, in1=order(NE), op=ALU.mult)
                elif n == 22:
                    ins = v.tensor_reduce(out=best, in_=c, axis=AX.X, op=ALU.max)
                elif n == 23:
                    ins = v.tensor_tensor(out=d, in0=c, in1=over(best, NE), op=ALU.is_equal)
                elif n == 24:
                    ins = v.scalar_tensor_tensor(out=b, in0=d, scalar=-2e30, in1=b, op0=ALU.mult, op1=ALU.add)
                elif n == 25:
                    ins = v.tensor_reduce(out=best, in_=b, axis=AX.X, op=ALU.max)
                elif n == 26:
                    ins = v.tensor_tensor(out=c, in0=b, in1=over(best, NE), op=ALU.is_equal)
                elif n == 27:
                    ins = v.tensor_tensor(out=c, in0=c, in1=order(NE), op=ALU.mult)
                elif n == 28:
                    ins = v.tensor_reduce(out=best, in_=c, axis=AX.X, op=ALU.max)
                elif n == 29:
                    ins = v.tensor_tensor(out=b, in0=c, in1=over(best, NE), op=ALU.is_equal)
                elif n == 30:
                    ins = v.tensor_tensor(out=d, in0=d, in1=b, op=ALU.add)
                elif n == 31:
                    ins = v.tensor_tensor(out=a, in0=a, in1=d, op=ALU.mult)
                elif n == 32:
                    ins = v.tensor_reduce(out=best, in_=a, axis=AX.X, op=ALU.add)
                elif n == 33:
                    ins = v.tensor_scalar(best, best, 1e-6, None, ALU.add)
                elif n == 34:
                    ins = v.reciprocal(best, best)
                elif n == 35:
                    ins = v.tensor_tensor(out=a, in0=a, in1=over(best, NE), op=ALU.mult)
                elif n == 36:
                    wait(dve, aux_full, g.at(NR, 0))
                    ins = v.tensor_copy(CS[:, :, 0, :], a)
                elif n == 37:
                    ins = v.tensor_tensor(out=b, in0=a, in1=CS[:, :, 0, :], op=ALU.subtract)
                elif n == 38:
                    ins = v.tensor_copy(CS[:, :, 1, :], b)
                elif n == 39:
                    ins = v.tensor_tensor(out=CS[:, :, 2, :], in0=b, in1=CS[:, :, 1, :], op=ALU.subtract)
                if n == GATES - 1:
                    ins.then_inc(cs_ready, 1)
                    assert links[0] == LINKS, links[0]
                else:
                    links[0] += 1
                    ins.then_inc(dve_link, 1)

            def step_dve(g, step, left, skip=0):
                if left:
                    for kind, i in items_at(step)[skip:]:
                        item(g.plus(1), "S_max" if kind == "S" else kind, i)
                for gt_, t in tiles_at(g, step, left):
                    dve_sums(gt_, t)

            def evacuate(g, c):
                dve.wait_ge(l2_step, g.at(STEPS, (c + 1) * EX))
                wait(dve, out_stored[(g.par + c) % 2], g.before(c))
                for b in range(2):
                    v.tensor_tensor(out=stage[:, (g.par + c) % 2, 2 * b:2 * b + 2, :],
                                    in0=out_ps[b][:, 0:2 * D].rearrange("p (t d) -> p t d", t=2),
                                    in1=h2q[:, 4 * c + 2 * b:4 * c + 2 * b + 2, :], op=ALU.add).then_inc(evac_dve, 1)

            def ffn_dve(g, left):
                for step in range(STEPS):
                    c, e = divmod(step, EX)
                    n = CHUNKS[c][2]
                    if e == 1 and c in (1, 2):
                        evacuate(g, c - 1)
                    p = (g.par + step) % 2
                    dve.wait_ge(silu_done, g.at(STEPS, step + 1))
                    dve.wait_ge(h3_ready, g.at(STEPS, step + 1))
                    if e == NE:
                        wait(dve, l2_step, g.at(STEPS, step - HR + 1))
                        v.tensor_tensor(out=h[step % HR][:, 0:n], in0=h_ps(step, 1)[:, 0:n], in1=silu[p][:, 0:n],
                                        op=ALU.mult).then_inc(gated_done, 1)
                    else:
                        v.tensor_tensor(out=gated[p][:, 0:n], in0=h_ps(step, 1)[:, 0:n], in1=silu[p][:, 0:n],
                                        op=ALU.mult).then_inc(gated_done, 1)
                    between = left and e < NE and items_at(step)[:1] and items_at(step)[0][0] == "gate"
                    if between:
                        item(g.plus(1), *items_at(step)[0])
                    if e < NE:
                        dve.wait_ge(gated_done, g.at(STEPS, step + 1))
                        dve.wait_ge(cw_ready, g.at(NCH * NE, c * NE + e + 1))
                        wait(dve, l2_step, g.at(STEPS, step - HR + 1))
                        v.tensor_tensor(out=h[step % HR][:, 0:n], in0=cw_ps[:, 0:n], in1=gated[p][:, 0:n],
                                        op=ALU.mult).then_inc(h_done, 1)
                    step_dve(g, step, left, 1 if between else 0)

            for step in range(A_FIRST, STEPS):
                step_dve(G(None, -1), step, 2)
            ffn_dve(G(None, 0), 2)
            with dve.Fori(0, 2) as k:
                for off in (1, 2):
                    ffn_dve(G(k, off), 2)
            ffn_dve(G(None, 5), 2)
            ffn_dve(G(None, 6), 1)
            ffn_dve(G(None, 7), 0)

        @block.tensor
        def _(pe):
            mm = nc.tensor.matmul
            pe.wait_ge(const_done, 2)
            for r, (kind, i) in enumerate(PREP):
                ps = aux[r % 2]
                if r >= 2:
                    pe.wait_ge(prep_dve if P_DVE[r - 2] else prep_act, P_DVE_N[r - 2] if P_DVE[r - 2] else P_ACT_N[r - 2])
                if kind == "CWcT":
                    pe.wait_ge(cwc_ready, 1)
                    n = 128 if i == 0 else 64
                    last = nc.tensor.transpose(ps[0:n, 0:CH], CW14[0:CH, 128 * i:128 * i + n], ident[0:CH, 0:CH])
                    if i == 1:
                        last = mm(ps[64:128, 0:CH], CW14[0:CH, 128:D], ident[0:CH, 0:CH], start=True, stop=True)
                elif kind == "G":
                    pe.wait_ge(prep_dve, 1)
                    pe.wait_ge(prep_act, 1)
                    mm(ps[0:CH, 0:CH], CWcT[0], CWcT[0], start=True, stop=False)
                    last = mm(ps[0:CH, 0:CH], CWcT[1][0:64], CWcT[1][0:64], start=False, stop=True)
                elif kind == "repG":
                    pe.wait_ge(prep_dve, P_DVE_N[P_AT[("G", 0)]])
                    pe.wait_ge(const_done, 3)
                    for k in range(CG):
                        last = mm(ps[:, k * (CH + 1):(k + 1) * (CH + 1)], rep[:, k, :], G13, start=True, stop=True)
                elif kind == "gate":
                    pe.wait_ge(w_in, 11 * 16)
                    n = 128 if i == 0 else 64
                    last = nc.tensor.transpose(ps[0:n, 0:NE], g_nat[:, 128 * i:128 * i + n], ident[0:NE, 0:NE])
                    if i == 1:
                        last = mm(ps[64:128, 0:NE], g_nat[:, 128:D], ident[0:NE, 0:NE], start=True, stop=True)
                elif kind == "W0":
                    a, k = w4(i)
                    for j in range(k):
                        last = nc.tensor.transpose(ps[:, 128 * j:128 * j + 128], w13_nat[:, a + j, 0:128], ident[:, :])
                elif kind == "W1":
                    a, k = w4(i)
                    for j in range(k):
                        nc.tensor.transpose(ps[0:64, 128 * j:128 * j + 128], w13_nat[:, a + j, 128:D], ident[:, :])
                        last = mm(ps[64:128, 128 * j:128 * j + 128], w13_nat[:, a + j, 128:D], ident[:, :],
                                  start=True, stop=True)
                elif kind == "Wc":
                    pe.wait_ge(prep_dve, P_DVE_N[P_AT[("W1", 4)]])
                    a, n = wc(i)
                    m = min(n, WCOLS - a)
                    for lo, hi, parts in ((0, m, [w[:, a:a + m] for w in (WT0h, WT0l, WT1s)]),
                                          (m, n, [w[:, :] for w in (gT0h, gT0l, gT1s)])):
                        if lo < hi:
                            for q in range(3):
                                last = mm(ps[0:CH, lo:hi], CWcT[q // 2], parts[q].bitcast(F32), start=(q == 0), stop=(q == 2))
                elif kind == "w2":
                    for j in range(min(2, EX - 2 * i)):
                        nc.tensor.transpose(ps[:, D * j:D * j + 128], w2_natA[:, 2 * i + j, :], ident[:, :])
                        last = nc.tensor.transpose(ps[:, D * j + 128:D * j + D], w2_natB[:, 2 * i + j, :], ident[0:64, 0:64])
                elif kind == "proj":
                    for j in range(2 if i == 0 else 1):
                        q = 2 * i + j
                        nc.tensor.transpose(ps[0:NQ, D * j:D * j + 128], pw_natA[:, NQ * q:NQ * q + NQ], ident[:, :])
                        last = nc.tensor.transpose(ps[0:NQ, D * j + 128:D * j + D], pw_natB[:, NQ * q:NQ * q + NQ],
                                                   ident[0:64, 0:64])
                last.then_inc(prep_full, 1)
            pe.wait_ge(prep_dve, P_DVE_N[-1])
            pe.wait_ge(prep_act, P_ACT_N[-1])
            pe.wait_ge(ready, 1)

            def products(o, left, right):
                for q in range(len(left)):
                    ins = mm(o, left[q], right[q], start=(q == 0), stop=(q == len(left) - 1))
                return ins

            def item(g, kind, i):
                if kind not in PE_KINDS + ("keyG",):
                    return
                r = R[("G", 0) if kind == "keyG" else (kind, i)]
                ps = aux[g.bank(r)]
                act_rounds = dve_rounds = None
                if r < 2:
                    act_rounds = BYACT[NR - 2 + r] - BYACT[-1]
                elif ROUNDS[r - 2][0] in DVE_KINDS:
                    dve_rounds = BYDVE[r - 2]
                else:
                    act_rounds = BYACT[r - 2]
                source = {"S": ("VHT", i // 3), "ET": ("S", 3 * (i // 2) + (1 if i % 2 == 0 else 2)),
                          "AH": ("ET", 2 * i + 1), "M": ("AH", i // 2), "keyG": ("X", 7),
                          "GQ": ("XT", 3), "H": ("M", 3 if i >= 4 else 1), "G": ("GQ", 1)}
                if kind in source:
                    src = R[source[kind]]
                    if kind == "H":
                        src = max(src, R[("U", 7)])
                    if ROUNDS[src][0] in DVE_KINDS:
                        dve_rounds = max(dve_rounds or 0, BYDVE[src])
                    else:
                        act_rounds = max(act_rounds or 0, BYACT[src])
                if act_rounds is not None:
                    wait(pe, aux_act, g.at(BYACT[-1], act_rounds))
                if dve_rounds is not None:
                    wait(pe, aux_dve, g.at(BYDVE[-1], dve_rounds))
                if kind == "tok":
                    for s in (dve_summed, act_summed, rows_used):
                        pe.wait_ge(s, g.at(TILES, TILES))
                    for k in range(CG):
                        last = nc.tensor.transpose(ps[0:HT, 128 * k:128 * k + 128], pooled[:, k, :], ident[:, :])
                elif kind == "V":
                    for k in range(CG):
                        last = mm(ps[0:HT, 0:UNITS * (CH + 1)], pooled[:, k, :], blockG[:, k, :],
                                  start=(k == 0), stop=(k == CG - 1))
                elif kind == "PHT":
                    pe.wait_ge(ph_ready, g.at(1, 1))
                    for b in range(4):
                        u = GB * i + 4 * b
                        last = nc.tensor.transpose(ps[:, HT * b:HT * b + HT],
                                                   PH[:, u:u + 4, :].rearrange("p u c -> p (u c)"), ident[0:HT, 0:HT])
                elif kind == "VHT":
                    pe.wait_ge(vh_ready, g.at(2, i + 1))
                    pe.sem_inc(pe_passed, 1)
                    for b in range(8):
                        last = nc.tensor.transpose(ps[:, NQ * b:NQ * b + NQ], VHpad[:, b, :], ident[0:NQ, 0:NQ])
                elif kind == "S":
                    b0, nb = S_IMGS[i]
                    for b in range(b0, b0 + nb):
                        at = (b - b0) * NK
                        mm(ps[0:NQ, at:at + HT - NQ], VHT[:, b % 8, :], PHT[:, 0, b // 4, NQ:HT], start=True, stop=True)
                        last = mm(ps[0:NQ, at + HT - NQ:at + NK], VHT[:, b % 8, :], PHT[:, 1, b // 4, :],
                                  start=True, stop=True)
                elif kind == "ET":
                    pe.sem_inc(pe_passed, 1)
                    for j in range(8):
                        b, s = 4 * (i % 2) + j // 2, j % 2
                        last = nc.tensor.transpose(ps[0:HT, NQ * j:NQ * j + NQ], E[:, b, HT * s:HT * s + HT],
                                                   ident[0:NQ, 0:NQ])
                elif kind == "AH":
                    for b in range(8):
                        for s in range(2):
                            last = mm(ps[0:NQ, CH * b:CH * b + CH], ET[:, 2 * b + s, :], PH[:, GB * s + 8 * i + b, 0:CH],
                                      start=(s == 0), stop=(s == 1))
                elif kind == "M":
                    half, part = divmod(i, 2)
                    n = 2 if part == 0 else 1
                    last = mm(ps[0:8 * CH, 0:n * D], Asb[:, half, :],
                              projT[:, 2 * part:2 * part + n, :].rearrange("p r d -> p (r d)"), start=True, stop=True)
                elif kind == "U":
                    pe.wait_ge(u_rep, g.at(2, 2))
                    for j in range(2):
                        for s in range(2):
                            at = TOK * j + HT * s
                            last = mm(ps[0:126, at:at + HT],
                                      SPT[:, GB * s + 2 * i + j, :, :, :].rearrange("p a b c -> p (a b c)"),
                                      identb[0:HT, 0:HT], start=True, stop=True)
                elif kind == "X":
                    pe.wait_ge(x_rep, g.at(2, 2))
                    for j in range(2):
                        for s in range(2):
                            at = NK * j + (HT - NQ) * s
                            n = HT - NQ if s == 0 else HT
                            last = mm(ps[0:126, at:at + n],
                                      SPT[:, GB * s + 2 * i + j, :, :, :].rearrange("p a b c -> p (a b c)"),
                                      identb[0:HT, HT - n:HT], start=True, stop=True)
                elif kind == "H":
                    mm(ps[:, 0:D], UTq[:, 128 * i:128 * i + 128], CWx[:, :], start=True, stop=False)
                    for q in range(3):
                        last = mm(ps[:, 0:D], CWr[:, q, i % 4, :], Msb[:, i // 4, D * q:D * q + D],
                                  start=False, stop=(q == 2))
                elif kind == "XT":
                    q, part = divmod(i, 2)
                    pe.wait_ge(x2_ready, g.at(8, 4 * q + 4))
                    pe.sem_inc(pe_passed, 1)
                    for j in range(4):
                        at = slice(128 * j, 128 * j + 128)
                        if part == 0:
                            last = nc.tensor.transpose(ps[:, at], x2q[:, j, 0:128], ident[:, :])
                        else:
                            nc.tensor.transpose(ps[0:64, at], x2q[:, j, 128:D], ident[:, :])
                            last = mm(ps[64:128, at], x2q[:, j, 128:D], ident[:, :], start=True, stop=True)
                elif kind == "GQ":
                    at = slice(512 * i, 512 * i + 512)
                    last = products(ps[0:NE, :], [gT0h[:, :], gT0l[:, :], gT0h[:, :], gT1s[:, :], gT1s[:, :]],
                                    [x0h[:, at], x0h[:, at], x0l[:, at], x1h[:, at], x1l[:, at]])
                elif kind == "G":
                    pe.sem_inc(pe_passed, 1)
                    for t in range(8):
                        last = nc.tensor.transpose(ps[:, NE * t:NE * t + NE], logT[:, 128 * t:128 * t + 128], ident[0:NE, 0:NE])
                elif kind == "keyG":
                    for t in range(9 * i, 9 if i == 0 else 17):
                        mm(ps[:, NE * (8 + t):NE * (9 + t)], X2T[g.par][0:126, 128 * t:128 * t + 128],
                           Wx[:, WCOLS:WCOLS + NE], start=True, stop=True)
                    return
                elif kind == "C":
                    pe.wait_ge(cs_ready, g.at(1, 1))
                    for j in range(4 if i < 6 else 1):
                        n = 128 if i < 6 else 64
                        last = mm(ps[0:SPL * NE, 128 * j:128 * j + n], CS[:, 4 * i + j, :, :].rearrange("p s e -> p (s e)"),
                                  identb[:, 0:n], start=True, stop=True)
                last.then_inc(aux_full, 1)

            def layer2(g, step):
                c, e = divmod(step, EX)
                query, col, n = CHUNKS[c]
                if e == 0:
                    if c in (1, 2):
                        pe.wait_ge(evac_dve, g.at(4, 2 * c))
                    elif c == 0:
                        wait(pe, evac_act, g.at(EVAC[-1], 0))
                    else:
                        pe.wait_ge(evac_act, g.at(EVAC[-1], EVAC[c - 1]))
                pe.wait_ge(h_done, g.at(NCH * NE, c * NE + min(e + 1, NE)))
                if e == NE:
                    pe.wait_ge(gated_done, g.at(STEPS, step + 1))
                m = min(n, 128)
                for t in range((n + 127) // 128):
                    o = out_ps[t // 2][0:m, D * (t % 2):D * (t % 2) + D]
                    if e == 0 and not query:
                        mm(o, UTk[g.par][:, col + 128 * t:col + 128 * t + m], CWx[:, :], start=(t % 2 == 0), stop=False,
                           skip_group_check=True)
                    last = mm(o, h[step % HR][:, 128 * t:128 * t + m], W2T[:, e, :],
                              start=(e == 0 and query and t % 2 == 0), stop=(e == NE), skip_group_check=True)
                last.then_inc(l2_step, 1)

            def ffn_pe(g, left):
                for step in range(STEPS):
                    c, e = divmod(step, EX)
                    query, col, n = CHUNKS[c]
                    wait(pe, gated_done, g.at(STEPS, step - 1))
                    if step == 0:
                        pe.wait_ge(aux_act, g.at(BYACT[-1], BYACT[-1]))
                    for k, o in ((0, h_ps(step, 0)), (1, h_ps(step, 1))):
                        if k == 1:
                            if step >= 2:
                                layer2(g, step - 2)
                            wait(pe, silu_done, g.at(STEPS, step))
                        w = (k * EX + e) * INTER
                        if query:
                            w, at = slice(w, w + INTER), slice(col, col + n)
                            last = products(o[:, 0:n], [WT0h[:, w], WT0l[:, w], WT0h[:, w], WT1s[:, w], WT1s[:, w]],
                                            [x0h[:, at], x0h[:, at], x0l[:, at], x1h[:, at], x1l[:, at]])
                        else:
                            last = mm(o[:, 0:n], Wx[:, w:w + INTER], X2T[g.par][:, col:col + n], start=True, stop=True)
                        last.then_inc(h1_ready if k == 0 else h3_ready, 1)
                    if e < NE:
                        wait(pe, h_done, g.at(NCH * NE, c * NE + e))
                        at = col if query else 1024 + col
                        mm(cw_ps[:, 0:n], sel[:, e, :], cwT[:, at:at + n], start=True, stop=True).then_inc(cw_ready, 1)
                    if left:
                        for kind, i in items_at(step):
                            item(g.plus(1), kind, i)
                layer2(g, STEPS - 2)
                layer2(g, STEPS - 1)

            for kind, i in ITEMS:
                item(G(None, 0), kind, i)
            ffn_pe(G(None, 0), 1)
            with pe.Fori(0, 2) as k:
                for off in (1, 2):
                    ffn_pe(G(k, off), 1)
            ffn_pe(G(None, 5), 1)
            ffn_pe(G(None, 6), 1)
            ffn_pe(G(None, 7), 0)


INS = ["x", "L0_tok_channel_weights", "L0_attn_proj_w", "L0_attn_proj_b", "L0_ffn_gate_weight", "L0_ffn_gate_bias",
       "L0_ffn_w1", "L0_ffn_w2", "L0_ffn_w3", "L0_ffn_sw1", "L0_ffn_sw2", "L0_ffn_sw3"]


def kernel(**inputs):
    import numpy as np
    import concourse.bacc as bacc
    from concourse.bass_utils import run_bass_kernel_spmd

    nc = bacc.Bacc("TRN2", target_bir_lowering=False, num_devices=1)
    arrays, args = {}, []
    for name in INS:
        a = np.ascontiguousarray(inputs[name])
        arrays[f"in_{name}"] = a
        args.append(nc.dram_tensor(f"in_{name}", a.shape, mybir.dt.from_np(a.dtype), kind="ExternalInput").ap())
    out = nc.dram_tensor("out_0", (NB, TOK, D), F32, kind="ExternalOutput").ap()
    build(nc, *args, out)
    r = run_bass_kernel_spmd(nc, [arrays], core_ids=[0])
    return r.results[0]["out_0"]
```
